# Optimizing a Trainium2 kernel written in Bass

```python
import numpy as np
import jax
import jax.numpy as jnp

def _softmax(x, axis=-1):
    return jax.nn.softmax(x, axis=axis)

def _gelu(x):
    return jax.nn.gelu(x, approximate=True)

def _silu(x):
    return jax.nn.silu(x)

def _sigmoid(x):
    return jax.nn.sigmoid(x)

def _layernorm(x, axis=-1, eps=1e-05):
    m = jnp.mean(x, axis=axis, keepdims=True)
    v = jnp.var(x, axis=axis, keepdims=True)
    return (x - m) / jnp.sqrt(v + eps)

def _scatter_add(tgt, idx, src, axis=0):
    return tgt.at[idx].add(src)

def _segment_sum(src, seg, n):
    return jax.ops.segment_sum(src, seg, n)
kernel_name = 'mk_flamingo_gated_d2_seqx_r8_b89a95'

def setup_inputs(seed: int=0):
    np.random.seed(seed)
    _w = jnp.asarray

    def _rec_inputs():
        import jax
        import jax.numpy as jnp
        _rk = jax.random.key(seed)
        x = 6.313e-05 + 0.9998 * jax.random.normal(jax.random.fold_in(_rk, 1), (4, 512, 128), jnp.float32)
        _lenS = 512 - jax.random.randint(jax.random.fold_in(_rk, 7), (4,), 0, max(1, 512 // 4) + 1, jnp.int32)
        _lenS2 = 77 - jax.random.randint(jax.random.fold_in(_rk, 8), (4,), 0, max(1, 77 // 4) + 1, jnp.int32)
        _ctx_1024P = jax.random.normal(jax.random.fold_in(_rk, 11), (4, 16, 128), jnp.float32)
        _ctx_1024c = jax.random.dirichlet(jax.random.fold_in(_rk, 511), 0.3 * jnp.ones((16,), jnp.float32), (4, 77))
        _ctx_1024t = jnp.einsum('bsk,bkd->bsd', _ctx_1024c, _ctx_1024P)
        _ctx_1024t = _ctx_1024t * jax.lax.rsqrt(jnp.mean(jnp.square(_ctx_1024t)) + 1e-12) * 0.953939
        ctx_1024 = -0.000214406 + 1.00034 * (_ctx_1024t + 0.3 * jax.random.normal(jax.random.fold_in(_rk, 611), (4, 77, 128), jnp.float32))
        _g = jax.random.normal(jax.random.fold_in(_rk, 9001), (2, 2), jnp.float32)
        _g = jnp.sign(_g) * jnp.maximum(jnp.abs(_g), 1.0) + (_g == 0) * 1.0
        g_xattn = _g[0]
        g_ffn = _g[1]
        return (x, ctx_1024, g_xattn, g_ffn)
    x, ctx_1024, g_xattn, g_ffn = _rec_inputs()

    def _L0_xattn_setup():
        import jax, jax.numpy as jnp
        import numpy as np
        from jax import lax
        BIG = jnp.float32(1e+30)

        def _pairwise_euclidean(a, b):
            aa = jnp.sum(a * a, axis=-1)[:, None]
            bb = jnp.sum(b * b, axis=-1)[None, :]
            ab = a @ b.T
            return jnp.sqrt(jnp.maximum(aa + bb - 2.0 * ab, 0.0))

        def _dtw_cost(D):
            row0 = jnp.cumsum(D[0])

            def row_step(prev_row, d_row):
                first = d_row[0] + prev_row[0]

                def col_step(left, inp):
                    d_ij, up, diag = inp
                    r = d_ij + jnp.minimum(jnp.minimum(up, left), diag)
                    return (r, r)
                _, rest = lax.scan(col_step, first, (d_row[1:], prev_row[1:], prev_row[:-1]))
                row = jnp.concatenate([first[None], rest])
                return (row, row)
            _, rows = lax.scan(row_step, row0, D[1:])
            return jnp.concatenate([row0[None], rows], axis=0)

        def _backtrack(R, T1, T2):
            L = T1 + T2 - 1

            def step(carry, _):
                i, j, done = carry
                valid = jnp.logical_not(done)
                cd = jnp.where((i > 0) & (j > 0), R[jnp.maximum(i - 1, 0), jnp.maximum(j - 1, 0)], BIG)
                cu = jnp.where(i > 0, R[jnp.maximum(i - 1, 0), j], BIG)
                cl = jnp.where(j > 0, R[i, jnp.maximum(j - 1, 0)], BIG)
                choice = jnp.argmin(jnp.stack([cd, cu, cl]))
                ni = jnp.where(choice <= 1, i - 1, i)
                nj = jnp.where((choice == 0) | (choice == 2), j - 1, j)
                at_origin = (i == 0) & (j == 0)
                ni = jnp.where(at_origin, 0, ni)
                nj = jnp.where(at_origin, 0, nj)
                return ((ni, nj, done | at_origin), (i, j, valid))
            init = (jnp.int32(T1 - 1), jnp.int32(T2 - 1), jnp.bool_(False))
            _, (i_idx, j_idx, valid) = lax.scan(step, init, None, length=L)
            return (i_idx, j_idx, valid)

        def _align_one(small, large):
            T_small, d = small.shape
            T_large = large.shape[0]
            D = _pairwise_euclidean(small, large)
            R = _dtw_cost(D)
            i_idx, j_idx, valid = _backtrack(R, T_small, T_large)
            contrib = small[i_idx] * valid[:, None].astype(small.dtype)
            expanded = jnp.zeros((T_large, d), dtype=small.dtype).at[j_idx].add(contrib)
            return expanded
        key = jax.random.key(seed)
        k1, k2 = jax.random.split(key)
        teacher = jax.random.normal(k1, (16, 50, 128), dtype=jnp.float32)
        student = jax.random.normal(k2, (16, 75, 128), dtype=jnp.float32)
        return {'teacher_features': teacher, 'student_features': student}
    _L0_xattn_all = _L0_xattn_setup()
    _L0_xattn_in = {k: v for k, v in _L0_xattn_all.items() if k in ()}
    del _L0_xattn_all

    def _L0_ffn_setup():
        import jax, jax.numpy as jnp
        import numpy as np
        B, S, H, I, E, K = (2, 64, 128, 64, 64, 8)
        key = jax.random.key(seed)
        ks = jax.random.split(key, 8)
        return {'hidden_states': jax.random.normal(ks[0], (B, S, H), dtype=jnp.float32), 'router_w': jax.random.normal(ks[1], (H, E), dtype=jnp.float32) * 0.02, 'shared_gate_w': jax.random.normal(ks[2], (H, I), dtype=jnp.float32) * 0.02, 'shared_up_w': jax.random.normal(ks[3], (H, I), dtype=jnp.float32) * 0.02, 'shared_down_w': jax.random.normal(ks[4], (I, H), dtype=jnp.float32) * 0.02, 'expert_gate_k': jax.random.normal(ks[5], (E, H, I), dtype=jnp.float32) * 0.02, 'expert_up_k': jax.random.normal(ks[6], (E, H, I), dtype=jnp.float32) * 0.02, 'expert_down_k': jax.random.normal(ks[7], (E, I, H), dtype=jnp.float32) * 0.02}
    _L0_ffn_all = _L0_ffn_setup()
    _L0_ffn_in = {k: v for k, v in _L0_ffn_all.items() if k in ('router_w', 'shared_gate_w', 'shared_up_w', 'shared_down_w', 'expert_gate_k', 'expert_up_k', 'expert_down_k')}
    del _L0_ffn_all

    def _L1_xattn_setup():
        import jax, jax.numpy as jnp
        import numpy as np
        D_MODEL = 128
        NUM_HEADS = 16
        D_K = D_MODEL // NUM_HEADS

        def _split_heads(x):
            B, S, _ = x.shape
            return x.reshape(B, S, NUM_HEADS, D_K).transpose(0, 2, 1, 3)
        key = jax.random.key(seed)
        ks = jax.random.split(key, 11)
        B, S = (2, 256)
        scale = 1.0 / np.sqrt(D_MODEL)
        inp = {'q': jax.random.normal(ks[0], (B, S, D_MODEL), jnp.float32), 'k': jax.random.normal(ks[1], (B, S, D_MODEL), jnp.float32), 'v': jax.random.normal(ks[2], (B, S, D_MODEL), jnp.float32), 'Wq': jax.random.normal(ks[3], (D_MODEL, D_MODEL), jnp.float32) * scale, 'bq': jnp.zeros((D_MODEL,), jnp.float32), 'Wk': jax.random.normal(ks[4], (D_MODEL, D_MODEL), jnp.float32) * scale, 'bk': jnp.zeros((D_MODEL,), jnp.float32), 'Wv': jax.random.normal(ks[5], (D_MODEL, D_MODEL), jnp.float32) * scale, 'bv': jnp.zeros((D_MODEL,), jnp.float32), 'Wo': jax.random.normal(ks[6], (D_MODEL, D_MODEL), jnp.float32) * scale, 'bo': jnp.zeros((D_MODEL,), jnp.float32)}
        return inp
    _L1_xattn_all = _L1_xattn_setup()
    _L1_xattn_in = {k: v for k, v in _L1_xattn_all.items() if k in ('Wq', 'bq', 'Wk', 'bk', 'Wv', 'bv', 'Wo', 'bo')}
    del _L1_xattn_all

    def _L1_ffn_setup():
        import jax, jax.numpy as jnp
        import numpy as np
        B, S, H = (4, 256, 128)
        I = 344
        E = 8
        K = 2

        def _ffn(x, wg, wu, wd):
            return jax.nn.silu(x @ wg.T) * (x @ wu.T) @ wd.T

        def _moe_forward(x, gate_w, wg, wu, wd, swg, swu, swd):
            b, s, h = x.shape
            xf = x.reshape(-1, h)
            T = xf.shape[0]
            logits = xf @ gate_w.T
            scores = jax.nn.softmax(logits, axis=-1)
            topk_w, topk_idx = jax.lax.top_k(scores, K)
            topk_w = topk_w / (jnp.sum(topk_w, axis=-1, keepdims=True) + 1e-20)
            cw = jnp.zeros((T, E), dtype=xf.dtype).at[jnp.arange(T)[:, None], topk_idx].set(topk_w)
            y = jnp.zeros_like(xf)
            for e in range(E):
                y = y + cw[:, e:e + 1] * _ffn(xf, wg[e], wu[e], wd[e])
            y = y.reshape(b, s, h)
            y = y + _ffn(x, swg, swu, swd)
            return y
        key = jax.random.key(seed)
        ks = jax.random.split(key, 9)
        sH = 1.0 / np.sqrt(H)
        sI = 1.0 / np.sqrt(I)
        return {'x': jax.random.normal(ks[0], (B, S, H), dtype=jnp.float32), 'gate_w': jax.random.normal(ks[1], (E, H), dtype=jnp.float32) * sH, 'wg': jax.random.normal(ks[2], (E, I, H), dtype=jnp.float32) * sH, 'wu': jax.random.normal(ks[3], (E, I, H), dtype=jnp.float32) * sH, 'wd': jax.random.normal(ks[4], (E, H, I), dtype=jnp.float32) * sI, 'swg': jax.random.normal(ks[5], (I, H), dtype=jnp.float32) * sH, 'swu': jax.random.normal(ks[6], (I, H), dtype=jnp.float32) * sH, 'swd': jax.random.normal(ks[7], (H, I), dtype=jnp.float32) * sI}
    _L1_ffn_all = _L1_ffn_setup()
    _L1_ffn_in = {k: v for k, v in _L1_ffn_all.items() if k in ('gate_w', 'wg', 'wu', 'wd', 'swg', 'swu', 'swd')}
    del _L1_ffn_all
    return {'x': x, 'ctx_1024': ctx_1024, 'g_xattn': g_xattn, 'g_ffn': g_ffn, 'L0_ffn_router_w': _L0_ffn_in['router_w'], 'L0_ffn_shared_gate_w': _L0_ffn_in['shared_gate_w'], 'L0_ffn_shared_up_w': _L0_ffn_in['shared_up_w'], 'L0_ffn_shared_down_w': _L0_ffn_in['shared_down_w'], 'L0_ffn_expert_gate_k': _L0_ffn_in['expert_gate_k'], 'L0_ffn_expert_up_k': _L0_ffn_in['expert_up_k'], 'L0_ffn_expert_down_k': _L0_ffn_in['expert_down_k'], 'L1_xattn_Wq': _L1_xattn_in['Wq'], 'L1_xattn_bq': _L1_xattn_in['bq'], 'L1_xattn_Wk': _L1_xattn_in['Wk'], 'L1_xattn_bk': _L1_xattn_in['bk'], 'L1_xattn_Wv': _L1_xattn_in['Wv'], 'L1_xattn_bv': _L1_xattn_in['bv'], 'L1_xattn_Wo': _L1_xattn_in['Wo'], 'L1_xattn_bo': _L1_xattn_in['bo'], 'L1_ffn_gate_w': _L1_ffn_in['gate_w'], 'L1_ffn_wg': _L1_ffn_in['wg'], 'L1_ffn_wu': _L1_ffn_in['wu'], 'L1_ffn_wd': _L1_ffn_in['wd'], 'L1_ffn_swg': _L1_ffn_in['swg'], 'L1_ffn_swu': _L1_ffn_in['swu'], 'L1_ffn_swd': _L1_ffn_in['swd']}

def reference(x, ctx_1024, g_xattn, g_ffn, L0_ffn_router_w, L0_ffn_shared_gate_w, L0_ffn_shared_up_w, L0_ffn_shared_down_w, L0_ffn_expert_gate_k, L0_ffn_expert_up_k, L0_ffn_expert_down_k, L1_xattn_Wq, L1_xattn_bq, L1_xattn_Wk, L1_xattn_bk, L1_xattn_Wv, L1_xattn_bv, L1_xattn_Wo, L1_xattn_bo, L1_ffn_gate_w, L1_ffn_wg, L1_ffn_wu, L1_ffn_wd, L1_ffn_swg, L1_ffn_swu, L1_ffn_swd):
    import jax
    import jax.numpy as jnp

    def _L0_xattn_ref(teacher_features, student_features):
        import jax, jax.numpy as jnp
        import numpy as np
        from jax import lax
        BIG = jnp.float32(1e+30)

        def _pairwise_euclidean(a, b):
            aa = jnp.sum(a * a, axis=-1)[:, None]
            bb = jnp.sum(b * b, axis=-1)[None, :]
            ab = a @ b.T
            return jnp.sqrt(jnp.maximum(aa + bb - 2.0 * ab, 0.0))

        def _dtw_cost(D):
            row0 = jnp.cumsum(D[0])

            def row_step(prev_row, d_row):
                first = d_row[0] + prev_row[0]

                def col_step(left, inp):
                    d_ij, up, diag = inp
                    r = d_ij + jnp.minimum(jnp.minimum(up, left), diag)
                    return (r, r)
                _, rest = lax.scan(col_step, first, (d_row[1:], prev_row[1:], prev_row[:-1]))
                row = jnp.concatenate([first[None], rest])
                return (row, row)
            _, rows = lax.scan(row_step, row0, D[1:])
            return jnp.concatenate([row0[None], rows], axis=0)

        def _backtrack(R, T1, T2):
            L = T1 + T2 - 1

            def step(carry, _):
                i, j, done = carry
                valid = jnp.logical_not(done)
                cd = jnp.where((i > 0) & (j > 0), R[jnp.maximum(i - 1, 0), jnp.maximum(j - 1, 0)], BIG)
                cu = jnp.where(i > 0, R[jnp.maximum(i - 1, 0), j], BIG)
                cl = jnp.where(j > 0, R[i, jnp.maximum(j - 1, 0)], BIG)
                choice = jnp.argmin(jnp.stack([cd, cu, cl]))
                ni = jnp.where(choice <= 1, i - 1, i)
                nj = jnp.where((choice == 0) | (choice == 2), j - 1, j)
                at_origin = (i == 0) & (j == 0)
                ni = jnp.where(at_origin, 0, ni)
                nj = jnp.where(at_origin, 0, nj)
                return ((ni, nj, done | at_origin), (i, j, valid))
            init = (jnp.int32(T1 - 1), jnp.int32(T2 - 1), jnp.bool_(False))
            _, (i_idx, j_idx, valid) = lax.scan(step, init, None, length=L)
            return (i_idx, j_idx, valid)

        def _align_one(small, large):
            T_small, d = small.shape
            T_large = large.shape[0]
            D = _pairwise_euclidean(small, large)
            R = _dtw_cost(D)
            i_idx, j_idx, valid = _backtrack(R, T_small, T_large)
            contrib = small[i_idx] * valid[:, None].astype(small.dtype)
            expanded = jnp.zeros((T_large, d), dtype=small.dtype).at[j_idx].add(contrib)
            return expanded
        return jax.vmap(_align_one)(teacher_features, student_features)

    def _L0_ffn_ref(hidden_states, router_w, shared_gate_w, shared_up_w, shared_down_w, expert_gate_k, expert_up_k, expert_down_k):
        import jax, jax.numpy as jnp
        import numpy as np
        B, S, H, I, E, K = (2, 64, 128, 64, 64, 8)
        logits = jnp.einsum('bsh,he->bse', hidden_states.astype(jnp.float32), router_w)
        affinity = jax.nn.sigmoid(logits)
        top_scores, top_idx = jax.lax.top_k(affinity, K)
        top_w = top_scores / (jnp.sum(top_scores, axis=-1, keepdims=True) + 1e-09)
        one_hot = jax.nn.one_hot(top_idx, E, dtype=top_w.dtype)
        router_mask = jnp.einsum('bske,bsk->bse', one_hot, top_w).astype(hidden_states.dtype)
        shared = jnp.einsum('bsi,ih->bsh', jax.nn.silu(hidden_states @ shared_gate_w) * (hidden_states @ shared_up_w), shared_down_w)
        gate_out = jnp.einsum('bsh,ehi->bsei', hidden_states, expert_gate_k)
        up_out = jnp.einsum('bsh,ehi->bsei', hidden_states, expert_up_k)
        expert_act = jax.nn.silu(gate_out) * up_out
        routed = jnp.einsum('bsei,eih->bsh', expert_act * router_mask[..., None], expert_down_k)
        return shared + routed

    def _L1_xattn_ref(q, k, v, Wq, bq, Wk, bk, Wv, bv, Wo, bo):
        import jax, jax.numpy as jnp
        import numpy as np
        D_MODEL = 128
        NUM_HEADS = 16
        D_K = D_MODEL // NUM_HEADS

        def _split_heads(x):
            B, S, _ = x.shape
            return x.reshape(B, S, NUM_HEADS, D_K).transpose(0, 2, 1, 3)
        B, S, _ = q.shape
        qh = _split_heads(q @ Wq + bq)
        kh = _split_heads(k @ Wk + bk)
        vh = _split_heads(v @ Wv + bv)
        scores = jnp.einsum('bhsd,bhtd->bhst', qh, kh) / np.sqrt(D_K)
        attn = jax.nn.softmax(scores, axis=-1)
        out = jnp.einsum('bhst,bhtd->bhsd', attn, vh)
        out = out.transpose(0, 2, 1, 3).reshape(B, S, D_MODEL)
        return out @ Wo + bo

    def _L1_ffn_ref(x, gate_w, wg, wu, wd, swg, swu, swd):
        import jax, jax.numpy as jnp
        import numpy as np
        B, S, H = (4, 256, 128)
        I = 344
        E = 8
        K = 2

        def _ffn(x, wg, wu, wd):
            return jax.nn.silu(x @ wg.T) * (x @ wu.T) @ wd.T

        def _moe_forward(x, gate_w, wg, wu, wd, swg, swu, swd):
            b, s, h = x.shape
            xf = x.reshape(-1, h)
            T = xf.shape[0]
            logits = xf @ gate_w.T
            scores = jax.nn.softmax(logits, axis=-1)
            topk_w, topk_idx = jax.lax.top_k(scores, K)
            topk_w = topk_w / (jnp.sum(topk_w, axis=-1, keepdims=True) + 1e-20)
            cw = jnp.zeros((T, E), dtype=xf.dtype).at[jnp.arange(T)[:, None], topk_idx].set(topk_w)
            y = jnp.zeros_like(xf)
            for e in range(E):
                y = y + cw[:, e:e + 1] * _ffn(xf, wg[e], wu[e], wd[e])
            y = y.reshape(b, s, h)
            y = y + _ffn(x, swg, swu, swd)
            return y
        return _moe_forward(x, gate_w, wg, wu, wd, swg, swu, swd)
    x = x + jnp.tanh(g_xattn[0]) * _L0_xattn_ref(ctx_1024, _layernorm(x, axis=-1))
    x = x + jnp.tanh(g_ffn[0]) * _L0_ffn_ref(_layernorm(x, axis=-1), L0_ffn_router_w, L0_ffn_shared_gate_w, L0_ffn_shared_up_w, L0_ffn_shared_down_w, L0_ffn_expert_gate_k, L0_ffn_expert_up_k, L0_ffn_expert_down_k)
    x = x + jnp.tanh(g_xattn[1]) * _L1_xattn_ref(_layernorm(x, axis=-1), ctx_1024, ctx_1024, L1_xattn_Wq, L1_xattn_bq, L1_xattn_Wk, L1_xattn_bk, L1_xattn_Wv, L1_xattn_bv, L1_xattn_Wo, L1_xattn_bo)
    x = x + jnp.tanh(g_ffn[1]) * _L1_ffn_ref(_layernorm(x, axis=-1), L1_ffn_gate_w, L1_ffn_wg, L1_ffn_wu, L1_ffn_wd, L1_ffn_swg, L1_ffn_swu, L1_ffn_swd)
    return x

_drawn_inputs = setup_inputs


def setup_inputs(seed=0):
    import zlib

    import numpy as np

    out = dict(_drawn_inputs(seed))
    spreads = {'g_ffn': (-1.0, 0.547),
     'L1_xattn_bq': (0.0, 0.346),
     'L1_xattn_bk': (0.0, 2.0),
     'L1_xattn_bv': (0.0, 0.1),
     'L1_xattn_bo': (0.0, 0.1)}
    factors = {'L0_ffn_router_w': 8.0,
     'L0_ffn_shared_gate_w': 5.354,
     'L0_ffn_shared_up_w': 5.305,
     'L0_ffn_shared_down_w': 5.419,
     'L0_ffn_expert_gate_k': 8.0,
     'L0_ffn_expert_up_k': 8.0,
     'L0_ffn_expert_down_k': 8.0}
    for name, (base, spread) in spreads.items():
        noise = np.random.default_rng([zlib.crc32(name.encode()), seed]).standard_normal(out[name].shape)
        drawn = base * np.exp(spread * noise) if base else spread * noise
        out[name] = jnp.asarray(drawn.astype(out[name].dtype))
    for name, factor in factors.items():
        out[name] = (out[name] * factor).astype(out[name].dtype)
    return out
```

```python
from contextlib import ExitStack

import concourse.bass as bass
import concourse.mybir as mybir
from concourse.alu_op_type import AluOpType as ALU

F32 = mybir.dt.float32
F32R = mybir.dt.float32r
F16 = mybir.dt.float16
U32 = mybir.dt.uint32
ACT = mybir.ActivationFunctionType
AX_X = mybir.AxisListType.X

P = 128
BIG = 1e30
TINY = 1e-30
LN_EPS = 1e-5


def program(nc, x, ctx_1024, g_xattn, g_ffn, r0_w, sg0, su0, sd0, eg0, eu0, ed0,
            Wq, bq, Wk, bk, Wv, bv, Wo, bo, r1_w, wg1, wu1, wd1, swg1, swu1, swd1, out):
    B, S, H = x.shape
    KEYS = ctx_1024.shape[1]
    TOK = B * S
    TILES = TOK // P
    TPB = S // P
    assert H == P and S == 512 and B == 4

    CH = 16
    CW = S // CH
    SLOTS = KEYS + CH - 1
    LANE = SLOTS * CW
    LANES = [32 * b for b in range(B)]

    E0, I0 = eg0.shape[0], eg0.shape[2]
    E1, I1 = wg1.shape[0], wg1.shape[1]
    K0 = 8
    assert P == 2 * I0
    EXPERTS = [E0, E1]
    CHUNKS = TOK // 512
    GROUPS = [1 + E0 // 2, -(-I1 * (E1 + 1) // P)]
    UP, DOWN, WIDE = P, 2 * P, 3 * P
    assert GROUPS[0] % 2 == 1 and GROUPS[1] % 2 == 1

    HEADS, HD = 16, H // 16
    HPB = 6
    HSPLIT = [(0, HPB), (HPB, 2 * HPB), (2 * HPB, HEADS)]
    HT = 4

    def pieces(first, last):
        found = []
        while first < last:
            n = min(last, (first // I1 + 1) * I1) - first
            found.append((first // I1 - 1, first % I1, n))
            first += n
        return found

    ctx = ExitStack()
    with ctx:
        def sb(name, shape, dt=F32):
            return ctx.enter_context(nc.sbuf_tensor(name, shape, dt))

        def sem(name):
            return ctx.enter_context(nc.semaphore(name))

        ps = [ctx.enter_context(nc.psum_tensor(f"bank{i}", [P, 512], F32)) for i in range(8)]

        scr_d = nc.dram_tensor("scr_d", (B, CH, SLOTS, CW), F32).ap()
        scr_one = nc.dram_tensor("scr_one", (TOK,), F32).ap()
        scr_w1 = nc.dram_tensor("scr_w1", (GROUPS[1], P, WIDE), F32).ap()
        scr_mask = [nc.dram_tensor("scr_mask0", (E0, TOK), F32).ap(),
                    nc.dram_tensor("scr_mask1", (E1, TOK), F32).ap()]
        scr_lg = nc.dram_tensor("scr_lg", (B, CH, SLOTS, 2, CW), F16).ap()

        x_res = sb("x_res", [P, TILES, H])
        xn = sb("xn", [P, TILES, H])
        xn_hi = sb("xn_hi", [P, TOK], F32R)
        xn_lo = sb("xn_lo", [P, TOK], F32R)
        stats = sb("stats", [P, TILES, 6])
        mv = sb("mv", [P, TILES, 2])
        veps = sb("veps", [P, TILES])
        std = sb("std", [P, TILES])
        rstd = sb("rstd", [P, 4, TILES])
        ident = sb("ident", [P, P])
        ones = sb("ones", [P, P])
        gates = sb("gates", [P, 4])
        tgate = sb("tgate", [P, 4])
        ctx_sb = sb("ctx_sb", [KEYS, B, H])
        ctxT = sb("ctxT", [P, B, KEYS])
        ctxT_hi = sb("ctxT_hi", [P, B, KEYS], F32R)
        ctxT_lo = sb("ctxT_lo", [P, B, KEYS], F32R)
        zeros = sb("zeros", [1, 512], F32R)
        iota_e = sb("iota_e", [P, E1])
        jrow = sb("jrow", [P, S], F16)
        ecol = sb("ecol", [P, KEYS])
        erow = sb("erow", [KEYS, B])
        junk = sb("junk", [P, S], F16)
        aa = sb("aa", [KEYS, B])
        aasq = sb("aasq", [KEYS, B, H])

        w_raw = sb("w_raw", [P, 2, WIDE])
        w_hi = sb("w_hi", [P, 2, WIDE], F32R)
        w_lo = sb("w_lo", [P, 2, WIDE], F32R)
        prep_in = sb("prep_in", [P, 2, WIDE])
        prep_out = sb("prep_out", [P, 2, WIDE])
        router = [sb("router0", [P, E0]), sb("router1", [P, E1])]
        router_hi = [sb("router0_hi", [P, E0], F32R), sb("router1_hi", [P, E1], F32R)]
        router_lo = [sb("router0_lo", [P, E0], F32R), sb("router1_lo", [P, E1], F32R)]
        act_hi = sb("act_hi", [P, 2, 512], F32R)
        act_lo = sb("act_lo", [P, 2, 512], F32R)
        kbd_hi = sb("kbd_hi", [P, B, HEADS, KEYS], F32R)
        kbd_lo = sb("kbd_lo", [P, B, HEADS, KEYS], F32R)
        qs_hi = sb("qs_hi", [P, 2, P], F32R)
        qs_lo = sb("qs_lo", [P, 2, P], F32R)
        router1_rows = sb("router1_rows", [E1, P])
        w4 = sb("w4", [P, 4, P])
        wq_hi = sb("wq_hi", [P, P], F32R)
        wq_lo = sb("wq_lo", [P, P], F32R)
        bias2 = sb("bias2", [P, 2])
        brow2 = sb("brow2", [1, 2, P])
        headmask = sb("headmask", [P, HEADS])

        ARENA = 20600
        arena = sb("arena", [P, ARENA])
        mark = [0]

        def view(shape, dt=F32):
            n = 1
            for k in shape:
                n *= k
            cols = n // 2 if dt == F16 else n
            v = arena[:, mark[0]:mark[0] + cols]
            mark[0] += cols
            assert mark[0] <= ARENA
            if dt != F32:
                v = v.bitcast(dt)
            if len(shape) == 2:
                v = v.rearrange("p (a b) -> p a b", a=shape[0])
            if len(shape) == 3:
                v = v.rearrange("p (a b c) -> p a b c", a=shape[0], b=shape[1])
            return v

        sq = view([2, S])
        dsum = view([B, S])
        d2 = view([B, S])
        droot = view([B, S])
        droot2 = view([B, S])
        drows = view([B, S])
        dl = view([SLOTS, CW])
        rst = view([SLOTS + 1, CW + 1])
        MST = 8
        mst = view([MST, CW])
        lg = view([SLOTS, 2, CW], F16)
        mark[0] = 0
        lgr = view([2, B, S], F16)
        nlj = view([B, S], F16)
        nup = view([B, S], F16)
        ubig = view([B, S], F16)
        srow = view([B, S + 8], F16)
        trow = view([B, S], F16)
        pcond = view([B, S], F16)
        mark[0] = 0
        pmask = view([B, S])
        CHASE = slice(96, 96 + B)
        mark[0] = 0
        chase = view([KEYS, S], F16)[CHASE]
        mark[0] = 0
        mask = view([2, TOK])
        act_s = view([2, 512])
        act_t = view([2, 512])
        act_a = view([2, 512])
        yT = view([CHUNKS, 512])
        maskT = view([1, TOK])[:, 0]
        aff = [view([TILES, E]) for E in EXPERTS]
        rest = [view([TILES, E]) for E in EXPERTS]
        wsel = [view([TILES, E]) for E in EXPERTS]
        top8 = view([TILES, 8])
        topi = view([TILES, 8], U32)
        topf = view([TILES, 8])
        hit = [view([TILES, E1]) for c in range(2)]
        rsum = view([4, TILES])

        kT_hi = view([B * KEYS], F32R)
        kT_lo = view([B * KEYS], F32R)
        kT = view([B * KEYS])
        v_ext = view([B * HEADS, HD + 1])
        mark[0] = 0
        qT_hi = view([TOK], F32R)
        qT_lo = view([TOK], F32R)
        expw = view([2, HEADS * KEYS])
        smax = view([2, HEADS])
        expT = view([HEADS, P])
        rden = view([2, HEADS])
        av = view([2, H])
        avT = view([P])

        s_aw = sem("attn_weights_loaded")
        s_kp = sem("k_projected")
        s_vp = sem("v_projected")
        s_khi = sem("kT_hi_ready")
        s_klo = sem("kT_lo_ready")
        s_vx = sem("v_ready")
        s_vone = sem("v_ones")
        s_kbh = sem("kbd_hi_ready")
        s_kbl = sem("kbd_lo_ready")
        s_wql = sem("wq_lo_ready")
        s_wqh = sem("wq_hi_ready")
        s_qp = sem("q_projected")
        s_qhi = sem("qT_hi_ready")
        s_qlo = sem("qT_lo_ready")
        s_qs = sem("q_tile_ready")
        s_sc = sem("scores")
        s_mx = sem("scores_max")
        s_sub = sem("scores_shifted")
        s_exp = sem("exp_ready")
        s_tr = sem("exp_transposed")
        s_ev = sem("exp_copied")
        s_av = sem("av_products")
        s_rd = sem("av_reciprocal")
        s_nrm = sem("av_normalised")
        s_avt = sem("av_transposed")
        s_avc = sem("av_copied")
        s_wo = sem("out_projected")
        s_au = sem("x_updated_attn")
        s_one = sem("ones_stored")
        s_rw = [sem("router0_loaded"), sem("router1_loaded")]
        s_rt = sem("router1_transposed")
        s_rhi = sem("router_hi_ready")
        s_rlo = sem("router_lo_ready")
        s_logit = sem("router_logits")
        s_score = sem("router_scores")
        s_rsub = sem("router_shifted")
        s_rexp = sem("router_exp")
        s_sel = sem("router_weights")
        s_selT = sem("router_weights_transposed")
        s_mrow = sem("mask_rows")
        s_mst = sem("mask_stored")
        s_pin = [sem(f"prep_loaded{j}") for j in range(2)]
        s_pzero = sem("prep_zeroed")
        s_pt = sem("prep_transposed")
        s_pout = sem("prep_copied")
        s_pst = [sem(f"prep_stored{j}") for j in range(2)]
        FF = [dict((n, sem(f"ff{f}_{n}")) for n in (
            "whi", "wlo", "gate", "up", "silu", "t", "act", "ahi", "alo", "down", "sum", "yT", "back")) for f in range(2)]
        FF_RAW = [[sem(f"ff{f}_raw_loaded{j}") for j in range(2)] for f in range(2)]
        FF_MASK = [[sem(f"ff{f}_mask_loaded{j}") for j in range(2)] for f in range(2)]
        RAW_DMAS, MASK_DMAS = [3, 1], 2
        s_x = [sem(f"x_loaded{b}") for b in range(B)]
        s_ctx = sem("ctx_loaded")
        s_gate = sem("gates_loaded")
        s_zero = sem("scratch_zeroed")
        s_pool = sem("pool_step")
        s_dve = sem("dve_step")
        s_act = sem("act_step")
        s_bn = sem("ln_var_ready")
        s_std = sem("ln_std_ready")
        s_xn = sem("xn_ready")
        s_xt = sem("xn_transposed")
        s_xhi = sem("xn_hi_ready")
        s_xlo = sem("xn_lo_ready")
        s_ct = sem("ctx_transposed")
        s_cthi = sem("ctxT_hi_ready")
        s_ctlo = sem("ctxT_lo_ready")
        s_ab = sem("dist_products")
        s_dsum = sem("dist_sum")
        s_d2 = sem("dist_squared")
        s_root = sem("dist_root")
        s_dist = sem("dist_ready")
        s_dst = [sem(f"dist_stored{b}") for b in range(B)]
        s_dld = [sem(f"dist_lanes{b}") for b in range(B)]
        s_halo = sem("wave_halo")
        s_scan = sem("wave_row")
        s_steps = sem("wave_steps")
        s_lgst = [sem(f"steps_stored{b}") for b in range(B)]
        s_lgld = [sem(f"steps_rows{b}") for b in range(B)]
        s_trow = sem("t_rows_ready")
        s_tch = [sem(f"chase_rows{b}") for b in range(B)]
        s_chase = sem("chase_step")
        s_et = sem("entries_transposed")
        s_er = sem("entries_by_row")
        s_path = sem("path_ready")
        s_xa = sem("aligned_sum")
        s_upd = sem("x_updated")
        s_out = sem("out_stored")

        x_t = x.rearrange("b (q p) h -> b p q h", p=P)
        out_t = out.rearrange("b (q p) h -> b p q h", p=P)

        def at(t, offset, ap):
            return bass.AP(tensor=t.tensor, offset=t.offset + offset, ap=ap)

        def sl(b):
            return slice(S * b, S * (b + 1))

        block = ctx.enter_context(nc.Block())
        POOL_CONST = 10 + B

        @block.sync
        def _(sp):
            for b in range(B):
                sp.dma_start(x_res[:, TPB * b:TPB * (b + 1), :], x_t[b]).then_inc(s_x[b], 16)
                if b == 0:
                    sp.dma_start(ctx_sb[:], ctx_1024.rearrange("b k d -> k b d")).then_inc(s_ctx, 16)
            sp.dma_start(gates[:, 0:2], g_xattn.partition_broadcast(P)).then_inc(s_gate, 16)
            sp.dma_start(gates[:, 2:4], g_ffn.partition_broadcast(P)).then_inc(s_gate, 16)
            sp.dma_start(router[0][:], r0_w).then_inc(s_rw[0], 16)
            for m, w in enumerate((Wq, Wk, Wv, Wo)):
                sp.dma_start(w4[:, m, :], w).then_inc(s_aw, 16)
            for m, v in enumerate((bq, bk)):
                sp.dma_start(bias2[:, m:m + 1], v.rearrange("(p o) -> p o", o=1)).then_inc(s_aw, 16)
            for m, v in enumerate((bv, bo)):
                sp.dma_start(brow2[:, m, :], v.rearrange("(o p) -> o p", o=1)).then_inc(s_aw, 16)
            sp.dma_start(router1_rows[:], r1_w).then_inc(s_rw[1], 16)
            sp.wait_ge(s_pool, 2)
            sp.dma_start(scr_one.rearrange("(p c) -> p c", c=P), ones[0:TOK // P, :]).then_inc(s_one, 16)
            sp.dma_start(w_raw[:, 0, 0:I0], sg0).then_inc(FF_RAW[0][0], 16)
            sp.dma_start(w_raw[:, 0, UP:UP + I0], su0).then_inc(FF_RAW[0][0], 16)
            sp.dma_start(w_raw[0:I0, 0, DOWN:DOWN + P], sd0).then_inc(FF_RAW[0][0], 16)
            sp.wait_ge(s_pool, POOL_CONST)
            sp.dma_start(scr_d.rearrange("b c s w -> (b c) (s w)"),
                         dl[0:B * CH].rearrange("p s w -> p (s w)")).then_inc(s_zero, 16)
            sp.wait_ge(s_zero, 16)
            for b in range(B):
                sp.wait_ge(s_dist, b + 1)
                sp.dma_start(at(scr_d[b], 0, [[CW, KEYS], [LANE + CW, CH], [1, CW]]),
                             drows[0:KEYS, b, :].rearrange("i (c w) -> i c w", w=CW)).then_inc(s_dst[b], 16)
            for b in range(B):
                sp.wait_ge(s_dst[b], 16)
                sp.dma_start(dl[LANES[b]:LANES[b] + CH].rearrange("c s w -> c (s w)"),
                             scr_d[b].rearrange("c s w -> c (s w)")).then_inc(s_dld[b], 16)
            sp.wait_ge(s_steps, SLOTS)
            for b in range(B):
                sp.dma_start(scr_lg[b].rearrange("c s a w -> c (s a w)"),
                             lg[LANES[b]:LANES[b] + CH].rearrange("c s a w -> c (s a w)")).then_inc(s_lgst[b], 16)
            for b in range(B):
                sp.wait_ge(s_lgst[b], 16)
                for a in range(2):
                    sp.dma_start(lgr[0:KEYS, a, b, :].rearrange("i (c w) -> i c w", w=CW),
                                 at(scr_lg[b], a * CW, [[2 * CW, KEYS], [2 * (LANE + CW), CH], [1, CW]])
                                 ).then_inc(s_lgld[b], 16)
            for b in range(B):
                sp.wait_ge(s_trow, b + 1)
                sp.dma_start(chase[b:b + 1], trow[0:KEYS, b, :]).then_inc(s_tch[b], 16)

            def raw0(g, j):
                e = bass.ds(2 * g - 2, 2)
                dst = w_raw[:, j, 0:DOWN].rearrange("p (m e i) -> p m e i", m=2, e=2)
                sp.dma_start(dst[:, 0], eg0[e].rearrange("e h i -> h e i")).then_inc(FF_RAW[0][j], 16)
                sp.dma_start(dst[:, 1], eu0[e].rearrange("e h i -> h e i")).then_inc(FF_RAW[0][j], 16)
                sp.dma_start(w_raw[:, j, DOWN:DOWN + P],
                             ed0[e].rearrange("e i h -> (e i) h")).then_inc(FF_RAW[0][j], 16)

            def mask0(g, j):
                for k in range(2):
                    row = scr_mask[0][bass.ds(2 * g - 2 + k, 1), :].rearrange("a t -> (a t)")
                    sp.dma_start(mask[I0 * k:I0 * (k + 1), j, :], row.partition_broadcast(I0)).then_inc(FF_MASK[0][j], 16)

            def raw1(g, j):
                sp.dma_start(w_raw[:, j, :], scr_w1[g]).then_inc(FF_RAW[1][j], 16)

            def mask1(g, j):
                parts = pieces(P * g, min(P * (g + 1), I1 * (E1 + 1)))
                if len(parts) == 1:
                    e, i, n = parts[0]
                    parts = [(e, i, I0), (e, i, P - I0)]
                at_row = 0
                for e, i, n in parts:
                    row = scr_one if e < 0 else scr_mask[1][e]
                    sp.dma_start(mask[at_row:at_row + n, j, :], row.partition_broadcast(n)).then_inc(FF_MASK[1][j], 16)
                    at_row += n

            def stored_masks(f):
                sp.wait_ge(s_mrow, CHUNKS * (f + 1))
                sp.dma_start(scr_mask[f], maskT[0:EXPERTS[f], :]).then_inc(s_mst, 16)
                sp.wait_ge(s_mst, 16 * (f + 1))

            sp.wait_ge(s_one, 16)
            raw0(1, 1)
            sp.wait_ge(s_upd, B)
            for k in range(2):
                sp.dma_start(mask[I0 * k:I0 * (k + 1), 0, :], scr_one.partition_broadcast(I0)).then_inc(FF_MASK[0][0], 16)
            stored_masks(0)
            mask0(1, 1)
            with sp.Fori(0, GROUPS[0] // 2 - 1) as t:
                for j in range(2):
                    g = 2 * t + 2 + j
                    sp.wait_ge(FF[0]["wlo"], g - 1)
                    raw0(g, j)
                    sp.wait_ge(FF[0]["act"], CHUNKS * (g - 1))
                    mask0(g, j)
            g = GROUPS[0] - 1
            sp.wait_ge(FF[0]["wlo"], g - 1)
            raw0(g, 0)
            sp.wait_ge(FF[0]["act"], CHUNKS * (g - 1))
            mask0(g, 0)
            for g in range(GROUPS[1]):
                j = g % 2
                if g == 0:
                    for i in range(2):
                        sp.wait_ge(s_pst[i], 16 * ((GROUPS[1] + 1 - i) // 2))
                if g < 2:
                    sp.wait_ge(FF[0]["wlo"], GROUPS[0])
                    raw1(g, j)
                    if g == 0:
                        sp.wait_ge(s_au, TILES)
                    mask1(g, j)
                else:
                    if g == 2:
                        stored_masks(1)
                    sp.wait_ge(FF[1]["wlo"], g - 1)
                    raw1(g, j)
                    sp.wait_ge(FF[1]["act"], CHUNKS * (g - 1))
                    mask1(g, j)
            sp.wait_ge(s_upd, 3 * B)
            sp.wait_ge(s_au, TILES)
            for b in range(B):
                sp.dma_start(out_t[b], x_res[:, TPB * b:TPB * (b + 1), :]).then_inc(s_out, 16)
            sp.wait_ge(s_out, 16 * B)

        @block.gpsimd
        def _(pool):
            nc.gpsimd.memset(w_raw[:, 0, :], 0.0).then_inc(s_pool, 1)
            nc.gpsimd.memset(ones[:], 1.0).then_inc(s_pool, 1)
            pool.wait_ge(s_pool, 2)
            nc.gpsimd.affine_select(out=ident[:], in_=ones[:], compare_op=ALU.is_equal, fill=0.0, base=0,
                                    pattern=[[-1, P]], channel_multiplier=1).then_inc(s_pool, 1)
            nc.gpsimd.iota(iota_e[:], pattern=[[1, E1]], base=0, channel_multiplier=0,
                           allow_small_or_imprecise_dtypes=True).then_inc(s_pool, 1)
            nc.gpsimd.affine_select(out=headmask[:], in_=ones[:, 0:HEADS], compare_op=ALU.is_ge, fill=0.0, base=0,
                                    pattern=[[-HD, HEADS]], channel_multiplier=1).then_inc(s_pool, 1)
            pool.wait_ge(s_pool, 5)
            nc.gpsimd.affine_select(out=headmask[:], in_=headmask[:], compare_op=ALU.is_ge, fill=0.0, base=HD - 1,
                                    pattern=[[HD, HEADS]], channel_multiplier=-1).then_inc(s_pool, 1)
            nc.gpsimd.memset(dl, 0.0).then_inc(s_pool, 1)
            nc.gpsimd.iota(jrow[:], pattern=[[1, S]], base=0, channel_multiplier=0,
                           allow_small_or_imprecise_dtypes=True).then_inc(s_pool, 1)
            nc.gpsimd.memset(rst[:, 0, :], BIG).then_inc(s_pool, 1)
            nc.gpsimd.memset(ecol[:], S - 1.0).then_inc(s_pool, 1)
            pool.wait_ge(s_pool, 10)
            for b in range(B):
                nc.gpsimd.memset(rst[LANES[b]:LANES[b] + 1, 0, 0:1], 0.0).then_inc(s_pool, 1)

            pool.wait_ge(s_pool, POOL_CONST)
            loads = [0, 0]

            def prep_store(g):
                pool.wait_ge(s_pout, g + 1)
                pool.dma_start(scr_w1[g], prep_out[:, g % 2, :]).then_inc(s_pst[g % 2], 16)

            for g in range(GROUPS[1]):
                j = g % 2
                if g >= 2:
                    pool.wait_ge(s_pt, g - 1)
                if P * (g + 1) > I1 * (E1 + 1):
                    nc.gpsimd.memset(prep_in[:, j, :], 0.0).then_inc(s_pzero, 1)
                    pool.wait_ge(s_pzero, 1)
                at_row = 0
                for e, i, n in pieces(P * g, min(P * (g + 1), I1 * (E1 + 1))):
                    wg, wu, wd = (swg1, swu1, swd1) if e < 0 else (wg1[e], wu1[e], wd1[e])
                    rows = slice(at_row, at_row + n)
                    pool.dma_start(prep_in[rows, j, 0:P], wg[i:i + n, :]).then_inc(s_pin[j], 16)
                    pool.dma_start(prep_in[rows, j, UP:UP + P], wu[i:i + n, :]).then_inc(s_pin[j], 16)
                    pool.dma_start(prep_in[:, j, DOWN + at_row:DOWN + at_row + n], wd[:, i:i + n]).then_inc(s_pin[j], 16)
                    at_row += n
                if g >= 1:
                    prep_store(g - 1)
            prep_store(GROUPS[1] - 1)

            def split_lo(f, g, j):
                pool.wait_ge(FF[f]["whi"], g + 1)
                nc.gpsimd.tensor_tensor(w_lo[:, j, :], w_raw[:, j, :], w_hi[:, j, :].bitcast(F32),
                                        ALU.subtract).then_inc(FF[f]["wlo"], 1)

            def attention_prep():
                pool.wait_ge(s_upd, B)
                nc.gpsimd.memset(v_ext[0:KEYS], 1.0).then_inc(s_vone, 1)
                pool.wait_ge(s_wqh, 1)
                nc.gpsimd.tensor_tensor(wq_lo[:], w4[:, 0, :], wq_hi[:].bitcast(F32), ALU.subtract).then_inc(s_wql, 1)
                pool.wait_ge(s_khi, 1)
                nc.gpsimd.tensor_tensor(kT_lo, kT, kT_hi.bitcast(F32), ALU.subtract).then_inc(s_klo, 1)
                pool.wait_ge(s_klo, 1)
                for h in range(HEADS):
                    mm = nc.gpsimd.tensor_scalar(kbd_lo[:, :, h, :], kT_lo.bitcast(F32).rearrange("p (b k) -> p b k", b=B),
                                                 headmask[:, h:h + 1], None, ALU.mult)
                mm.then_inc(s_kbl, 1)

            def attention():
                def tile(i, j):
                    if isinstance(i, int):
                        tok = slice(P * i, P * (i + 1))
                        pool.wait_ge(s_qlo, min(i // TPB + 1, CHUNKS))
                        if i >= 2:
                            pool.wait_ge(s_sc, 3 * (i - 1))
                    else:
                        tok = bass.ds(P * i, P)
                        pool.wait_ge(s_sc, 3 * i - 3)
                    nc.gpsimd.tensor_copy(qs_hi[:, j, :], qT_hi[:, tok].bitcast(F32))
                    nc.gpsimd.tensor_copy(qs_lo[:, j, :], qT_lo[:, tok].bitcast(F32)).then_inc(s_qs, 1)

                for i in range(TPB):
                    tile(i, i % 2)
                pool.wait_ge(s_qlo, CHUNKS)
                with pool.Fori(1, B) as t:
                    for q in range(TPB):
                        tile(TPB * t + q, q % 2)

            def feed_forward(f):
                T = GROUPS[f] // 2
                split_lo(f, 0, 0)
                split_lo(f, 1, 1)
                if f == 0:
                    attention_prep()

                def unit(g, k, j, last=False):
                    u = CHUNKS * g + k
                    if k == 2 and not last and not (isinstance(g, int) and g == 0):
                        split_lo(f, g + 1, 1 - j)
                    pool.wait_ge(FF[f]["ahi"], u + 1)
                    if not (isinstance(g, int) and u < 2):
                        pool.wait_ge(FF[f]["down"], u - 1)
                    nc.gpsimd.tensor_tensor(act_lo[:, k % 2, :], act_a[:, k % 2, :], act_hi[:, k % 2, :].bitcast(F32),
                                            ALU.subtract).then_inc(FF[f]["alo"], 1)

                for k in range(CHUNKS):
                    unit(0, k, 0)
                with pool.Fori(0, T - 1) as t:
                    for jj in range(2):
                        for k in range(CHUNKS):
                            unit(2 * t + 1 + jj, k, 1 - jj)
                for jj in range(2):
                    for k in range(CHUNKS):
                        unit(2 * T - 1 + jj, k, 1 - jj, last=jj == 1)

            feed_forward(0)
            attention()
            feed_forward(1)

        @block.scalar
        def _(act):
            act.wait_ge(s_gate, 32)
            nc.scalar.activation(tgate[:], gates[:], ACT.Tanh)
            act.wait_ge(s_ct, 1)
            nc.scalar.activation(ctxT[:], ps[6][:, 0:B * KEYS].rearrange("p (b k) -> p b k", b=B), ACT.Copy)
            nc.scalar.activation(ctxT_hi[:], ps[6][:, 0:B * KEYS].rearrange("p (b k) -> p b k", b=B),
                                 ACT.Copy).then_inc(s_cthi, 1)

            def norm(k):
                act.wait_ge(s_bn, k + 1)
                nc.scalar.activation(std[:], veps[:], ACT.Sqrt).then_inc(s_std, 1)
                for b in range(B):
                    act.wait_ge(s_xt, B * k + b + 1)
                    bank = ps[b % 2]
                    if k == 0:
                        nc.scalar.activation(xn_hi[:, sl(b)], bank[:], ACT.Copy)
                        if b >= 2:
                            act.wait_ge(s_ab, 2 * b - 2)
                        nc.scalar.activation(sq[:, b % 2, :], bank[:], ACT.Square).then_inc(s_xhi, 1)
                    else:
                        nc.scalar.activation(xn_hi[:, sl(b)], bank[:], ACT.Copy).then_inc(s_xhi, 1)

            norm(0)
            for b in range(B):
                act.wait_ge(s_d2, b + 1)
                nc.scalar.activation(droot[0:KEYS, b, :], d2[0:KEYS, b, :], ACT.Sqrt).then_inc(s_act, 1)
                act.wait_ge(s_act, b + 1)
                nc.scalar.activation(droot2[0:KEYS, b, :], droot[0:KEYS, b, :], ACT.Square).then_inc(s_root, 1)
            for g in range(GROUPS[1]):
                act.wait_ge(s_pt, g + 1)
                if g >= 2:
                    act.wait_ge(s_pst[g % 2], 16 * (g // 2))
                nc.scalar.activation(prep_out[:, g % 2, :], ps[7][:, 0:WIDE], ACT.Copy).then_inc(s_pout, 1)
            act.wait_ge(s_rw[0], 16)
            nc.scalar.activation(router_hi[0][:], router[0][:], ACT.Copy).then_inc(s_rhi, 1)
            act.wait_ge(s_rt, 1)
            nc.scalar.activation(router[1][:], ps[6][:, 0:E1], ACT.Copy)
            nc.scalar.activation(router_hi[1][:], ps[6][:, 0:E1], ACT.Copy).then_inc(s_rhi, 1)
            act.wait_ge(s_et, 1)
            nc.scalar.activation(erow[:], ps[6][0:KEYS, CHASE], ACT.Copy).then_inc(s_er, 1)

            def route(f):
                for h in range(2):
                    act.wait_ge(s_logit, 2 * f + h + 1)
                    tiles = slice(h * TILES // 2, (h + 1) * TILES // 2)
                    logits = ps[2 + h][:, 0:TILES // 2 * EXPERTS[f]].rearrange("p (t e) -> p t e", e=EXPERTS[f])
                    nc.scalar.activation(aff[f][:, tiles, :], logits, ACT.Sigmoid if f == 0 else ACT.Copy).then_inc(s_score, 1)
                if f == 0:
                    attention_prep()
                else:
                    act.wait_ge(s_rsub, 1)
                    nc.scalar.activation(rest[1], rest[1], ACT.Exp).then_inc(s_rexp, 1)
                for n in range(CHUNKS):
                    act.wait_ge(s_selT, CHUNKS * f + n + 1)
                    nc.scalar.activation(maskT[0:EXPERTS[f], 512 * n:512 * (n + 1)], ps[n][0:EXPERTS[f], :],
                                         ACT.Copy).then_inc(s_mrow, 1)

            def feed_forward(f):
                T, units = GROUPS[f] // 2, CHUNKS * GROUPS[f]

                def hi(u, j):
                    act.wait_ge(FF[f]["act"], u + 1)
                    if not (isinstance(u, int) and u < 2):
                        act.wait_ge(FF[f]["alo"], u - 1)
                        act.wait_ge(FF[f]["down"], u - 1)
                    nc.scalar.activation(act_hi[:, j, :], act_a[:, j, :], ACT.Copy).then_inc(FF[f]["ahi"], 1)

                def unit(g, k, j, load=None):
                    u = CHUNKS * g + k
                    if k == 2 and load is not None:
                        act.wait_ge(FF[f]["down"], CHUNKS * g)
                        act.wait_ge(FF_RAW[f][1 - j], 16 * RAW_DMAS[f] * load)
                        nc.scalar.activation(w_hi[:, 1 - j, :], w_raw[:, 1 - j, :], ACT.Copy).then_inc(FF[f]["whi"], 1)
                    act.wait_ge(FF[f]["gate"], u + 1)
                    if not (isinstance(g, int) and u < 2):
                        act.wait_ge(FF[f]["t"], u - 1)
                    nc.scalar.activation(act_s[:, k % 2, :], ps[4 + k % 2][:], ACT.Silu).then_inc(FF[f]["silu"], 1)
                    if not (isinstance(g, int) and u < 1):
                        hi(u - 1, (k + 1) % 2)

                for k in range(CHUNKS):
                    unit(0, k, 0)
                with act.Fori(0, T - 1) as t:
                    for jj in range(2):
                        for k in range(CHUNKS):
                            unit(2 * t + 1 + jj, k, 1 - jj, t + 2)
                for jj in range(2):
                    for k in range(CHUNKS):
                        unit(2 * T - 1 + jj, k, 1 - jj, T + 1 if jj == 0 else None)
                hi(units - 1, 1)
                for n in range(CHUNKS):
                    act.wait_ge(FF[f]["sum"], n + 1)
                    nc.scalar.activation(yT[:, n, :], ps[n][:], ACT.Copy).then_inc(FF[f]["yT"], 1)

            def split_first(f):
                for g in range(2):
                    act.wait_ge(FF_RAW[f][g], 16 * RAW_DMAS[f])
                    nc.scalar.activation(w_hi[:, g, :], w_raw[:, g, :], ACT.Copy).then_inc(FF[f]["whi"], 1)

            def attention_prep():
                act.wait_ge(s_aw, 16 * 8)
                nc.scalar.activation(wq_hi[:], w4[:, 0, :], ACT.Copy).then_inc(s_wqh, 1)
                act.wait_ge(s_kp, 1)
                nc.scalar.activation(kT, ps[0][:, 0:B * KEYS], ACT.Identity, bias=bias2[:, 1:2])
                nc.scalar.activation(kT_hi, ps[0][:, 0:B * KEYS], ACT.Identity, bias=bias2[:, 1:2]).then_inc(s_khi, 1)
                act.wait_ge(s_vp, 1)
                act.wait_ge(s_vone, 1)
                nc.scalar.activation(v_ext[0:KEYS, :, 0:HD], ps[1][0:KEYS, :].rearrange("p (h d) -> p h d", d=HD),
                                     ACT.Copy).then_inc(s_vx, 1)
                act.wait_ge(s_khi, 1)
                act.wait_ge(s_pool, POOL_CONST)
                for h in range(HEADS):
                    mm = nc.scalar.activation(kbd_hi[:, :, h, :], kT_hi.bitcast(F32).rearrange("p (b k) -> p b k", b=B),
                                              ACT.Copy, scale=headmask[:, h:h + 1])
                mm.then_inc(s_kbh, 1)

            def attention():
                for n in range(CHUNKS):
                    act.wait_ge(s_qp, n + 1)
                    nc.scalar.activation(qT_hi[:, 512 * n:512 * (n + 1)], ps[3 + n % 2][:], ACT.Identity,
                                         bias=bias2[:, 0:1]).then_inc(s_qhi, 1)

                def copy_av(i):
                    act.wait_ge(s_avt, i + 1)
                    nc.scalar.activation(avT, ps[6][:, 0:P], ACT.Copy).then_inc(s_avc, 1)

                def copy_exp(i):
                    if not (isinstance(i, int) and i == 0):
                        act.wait_ge(s_av, i)
                    for r in range(HEADS // HT):
                        act.wait_ge(s_tr, HEADS // HT * i + r + 1)
                        nc.scalar.activation(expT[0:KEYS, HT * r:HT * (r + 1), :].rearrange("p h t -> p (h t)"),
                                             ps[3 + r % 2][0:KEYS, :], ACT.Copy).then_inc(s_ev, 1)

                def exp(i, j):
                    act.wait_ge(s_sub, 3 * i + 3)
                    nc.scalar.activation(expw[:, j, :], expw[:, j, :], ACT.Exp, scale=float(HD) ** -0.5).then_inc(s_exp, 1)

                def step(i, j):
                    first = isinstance(i, int)
                    if not (first and i < 2):
                        copy_av(i - 2)
                    if not (first and i < 1):
                        copy_exp(i - 1)
                    exp(i, j)

                for i in range(TPB):
                    step(i, i % 2)
                with act.Fori(1, B) as t:
                    for q in range(TPB):
                        step(TPB * t + q, q % 2)
                copy_av(TILES - 2)
                copy_exp(TILES - 1)
                copy_av(TILES - 1)

            split_first(0)
            norm(1)
            route(0)
            feed_forward(0)
            norm(2)
            attention()
            split_first(1)
            norm(3)
            route(1)
            feed_forward(1)

        @block.tensor
        def _(pe):
            pe.wait_ge(s_ctx, 16)
            pe.wait_ge(s_pool, 3)
            for b in range(B):
                mm = nc.tensor.transpose(ps[6][:, KEYS * b:KEYS * (b + 1)], ctx_sb[:, b, :], ident[0:KEYS, 0:KEYS])
            mm.then_inc(s_ct, 1)

            def norm(k, after=None):
                for b in range(B):
                    if b >= 2:
                        pe.wait_ge(s_xlo, B * k + b - 1)
                    for q in range(TPB):
                        t = TPB * b + q
                        pe.wait_ge(s_xn, TILES * k + t + 1)
                        mm = nc.tensor.transpose(ps[b % 2][:, P * q:P * (q + 1)], xn[:, t, :], ident[:])
                    mm.then_inc(s_xt, 1)
                    if after is not None and b >= 1:
                        after(b - 1)
                if after is not None:
                    after(B - 1)

            def distances(b):
                pe.wait_ge(s_xhi, b + 1)
                if b >= 2:
                    pe.wait_ge(s_d2, b - 1)
                nc.tensor.matmul(ps[4 + b % 2][0:KEYS, :], ones[:, 0:KEYS], sq[:, b % 2, :],
                                 start=True, stop=True).then_inc(s_ab, 1)
                pe.wait_ge(s_ctlo, 1)
                pe.wait_ge(s_xlo, b + 1)
                prod = ps[2 + b % 2][0:KEYS, :]
                nc.tensor.matmul(prod, ctxT_hi[:, b, :], xn_hi[:, sl(b)], start=True, stop=False)
                nc.tensor.matmul(prod, ctxT_lo[:, b, :], xn_hi[:, sl(b)], start=False, stop=False)
                nc.tensor.matmul(prod, ctxT_hi[:, b, :], xn_lo[:, sl(b)], start=False, stop=True).then_inc(s_ab, 1)

            norm(0, distances)
            loads = [0, 0]
            for g in range(GROUPS[1]):
                j = g % 2
                loads[j] += 3 * 16 * len(pieces(P * g, min(P * (g + 1), I1 * (E1 + 1))))
                pe.wait_ge(s_pin[j], loads[j])
                if g >= 1:
                    pe.wait_ge(s_pout, g)
                for m in range(3):
                    mm = nc.tensor.transpose(ps[7][:, P * m:P * (m + 1)], prep_in[:, j, P * m:P * (m + 1)], ident[:])
                mm.then_inc(s_pt, 1)
            pe.wait_ge(s_rw[1], 16)
            pe.wait_ge(s_ctlo, 1)
            nc.tensor.transpose(ps[6][:, 0:E1], router1_rows[:], ident[0:E1, 0:E1]).then_inc(s_rt, 1)
            pe.wait_ge(s_chase, KEYS - 1)
            nc.tensor.transpose(ps[6][0:KEYS, 0:P], ecol[:], ident[:]).then_inc(s_et, 1)
            for b in range(B):
                pe.wait_ge(s_path, b + 1)
                for q in range(TPB):
                    mm = nc.tensor.matmul(ps[b][:, P * q:P * (q + 1)], pmask[0:KEYS, b, P * q:P * (q + 1)],
                                          ctx_sb[:, b, :], start=True, stop=True)
                mm.then_inc(s_xa, 1)

            def three_pass(out, w_h, w_l, x_h, x_l, start=True, stop=True):
                nc.tensor.matmul(out, w_h, x_h, start=start, stop=False)
                nc.tensor.matmul(out, w_l, x_h, start=False, stop=False)
                return nc.tensor.matmul(out, w_h, x_l, start=False, stop=stop)

            def attention_prep():
                pe.wait_ge(s_aw, 16 * 8)
                nc.tensor.matmul(ps[0][:, 0:B * KEYS], w4[:, 1, :], ctxT[:].rearrange("p b k -> p (b k)"),
                                 start=True, stop=True).then_inc(s_kp, 1)
                for b in range(B):
                    out_b = ps[1][0:KEYS, P * b:P * (b + 1)]
                    nc.tensor.matmul(out_b, ctxT[:, b, :], w4[:, 2, :], start=True, stop=False)
                    mm = nc.tensor.matmul(out_b, ones[0:1, 0:KEYS], brow2[:, 0, :], start=False, stop=True)
                mm.then_inc(s_vp, 1)
                pe.wait_ge(s_khi, 1)
                pe.wait_ge(s_vx, 1)

            def attention():
                pe.wait_ge(s_wql, 1)
                for n in range(CHUNKS):
                    pe.wait_ge(s_xlo, 2 * B + n + 1)
                    if n >= 2:
                        pe.wait_ge(s_qlo, n - 1)
                    tok = slice(512 * n, 512 * (n + 1))
                    three_pass(ps[3 + n % 2][:], wq_hi[:], wq_lo[:], xn_hi[:, tok], xn_lo[:, tok]).then_inc(s_qp, 1)
                pe.wait_ge(s_kbh, 1)
                pe.wait_ge(s_kbl, 1)
                pe.wait_ge(s_qlo, CHUNKS)

                def scores(i, b, j):
                    pe.wait_ge(s_qs, i + 1)
                    for r, (h0, h1) in enumerate(HSPLIT):
                        if not (isinstance(i, int) and i == 0):
                            pe.wait_ge(s_sub, 3 * i - 2 + r)
                        if isinstance(b, int):
                            k_hi, k_lo = kbd_hi[:, b, h0:h1, :], kbd_lo[:, b, h0:h1, :]
                        else:
                            k_hi, k_lo = [k[:].rearrange("p b h k -> p (b h k)")[:, bass.ds(b * (HEADS * KEYS) + h0 * KEYS, (h1 - h0) * KEYS)]
                                          for k in (kbd_hi, kbd_lo)]
                        three_pass(ps[r][:, 0:(h1 - h0) * KEYS], qs_hi[:, j, :], qs_lo[:, j, :], k_hi, k_lo).then_inc(s_sc, 1)

                def exp_back(i, j):
                    pe.wait_ge(s_exp, i + 1)
                    e = expw[:, j, :].rearrange("p (h k) -> p h k", h=HEADS)
                    for r in range(HEADS // HT):
                        n = HEADS // HT * i + r
                        if not (isinstance(i, int) and n < 2):
                            pe.wait_ge(s_ev, n - 1)
                        for h in range(HT):
                            mm = nc.tensor.transpose(ps[3 + r % 2][0:KEYS, P * h:P * (h + 1)], e[:, HT * r + h, :], ident[:])
                        mm.then_inc(s_tr, 1)

                def values(i, b):
                    if not (isinstance(i, int) and i == 0):
                        pe.wait_ge(s_nrm, i)
                    for h in range(HEADS):
                        if h % HT == 0:
                            pe.wait_ge(s_ev, HEADS // HT * i + h // HT + 1)
                        if isinstance(b, int):
                            v = v_ext[0:KEYS, HEADS * b + h, :]
                        else:
                            v = v_ext[0:KEYS].rearrange("p h d -> p (h d)")[:, bass.ds(b * (HEADS * (HD + 1)) + h * (HD + 1), HD + 1)]
                        mm = nc.tensor.matmul(ps[5][:, (HD + 1) * h:(HD + 1) * (h + 1)], expT[0:KEYS, h, :], v,
                                              start=True, stop=True)
                    mm.then_inc(s_av, 1)

                def av_back(i, j):
                    pe.wait_ge(s_nrm, i + 1)
                    if not (isinstance(i, int) and i == 0):
                        pe.wait_ge(s_au, i)
                    nc.tensor.transpose(ps[6][:, 0:P], av[:, j, :], ident[:]).then_inc(s_avt, 1)

                def project(i):
                    pe.wait_ge(s_avc, i + 1)
                    nc.tensor.matmul(ps[6][:, P:2 * P], avT, w4[:, 3, :], start=True, stop=False)
                    nc.tensor.matmul(ps[6][:, P:2 * P], ones[0:1, :], brow2[:, 1, :], start=False, stop=True).then_inc(s_wo, 1)

                def step(i, b, b_before, j):
                    first = isinstance(i, int)
                    scores(i, b, j)
                    if not (first and i < 2):
                        av_back(i - 2, j)
                    if not (first and i < 1):
                        exp_back(i - 1, 1 - j)
                    if not (first and i < 2):
                        project(i - 2)
                    if not (first and i < 1):
                        values(i - 1, b_before)

                for i in range(TPB):
                    step(i, 0, 0, i % 2)
                with pe.Fori(1, B) as t:
                    for q in range(TPB):
                        step(TPB * t + q, t, t - 1 if q == 0 else t, q % 2)
                av_back(TILES - 2, 0)
                exp_back(TILES - 1, 1)
                project(TILES - 2)
                values(TILES - 1, B - 1)
                av_back(TILES - 1, 1)
                project(TILES - 1)

            def route(f, k):
                E = EXPERTS[f]
                pe.wait_ge(s_rlo, f + 1)
                pe.wait_ge(s_xlo, B * (k + 1))
                for h in range(2):
                    for i in range(TILES // 2):
                        t = TILES // 2 * h + i
                        tok = slice(P * t, P * (t + 1))
                        mm = three_pass(ps[2 + h][:, E * i:E * (i + 1)], xn_hi[:, tok], xn_lo[:, tok],
                                        router_hi[f][:], router_lo[f][:])
                    mm.then_inc(s_logit, 1)
                if f == 0:
                    attention_prep()
                for n in range(CHUNKS):
                    for q in range(4):
                        t = 4 * n + q
                        pe.wait_ge(s_sel, TILES * f + t + 1)
                        mm = nc.tensor.transpose(ps[n][0:E, P * q:P * (q + 1)], wsel[f][:, t, :], ident[:])
                    mm.then_inc(s_selT, 1)

            def feed_forward(f):
                T, units = GROUPS[f] // 2, CHUNKS * GROUPS[f]

                def gate_up(g, k, j):
                    u = CHUNKS * g + k
                    if k == 0:
                        pe.wait_ge(FF[f]["wlo"], g + 1)
                    if not (isinstance(g, int) and u < 2):
                        pe.wait_ge(FF[f]["silu"], u - 1)
                        pe.wait_ge(FF[f]["t"], u - 1)
                    tok = slice(512 * k, 512 * (k + 1))
                    three_pass(ps[4 + k % 2][:], w_hi[:, j, 0:P], w_lo[:, j, 0:P],
                               xn_hi[:, tok], xn_lo[:, tok]).then_inc(FF[f]["gate"], 1)
                    three_pass(ps[6 + k % 2][:], w_hi[:, j, UP:UP + P], w_lo[:, j, UP:UP + P],
                               xn_hi[:, tok], xn_lo[:, tok]).then_inc(FF[f]["up"], 1)

                def down(u, n, j):
                    i = n % 2
                    pe.wait_ge(FF[f]["ahi"], u + 1)
                    nc.tensor.matmul(ps[n][:], w_hi[:, j, DOWN:DOWN + P], act_hi[:, i, :], start=False, stop=False)
                    nc.tensor.matmul(ps[n][:], w_lo[:, j, DOWN:DOWN + P], act_hi[:, i, :], start=False, stop=False)
                    pe.wait_ge(FF[f]["alo"], u + 1)
                    nc.tensor.matmul(ps[n][:], w_hi[:, j, DOWN:DOWN + P], act_lo[:, i, :],
                                     start=False, stop=False).then_inc(FF[f]["down"], 1)

                gate_up(0, 0, 0)
                gate_up(0, 1, 0)
                for n in range(CHUNKS):
                    pe.wait_ge(s_mrow, CHUNKS * f + n + 1)
                    nc.tensor.matmul(ps[n][:], zeros[0:1, 0:P], zeros[0:1, :], start=True, stop=False)
                for k in range(2, CHUNKS):
                    gate_up(0, k, 0)
                    down(k - 2, k - 2, 0)
                with pe.Fori(0, T) as t:
                    for jj in range(2):
                        g, j = 2 * t + 1 + jj, 1 - jj
                        for k in range(CHUNKS):
                            gate_up(g, k, j)
                            down(CHUNKS * g + k - 2, (k + 2) % CHUNKS, j if k >= 2 else 1 - j)
                for n in range(CHUNKS - 2, CHUNKS):
                    down(units - CHUNKS + n, n, 0)
                for n in range(CHUNKS):
                    nc.tensor.matmul(ps[n][:], zeros[0:1, 0:P], zeros[0:1, :], start=False, stop=True).then_inc(FF[f]["sum"], 1)
                pe.wait_ge(FF[f]["t"], units)
                for n in range(CHUNKS):
                    pe.wait_ge(FF[f]["yT"], n + 1)
                    for q in range(4):
                        mm = nc.tensor.transpose(ps[4 + n][:, P * q:P * (q + 1)], yT[:, n, P * q:P * (q + 1)], ident[:])
                    mm.then_inc(FF[f]["back"], 1)

            norm(1)
            route(0, 1)
            feed_forward(0)
            norm(2)
            attention()
            norm(3)
            route(1, 3)
            feed_forward(1)

        @block.vector
        def _(dve):
            steps = [0]

            def done(ins):
                steps[0] += 1
                ins.then_inc(s_dve, 1)

            def settle():
                dve.wait_ge(s_dve, steps[0])

            def norm(k):
                for t in range(TILES):
                    if k == 0 and t % TPB == 0:
                        dve.wait_ge(s_x[t // TPB], 16)
                    if k in (1, 2) and t % TPB == 0:
                        dve.wait_ge(s_upd, B * (k - 1) + t // TPB + 1)
                    if k == 3:
                        dve.wait_ge(s_au, t + 1)
                    done(nc.vector.bn_stats(stats[:, t, :], x_res[:, t, :]))
                settle()
                for t in range(TILES):
                    done(nc.vector.bn_aggr(mv[:, t, :], stats[:, t, :]))
                settle()
                nc.vector.tensor_scalar(veps[:], mv[:, :, 1], LN_EPS, None, ALU.add).then_inc(s_bn, 1)
                dve.wait_ge(s_std, k + 1)
                done(nc.vector.reciprocal(rstd[:, 0, :], std[:]))
                settle()
                done(nc.vector.tensor_tensor(rstd[:, 1, :], rstd[:, 0, :], rstd[:, 0, :], ALU.mult))
                settle()
                done(nc.vector.tensor_tensor(rstd[:, 2, :], rstd[:, 1, :], veps[:], ALU.mult))
                settle()
                done(nc.vector.tensor_scalar(rstd[:, 1, :], rstd[:, 2, :], -0.5, 1.5, ALU.mult, ALU.add))
                settle()
                done(nc.vector.tensor_tensor(rstd[:, 3, :], rstd[:, 1, :], rstd[:, 0, :], ALU.mult))
                settle()
                for t in range(TILES):
                    nc.vector.tensor_scalar(xn[:, t, :], x_res[:, t, :], mv[:, t, 0:1], rstd[:, 3, t:t + 1],
                                            ALU.subtract, ALU.mult).then_inc(s_xn, 1)
                for b in range(B):
                    dve.wait_ge(s_xhi, B * k + b + 1)
                    nc.vector.tensor_tensor(xn_lo[:, sl(b)], ps[b % 2][:], xn_hi[:, sl(b)].bitcast(F32),
                                            ALU.subtract).then_inc(s_xlo, 1)

            dve.wait_ge(s_ctx, 16)
            done(nc.vector.tensor_tensor(aasq[:], ctx_sb[:], ctx_sb[:], ALU.mult))
            settle()
            done(nc.vector.tensor_reduce(aa[:], aasq[:], AX_X, ALU.add))
            dve.wait_ge(s_cthi, 1)
            nc.vector.tensor_tensor(ctxT_lo[:], ps[6][:, 0:B * KEYS].rearrange("p (b k) -> p b k", b=B),
                                    ctxT_hi[:].bitcast(F32), ALU.subtract).then_inc(s_ctlo, 1)
            norm(0)
            settle()
            for b in range(B):
                j = b % 2
                dve.wait_ge(s_ab, 2 * b + 2)
                done(nc.vector.tensor_scalar(dsum[0:KEYS, b, :], ps[4 + j][0:KEYS, :], aa[:, b:b + 1], None, ALU.add))
                settle()
                done(nc.vector.scalar_tensor_tensor(dsum[0:KEYS, b, :], ps[2 + j][0:KEYS, :], -2.0, dsum[0:KEYS, b, :],
                                                    ALU.mult, ALU.add))
                settle()
                nc.vector.tensor_scalar(d2[0:KEYS, b, :], dsum[0:KEYS, b, :], TINY, None, ALU.max).then_inc(s_d2, 1)
            for b in range(B):
                dve.wait_ge(s_root, b + 1)
                done(nc.vector.reciprocal(dsum[0:KEYS, b, :], droot[0:KEYS, b, :]))
                done(nc.vector.tensor_tensor(d2[0:KEYS, b, :], d2[0:KEYS, b, :], droot2[0:KEYS, b, :], ALU.subtract))
                settle()
                done(nc.vector.tensor_tensor(d2[0:KEYS, b, :], d2[0:KEYS, b, :], dsum[0:KEYS, b, :], ALU.mult))
                settle()
                nc.vector.scalar_tensor_tensor(drows[0:KEYS, b, :], d2[0:KEYS, b, :], 0.5, droot[0:KEYS, b, :],
                                               ALU.mult, ALU.add).then_inc(s_dist, 1)

            for b in range(B):
                dve.wait_ge(s_dld[b], 16)
            dve.wait_ge(s_pool, POOL_CONST)
            shift = [31] + list(range(CH - 1)) + [31] * (32 - CH)

            def left_steps(s):
                nc.vector.tensor_tensor(lg[:, s, 0, :], rst[:, s + 1, 0:CW], mst[:, s % MST, :], ALU.is_lt).then_inc(s_steps, 1)

            for s in range(SLOTS):
                if s >= 1:
                    dve.wait_ge(s_scan, s)
                prev, cur = rst[:, s, :], rst[:, s + 1, :]
                if s >= MST:
                    dve.wait_ge(s_steps, s - MST + 1)
                nc.vector.tensor_tensor(mst[:, s % MST, :], prev[:, 1:CW + 1], prev[:, 0:CW], ALU.min)
                nc.vector.stream_shuffle(cur[:, 0:1], prev[:, CW:CW + 1], shift).then_inc(s_halo, 1)
                nc.vector.tensor_tensor(lg[:, s, 1, :], prev[:, 0:CW], prev[:, 1:CW + 1], ALU.is_le)
                dve.wait_ge(s_halo, s + 1)
                nc.vector.tensor_tensor_scan(cur[:, 1:CW + 1], mst[:, s % MST, :], dl[:, s, :], cur[:, 0:1],
                                             ALU.min, ALU.add).then_inc(s_scan, 1)
                if s >= 1:
                    left_steps(s - 1)
            dve.wait_ge(s_scan, SLOTS)
            left_steps(SLOTS - 1)

            done(nc.vector.memset(srow[0:KEYS, :, S:S + 1], 2.0 * S))
            for b in range(B):
                dve.wait_ge(s_lgld[b], 32)
                jr = jrow[0:KEYS, :]
                left, diag = lgr[0:KEYS, 0, b, :], lgr[0:KEYS, 1, b, :]
                done(nc.vector.scalar_tensor_tensor(nlj[0:KEYS, b, :], left, 1.0, jr, ALU.is_lt, ALU.mult))
                done(nc.vector.tensor_tensor(nup[0:KEYS, b, :], left, diag, ALU.max))
                settle()
                done(nc.vector.tensor_tensor_scan(srow[0:KEYS, b, 0:S][:, ::-1],
                                                  left[:, ::-1], nlj[0:KEYS, b, :][:, ::-1], 2.0 * S, ALU.mult, ALU.add))
                done(nc.vector.scalar_tensor_tensor(ubig[0:KEYS, b, :], nup[0:KEYS, b, :], 2.0 * S, jr, ALU.mult, ALU.add))
                settle()
                nc.vector.tensor_tensor(trow[0:KEYS, b, :], ubig[0:KEYS, b, :], srow[0:KEYS, b, 1:S + 1],
                                        ALU.min).then_inc(s_trow, 1)

            dve.wait_ge(s_pool, POOL_CONST)
            nc.vector.tensor_scalar(zeros[:], jrow[0:1, :], 0.0, None, ALU.mult)
            for f in range(2):
                dve.wait_ge(s_rhi, f + 1)
                nc.vector.tensor_tensor(router_lo[f][:], router[f][:], router_hi[f][:].bitcast(F32),
                                        ALU.subtract).then_inc(s_rlo, 1)

            for b in range(B):
                dve.wait_ge(s_tch[b], 16)
            for i in range(KEYS - 1, 0, -1):
                if i < KEYS - 1:
                    dve.wait_ge(s_chase, KEYS - 1 - i)
                nc.vector.tensor_scalar(junk[CHASE, 1:S], chase[:, i, 1:S], ecol[CHASE, i:i + 1], 0.0, ALU.is_le, ALU.add,
                                        accum_out=ecol[CHASE, i - 1:i]).then_inc(s_chase, 1)

            dve.wait_ge(s_er, 1)
            for b in range(B):
                done(nc.vector.tensor_scalar(pcond[0:KEYS, b, :], srow[0:KEYS, b, 1:S + 1], erow[:, b:b + 1], None, ALU.is_gt))
            settle()
            for b in range(B):
                nc.vector.scalar_tensor_tensor(pmask[0:KEYS, b, :], jrow[0:KEYS, :], erow[:, b:b + 1], pcond[0:KEYS, b, :],
                                               ALU.is_le, ALU.mult).then_inc(s_path, 1)
            for b in range(B):
                dve.wait_ge(s_xa, b + 1)
                xb = x_res[:, TPB * b:TPB * (b + 1), :].rearrange("p q h -> p (q h)")
                nc.vector.scalar_tensor_tensor(xb, ps[b][:], tgate[:, 0:1], xb, ALU.mult, ALU.add).then_inc(s_upd, 1)

            def route0():
                for t in range(TILES):
                    dve.wait_ge(s_score, 1 + t // (TILES // 2))
                    done(nc.vector.max(top8[:, t, :], aff[0][:, t, :]))
                settle()
                done(nc.vector.tensor_reduce(rsum[:, 0, :], top8, AX_X, ALU.add))
                for t in range(TILES):
                    done(nc.vector.match_replace(rest[0][:, t, :], top8[:, t, :], aff[0][:, t, :], 0.0))
                settle()
                done(nc.vector.tensor_scalar(rsum[:, 1, :], rsum[:, 0, :], 1e-9, None, ALU.add))
                settle()
                done(nc.vector.reciprocal(rsum[:, 2, :], rsum[:, 1, :]))
                done(nc.vector.tensor_tensor(rest[0], aff[0], rest[0], ALU.subtract))
                settle()
                for t in range(TILES):
                    nc.vector.tensor_scalar(wsel[0][:, t, :], rest[0][:, t, :], rsum[:, 2, t:t + 1], None,
                                            ALU.mult).then_inc(s_sel, 1)

            def route1():
                E = E1
                sc, ex = aff[1], rest[1]

                def by_tile(col):
                    return rsum[:, col, :].unsqueeze(2).broadcast_to([P, TILES, E])

                for h in range(2):
                    dve.wait_ge(s_score, 3 + h)
                done(nc.vector.tensor_reduce(rsum[:, 0, :], sc, AX_X, ALU.max))
                settle()
                nc.vector.tensor_tensor(ex, sc, by_tile(0), ALU.subtract).then_inc(s_rsub, 1)
                dve.wait_ge(s_rexp, 1)
                done(nc.vector.tensor_reduce(rsum[:, 1, :], ex, AX_X, ALU.add))
                settle()
                done(nc.vector.reciprocal(rsum[:, 2, :], rsum[:, 1, :]))
                settle()
                done(nc.vector.tensor_tensor(sc, ex, by_tile(2), ALU.mult))
                settle()
                for t in range(TILES):
                    done(nc.vector.max(top8[:, t, :], sc[:, t, :]))
                settle()
                for t in range(TILES):
                    done(nc.vector.max_index(topi[:, t, :], top8[:, t, :], sc[:, t, :]))
                done(nc.vector.tensor_tensor(rsum[:, 0, :], top8[:, :, 0], top8[:, :, 1], ALU.add))
                settle()
                done(nc.vector.tensor_scalar(rsum[:, 1, :], rsum[:, 0, :], 1e-20, None, ALU.add))
                done(nc.vector.tensor_copy(topf, topi))
                settle()
                done(nc.vector.reciprocal(rsum[:, 2, :], rsum[:, 1, :]))
                for c in range(2):
                    done(nc.vector.tensor_tensor(hit[c], iota_e[:].unsqueeze(1).broadcast_to([P, TILES, E]),
                                                 topf[:, :, c:c + 1].broadcast_to([P, TILES, E]), ALU.is_equal))
                settle()
                done(nc.vector.tensor_tensor(hit[0], hit[0], hit[1], ALU.add))
                done(nc.vector.tensor_tensor(ex, sc, by_tile(2), ALU.mult))
                settle()
                nc.vector.tensor_tensor(wsel[1], ex, hit[0], ALU.mult).then_inc(s_sel, TILES)

            def attention():
                for n in range(CHUNKS):
                    dve.wait_ge(s_qhi, n + 1)
                    tok = slice(512 * n, 512 * (n + 1))
                    nc.vector.scalar_tensor_tensor(qT_lo[:, tok], ps[3 + n % 2][:], bias2[:, 0:1], qT_hi[:, tok].bitcast(F32),
                                                   ALU.add, ALU.subtract).then_inc(s_qlo, 1)

                def shift_scores(i, j):
                    for r, (h0, h1) in enumerate(HSPLIT):
                        dve.wait_ge(s_sc, 3 * i + r + 1)
                        sc = ps[r][:, 0:(h1 - h0) * KEYS].rearrange("p (h k) -> p h k", k=KEYS)
                        nc.vector.tensor_reduce(smax[:, j, h0:h1], sc, AX_X, ALU.max).then_inc(s_mx, 1)
                    if not (isinstance(i, int) and i < 2):
                        dve.wait_ge(s_tr, HEADS // HT * (i - 1))
                    for r, (h0, h1) in enumerate(HSPLIT):
                        dve.wait_ge(s_mx, 3 * i + r + 1)
                        sc = ps[r][:, 0:(h1 - h0) * KEYS].rearrange("p (h k) -> p h k", k=KEYS)
                        to = expw[:, j, h0 * KEYS:h1 * KEYS].rearrange("p (h k) -> p h k", k=KEYS)
                        nc.vector.tensor_tensor(to, sc, smax[:, j, h0:h1].unsqueeze(2).broadcast_to([P, h1 - h0, KEYS]),
                                                ALU.subtract).then_inc(s_sub, 1)

                def normalise(i, j):
                    dve.wait_ge(s_av, i + 1)
                    o = ps[5][:, 0:HEADS * (HD + 1)].rearrange("p (h d) -> p h d", d=HD + 1)
                    nc.vector.reciprocal(rden[:, j, :], o[:, :, HD]).then_inc(s_rd, 1)
                    dve.wait_ge(s_rd, i + 1)
                    if not (isinstance(i, int) and i < 2):
                        dve.wait_ge(s_avt, i - 1)
                    nc.vector.tensor_tensor(av[:, j, :].rearrange("p (h d) -> p h d", d=HD), o[:, :, 0:HD],
                                            rden[:, j, :].unsqueeze(2).broadcast_to([P, HEADS, HD]), ALU.mult).then_inc(s_nrm, 1)

                def update(i):
                    dve.wait_ge(s_wo, i + 1)
                    xi = x_res[:, i, :] if isinstance(i, int) else x_res[:].rearrange("p t h -> p (t h)")[:, bass.ds(P * i, P)]
                    nc.vector.scalar_tensor_tensor(xi, ps[6][:, P:2 * P], tgate[:, 1:2], xi,
                                                   ALU.mult, ALU.add).then_inc(s_au, 1)

                def step(i, j):
                    first = isinstance(i, int)
                    shift_scores(i, j)
                    if not (first and i < 2):
                        update(i - 2)
                    if not (first and i < 1):
                        normalise(i - 1, 1 - j)

                for i in range(TPB):
                    step(i, i % 2)
                with dve.Fori(1, B) as t:
                    for q in range(TPB):
                        step(TPB * t + q, q % 2)
                update(TILES - 2)
                normalise(TILES - 1, 1)
                update(TILES - 1)

            def feed_forward(f):
                T, units = GROUPS[f] // 2, CHUNKS * GROUPS[f]

                def unit(g, k, j, load):
                    u = CHUNKS * g + k
                    i = k % 2
                    early = isinstance(g, int) and u < 2
                    dve.wait_ge(FF[f]["silu"], u + 1)
                    dve.wait_ge(FF[f]["up"], u + 1)
                    if not early:
                        dve.wait_ge(FF[f]["act"], u - 1)
                    nc.vector.tensor_tensor(act_t[:, i, :], act_s[:, i, :], ps[6 + i][:], ALU.mult).then_inc(FF[f]["t"], 1)
                    if k == 0:
                        dve.wait_ge(FF_MASK[f][j], 16 * MASK_DMAS * load)
                    dve.wait_ge(FF[f]["t"], u + 1)
                    if not early:
                        dve.wait_ge(FF[f]["alo"], u - 1)
                    nc.vector.tensor_tensor(act_a[:, i, :], act_t[:, i, :], mask[:, j, 512 * k:512 * (k + 1)],
                                            ALU.mult).then_inc(FF[f]["act"], 1)

                for k in range(CHUNKS):
                    unit(0, k, 0, 1)
                with dve.Fori(0, T) as t:
                    for jj in range(2):
                        for k in range(CHUNKS):
                            unit(2 * t + 1 + jj, k, 1 - jj, t + 1 + jj)
                for n in range(CHUNKS):
                    dve.wait_ge(FF[f]["back"], n + 1)
                    xb = x_res[:, TPB * n:TPB * (n + 1), :].rearrange("p q h -> p (q h)")
                    nc.vector.scalar_tensor_tensor(xb, ps[4 + n][:], tgate[:, 2 + f:3 + f], xb,
                                                   ALU.mult, ALU.add).then_inc(s_upd, 1)

            norm(1)
            route0()
            feed_forward(0)
            norm(2)
            attention()
            norm(3)
            route1()
            feed_forward(1)


INPUTS = ["x", "ctx_1024", "g_xattn", "g_ffn", "L0_ffn_router_w", "L0_ffn_shared_gate_w", "L0_ffn_shared_up_w",
          "L0_ffn_shared_down_w", "L0_ffn_expert_gate_k", "L0_ffn_expert_up_k", "L0_ffn_expert_down_k",
          "L1_xattn_Wq", "L1_xattn_bq", "L1_xattn_Wk", "L1_xattn_bk", "L1_xattn_Wv", "L1_xattn_bv",
          "L1_xattn_Wo", "L1_xattn_bo", "L1_ffn_gate_w", "L1_ffn_wg", "L1_ffn_wu", "L1_ffn_wd",
          "L1_ffn_swg", "L1_ffn_swu", "L1_ffn_swd"]


def kernel(**inputs):
    import numpy as _np
    import concourse.bacc as _bacc
    from concourse import mybir as _mybir
    from concourse.bass_utils import run_bass_kernel_spmd as _run

    nc = _bacc.Bacc("TRN2", target_bir_lowering=False, num_devices=1)
    arrays, args = {}, []
    for name in INPUTS:
        a = _np.ascontiguousarray(inputs[name])
        arrays[f"in_{name}"] = a
        args.append(nc.dram_tensor(f"in_{name}", a.shape, _mybir.dt.from_np(a.dtype), kind="ExternalInput").ap())
    shape = tuple(inputs["x"].shape)
    args.append(nc.dram_tensor("out", shape, _mybir.dt.float32, kind="ExternalOutput").ap())
    program(nc, *args)
    r = _run(nc, [arrays], core_ids=[0])
    return r.results[0]["out"]
```

```python
from contextlib import ExitStack

import concourse.bass as bass
import concourse.mybir as mybir
from concourse.alu_op_type import AluOpType as ALU

F32 = mybir.dt.float32
F32R = mybir.dt.float32r
F16 = mybir.dt.float16
U32 = mybir.dt.uint32
ACT = mybir.ActivationFunctionType
AX_X = mybir.AxisListType.X

P = 128
BIG = 1e30
TINY = 1e-30
LN_EPS = 1e-5


def program(nc, x, ctx_1024, g_xattn, g_ffn, r0_w, sg0, su0, sd0, eg0, eu0, ed0,
            Wq, bq, Wk, bk, Wv, bv, Wo, bo, r1_w, wg1, wu1, wd1, swg1, swu1, swd1, out):
    B, S, H = x.shape
    KEYS = ctx_1024.shape[1]
    TOK = B * S
    TILES = TOK // P
    TPB = S // P
    assert H == P and S == 512 and B == 4

    CH = 16
    CW = S // CH
    SLOTS = KEYS + CH - 1
    LANE = SLOTS * CW
    LANES = [32 * b for b in range(B)]

    E0, I0 = eg0.shape[0], eg0.shape[2]
    E1, I1 = wg1.shape[0], wg1.shape[1]
    K0 = 8
    assert P == 2 * I0
    EXPERTS = [E0, E1]
    CHUNKS = TOK // 512
    GROUPS = [1 + E0 // 2, -(-I1 * (E1 + 1) // P)]
    SPLIT_AT = 2
    UP, DOWN, WIDE = P, 2 * P, 3 * P
    assert GROUPS[0] % 2 == 1 and GROUPS[1] % 2 == 1

    HEADS, HD = 16, H // 16
    HPB = 6
    HSPLIT = [(0, HPB), (HPB, 2 * HPB), (2 * HPB, HEADS)]
    FLAT = HEADS * KEYS
    FT = -(-FLAT // P)
    HT = 4
    FIRST_HEAD = [P * c // KEYS for c in range(FT)]
    LAST_HEAD = [(min(P * (c + 1), FLAT) - 1) // KEYS for c in range(FT)]
    FH = max(b - a for a, b in zip(FIRST_HEAD, LAST_HEAD)) + 1
    RT = -(-FT // HT)
    EXP_BANKS = [3, 4, 7]
    assert RT == len(EXP_BANKS)

    def pieces(first, last):
        found = []
        while first < last:
            n = min(last, (first // I1 + 1) * I1) - first
            found.append((first // I1 - 1, first % I1, n))
            first += n
        return found

    ctx = ExitStack()
    with ctx:
        def sb(name, shape, dt=F32):
            return ctx.enter_context(nc.sbuf_tensor(name, shape, dt))

        def sem(name):
            return ctx.enter_context(nc.semaphore(name))

        ps = [ctx.enter_context(nc.psum_tensor(f"bank{i}", [P, 512], F32)) for i in range(8)]

        scr_d = nc.dram_tensor("scr_d", (B, CH, SLOTS, CW), F32).ap()
        scr_one = nc.dram_tensor("scr_one", (TOK,), F32).ap()
        scr_w1 = nc.dram_tensor("scr_w1", (GROUPS[1], P, WIDE), F32).ap()
        scr_mask = [nc.dram_tensor("scr_mask0", (E0, TOK), F32).ap(),
                    nc.dram_tensor("scr_mask1", (E1, TOK), F32).ap()]
        scr_lg = nc.dram_tensor("scr_lg", (B, CH, SLOTS, 2, CW), F16).ap()

        ND = TPB - 1

        x_res = sb("x_res", [P, TILES, H])
        xn = sb("xn", [P, TILES, H])
        xn_hi = sb("xn_hi", [P, TOK], F32R)
        xn_lo = sb("xn_lo", [P, TOK], F32R)
        stat = sb("stat", [P, TILES, 6])
        mv = sb("mv", [P, TILES, 2])
        veps = sb("veps", [P, TILES])
        std = sb("std", [P, TILES])
        rstd = sb("rstd", [P, 4, TILES])
        ident = sb("ident", [P, P])
        ones = sb("ones", [P, P])
        gates = sb("gates", [P, 4])
        tgate = sb("tgate", [P, 4])
        ctx_sb = sb("ctx_sb", [KEYS, B, H])
        ctxT = sb("ctxT", [P, B, KEYS])
        ctxT_hi = sb("ctxT_hi", [P, B, KEYS], F32R)
        ctxT_lo = sb("ctxT_lo", [P, B, KEYS], F32R)
        zeros = sb("zeros", [1, 512], F32R)
        iota_e = sb("iota_e", [P, E1])
        jrow = sb("jrow", [P, S], F16)
        ecol = sb("ecol", [P, KEYS])
        erow = sb("erow", [KEYS, B])
        junk = sb("junk", [P, S], F16)
        aa = sb("aa", [KEYS, B])
        aasq = sb("aasq", [KEYS, B, H])

        w_raw = sb("w_raw", [P, 2, WIDE])
        w_hi = sb("w_hi", [P, 2, WIDE], F32R)
        w_lo = sb("w_lo", [P, 2, WIDE], F32R)
        prep_in = sb("prep_in", [P, 2, WIDE])
        prep_out = sb("prep_out", [P, 2, WIDE])
        router = [sb("router0", [P, E0]), sb("router1", [P, E1])]
        router_hi = [sb("router0_hi", [P, E0], F32R), sb("router1_hi", [P, E1], F32R)]
        router_lo = [sb("router0_lo", [P, E0], F32R), sb("router1_lo", [P, E1], F32R)]
        act_hi = sb("act_hi", [P, 2, 512], F32R)
        act_lo = sb("act_lo", [P, 2, 512], F32R)
        kT = sb("kT", [P, B * KEYS])
        kT_hi = sb("kT_hi", [P, B * KEYS], F32R)
        kT_lo = sb("kT_lo", [P, B * KEYS], F32R)
        v_ext = sb("v_ext", [KEYS, B, HEADS, HD + 1])
        v_flat = sb("v_flat", [P, B, FT, FH * (HD + 1)])
        kbd_hi = sb("kbd_hi", [P, B, HEADS, KEYS], F32R)
        kbd_lo = sb("kbd_lo", [P, B, HEADS, KEYS], F32R)
        qs_hi = sb("qs_hi", [P, 2, P], F32R)
        qs_lo = sb("qs_lo", [P, 2, P], F32R)
        router1_rows = sb("router1_rows", [E1, P])
        w4 = sb("w4", [P, 4, P])
        wq_hi = sb("wq_hi", [P, P], F32R)
        wq_lo = sb("wq_lo", [P, P], F32R)
        bias2 = sb("bias2", [P, 2])
        brow2 = sb("brow2", [1, 2, P])
        headmask = sb("headmask", [P, HEADS])

        ARENA = 20600
        arena = sb("arena", [P, ARENA])
        mark = [0]

        def view(shape, dt=F32):
            n = 1
            for k in shape:
                n *= k
            cols = n // 2 if dt == F16 else n
            v = arena[:, mark[0]:mark[0] + cols]
            mark[0] += cols
            assert mark[0] <= ARENA
            if dt != F32:
                v = v.bitcast(dt)
            if len(shape) == 2:
                v = v.rearrange("p (a b) -> p a b", a=shape[0])
            if len(shape) == 3:
                v = v.rearrange("p (a b c) -> p a b c", a=shape[0], b=shape[1])
            return v

        sq = view([2, S])
        dsum = view([B, S])
        d2 = view([B, S])
        droot = view([B, S])
        droot2 = view([B, S])
        drows = view([B, S])
        dl = view([SLOTS, CW])
        rst = view([SLOTS + 1, CW + 1])
        MST = 8
        mst = view([MST, CW])
        lg = view([SLOTS, 2, CW], F16)
        mark[0] = 0
        lgr = view([2, B, S], F16)
        nlj = view([B, S], F16)
        nup = view([B, S], F16)
        ubig = view([B, S], F16)
        srow = view([B, S + 8], F16)
        trow = view([B, S], F16)
        pcond = view([B, S], F16)
        mark[0] = 0
        pmask = view([B, S])
        CHASE = slice(96, 96 + B)
        mark[0] = 0
        chase = view([KEYS, S], F16)[CHASE]
        mark[0] = 0
        mask = view([2, TOK])
        act_s = view([2, 512])
        act_t = view([2, 512])
        act_a = view([2, 512])
        yT = view([CHUNKS, 512])
        affT = view([1, TOK])[:, 0]
        aff = [view([TILES, E]) for E in EXPERTS]
        rest = [view([TILES, E]) for E in EXPERTS]
        wsel = [view([TILES, -(-E // 32) * 32]) for E in EXPERTS]
        wT = [view([TILES, -(-E // 32) * 32]) for E in EXPERTS]
        top8 = view([TILES, 8])
        topi = view([TILES, 8], U32)
        topf = view([TILES, 8])
        hit = [view([TILES, E1]) for c in range(2)]
        rsum = view([4, TILES])

        mark[0] = 0
        qT_hi = view([TOK], F32R)
        qT_lo = view([TOK], F32R)
        expw = view([2, FT * P])
        smax = view([2, HEADS])
        expT = view([FT, P])
        rden = view([2, HEADS])
        av = view([2, H])
        avT = view([P])

        s_aw = sem("attn_weights_loaded")
        s_kp = sem("k_projected")
        s_vp = sem("v_projected")
        s_khi = sem("kT_hi_ready")
        s_klo = sem("kT_lo_ready")
        s_vx = sem("v_ready")
        s_vf = sem("v_flat_loaded")
        s_epad = sem("exp_padded")
        s_kbd = sem("kbd_ready")
        s_wql = sem("wq_lo_ready")
        s_wqh = sem("wq_hi_ready")
        s_qp = sem("q_projected")
        s_qhi = sem("qT_hi_ready")
        s_qlo = sem("qT_lo_ready")
        s_qs = sem("q_tile_ready")
        s_sc = sem("scores")
        s_mx = sem("scores_max")
        s_sub = sem("scores_shifted")
        s_exp = sem("exp_ready")
        s_tr = sem("exp_transposed")
        s_ev = sem("exp_copied")
        s_av = sem("av_products")
        s_rd = sem("av_reciprocal")
        s_nrm = sem("av_normalised")
        s_avt = sem("av_transposed")
        s_avc = sem("av_copied")
        s_wo = sem("out_projected")
        s_st = sem("tile_stats")
        s_au = sem("x_updated_attn")
        s_one = sem("ones_stored")
        s_rw = [sem("router0_loaded"), sem("router1_loaded")]
        s_rt = sem("router1_transposed")
        s_rhi = sem("router_hi_ready")
        s_rlo = sem("router_lo_ready")
        s_logit = sem("router_logits")
        s_score = sem("router_scores")
        s_rsub = sem("router_shifted")
        s_rexp = sem("router_exp")
        s_aff = sem("router_scores_by_expert")
        s_affT = sem("router_scores_transposed")
        s_pad = sem("router_padded")
        s_wt = sem("router_weights_ready")
        s_mst = sem("mask_stored")
        s_pin = [sem(f"prep_loaded{j}") for j in range(2)]
        s_pzero = sem("prep_zeroed")
        s_pt = sem("prep_transposed")
        s_pout = sem("prep_copied")
        s_pst = [sem(f"prep_stored{j}") for j in range(2)]
        FF = [dict((n, sem(f"ff{f}_{n}")) for n in (
            "whi", "wlo", "gate", "up", "silu", "t", "act", "ahi", "alo", "down", "sum", "yT", "back")) for f in range(2)]
        FF_RAW = [[sem(f"ff{f}_raw_loaded{j}") for j in range(2)] for f in range(2)]
        FF_MASK = [[sem(f"ff{f}_mask_loaded{j}") for j in range(2)] for f in range(2)]
        RAW_DMAS, MASK_DMAS = [3, 1], 2
        s_x = [sem(f"x_loaded{b}") for b in range(B)]
        s_ctx = sem("ctx_loaded")
        s_gate = sem("gates_loaded")
        s_zero = sem("scratch_zeroed")
        s_pool = sem("pool_step")
        s_dve = sem("dve_step")
        s_act = sem("act_step")
        s_bn = sem("ln_var_ready")
        s_std = sem("ln_std_ready")
        s_rstd = sem("ln_rstd_ready")
        s_xn = sem("xn_ready_dve")
        s_xnp = sem("xn_ready_pool")
        s_xt = sem("xn_transposed")
        s_xhi = sem("xn_hi_ready")
        s_xlo = sem("xn_lo_ready")
        s_ct = sem("ctx_transposed")
        s_cthi = sem("ctxT_hi_ready")
        s_ctlo = sem("ctxT_lo_ready")
        s_ab = sem("dist_products")
        s_dsum = sem("dist_sum")
        s_d2 = sem("dist_squared")
        s_root = sem("dist_root")
        s_dist = sem("dist_ready")
        s_dst = [sem(f"dist_stored{b}") for b in range(B)]
        s_dld = [sem(f"dist_lanes{b}") for b in range(B)]
        s_halo = sem("wave_halo")
        s_scan = sem("wave_row")
        s_steps = sem("wave_steps")
        s_lgst = [sem(f"steps_stored{b}") for b in range(B)]
        s_lgld = [sem(f"steps_rows{b}") for b in range(B)]
        s_trow = sem("t_rows_ready")
        s_tch = [sem(f"chase_rows{b}") for b in range(B)]
        s_chase = sem("chase_step")
        s_et = sem("entries_transposed")
        s_er = sem("entries_by_row")
        s_path = sem("path_ready")
        s_xa = sem("aligned_sum")
        s_upd = sem("x_updated")
        s_out = sem("out_stored")

        x_t = x.rearrange("b (q p) h -> b p q h", p=P)
        out_t = out.rearrange("b (q p) h -> b p q h", p=P)

        def at(t, offset, ap):
            return bass.AP(tensor=t.tensor, offset=t.offset + offset, ap=ap)

        def sl(b):
            return slice(S * b, S * (b + 1))

        block = ctx.enter_context(nc.Block())
        POOL_CONST = 12 + B

        @block.sync
        def _(sp):
            for b in range(B):
                sp.dma_start(x_res[:, TPB * b:TPB * (b + 1), :], x_t[b]).then_inc(s_x[b], 16)
                if b == 0:
                    sp.dma_start(ctx_sb[:], ctx_1024.rearrange("b k d -> k b d")).then_inc(s_ctx, 16)
            sp.dma_start(gates[:, 0:2], g_xattn.partition_broadcast(P)).then_inc(s_gate, 16)
            sp.dma_start(gates[:, 2:4], g_ffn.partition_broadcast(P)).then_inc(s_gate, 16)
            sp.dma_start(router[0][:], r0_w).then_inc(s_rw[0], 16)
            for m, w in enumerate((Wq, Wk, Wv, Wo)):
                sp.dma_start(w4[:, m, :], w).then_inc(s_aw, 16)
            for m, v in enumerate((bq, bk)):
                sp.dma_start(bias2[:, m:m + 1], v.rearrange("(p o) -> p o", o=1)).then_inc(s_aw, 16)
            for m, v in enumerate((bv, bo)):
                sp.dma_start(brow2[:, m, :], v.rearrange("(o p) -> o p", o=1)).then_inc(s_aw, 16)
            sp.dma_start(router1_rows[:], r1_w).then_inc(s_rw[1], 16)
            sp.wait_ge(s_pool, 2)
            sp.dma_start(scr_one.rearrange("(p c) -> p c", c=P), ones[0:TOK // P, :]).then_inc(s_one, 16)
            sp.dma_start(w_raw[:, 0, 0:I0], sg0).then_inc(FF_RAW[0][0], 16)
            sp.dma_start(w_raw[:, 0, UP:UP + I0], su0).then_inc(FF_RAW[0][0], 16)
            sp.dma_start(w_raw[0:I0, 0, DOWN:DOWN + P], sd0).then_inc(FF_RAW[0][0], 16)
            sp.wait_ge(s_pool, POOL_CONST)
            sp.dma_start(scr_d.rearrange("b c s w -> (b c) (s w)"),
                         dl[0:B * CH].rearrange("p s w -> p (s w)")).then_inc(s_zero, 16)
            sp.wait_ge(s_zero, 16)
            for b in range(B):
                sp.wait_ge(s_dist, b + 1)
                sp.dma_start(at(scr_d[b], 0, [[CW, KEYS], [LANE + CW, CH], [1, CW]]),
                             drows[0:KEYS, b, :].rearrange("i (c w) -> i c w", w=CW)).then_inc(s_dst[b], 16)
            for b in range(B):
                sp.wait_ge(s_dst[b], 16)
                sp.dma_start(dl[LANES[b]:LANES[b] + CH].rearrange("c s w -> c (s w)"),
                             scr_d[b].rearrange("c s w -> c (s w)")).then_inc(s_dld[b], 16)
            sp.wait_ge(s_vx, 1)
            for h in range(HEADS):
                for c in range(FT):
                    r0, r1 = max(KEYS * h, P * c), min(KEYS * (h + 1), P * (c + 1))
                    if r0 < r1:
                        col = (HD + 1) * (h - FIRST_HEAD[c])
                        sp.dma_start(v_flat[r0 - P * c:r1 - P * c, :, c, col:col + HD + 1],
                                     v_ext[r0 - KEYS * h:r1 - KEYS * h, :, h, :]).then_inc(s_vf, 16)
            sp.wait_ge(s_steps, SLOTS)
            for b in range(B):
                sp.dma_start(scr_lg[b].rearrange("c s a w -> c (s a w)"),
                             lg[LANES[b]:LANES[b] + CH].rearrange("c s a w -> c (s a w)")).then_inc(s_lgst[b], 16)
            for b in range(B):
                sp.wait_ge(s_lgst[b], 16)
                for a in range(2):
                    sp.dma_start(lgr[0:KEYS, a, b, :].rearrange("i (c w) -> i c w", w=CW),
                                 at(scr_lg[b], a * CW, [[2 * CW, KEYS], [2 * (LANE + CW), CH], [1, CW]])
                                 ).then_inc(s_lgld[b], 16)
            for b in range(B):
                sp.wait_ge(s_trow, b + 1)
                sp.dma_start(chase[b:b + 1], trow[0:KEYS, b, :]).then_inc(s_tch[b], 16)

            def raw0(g, j):
                e = bass.ds(2 * g - 2, 2)
                dst = w_raw[:, j, 0:DOWN].rearrange("p (m e i) -> p m e i", m=2, e=2)
                sp.dma_start(dst[:, 0], eg0[e].rearrange("e h i -> h e i")).then_inc(FF_RAW[0][j], 16)
                sp.dma_start(dst[:, 1], eu0[e].rearrange("e h i -> h e i")).then_inc(FF_RAW[0][j], 16)
                sp.dma_start(w_raw[:, j, DOWN:DOWN + P],
                             ed0[e].rearrange("e i h -> (e i) h")).then_inc(FF_RAW[0][j], 16)

            def mask0(g, j):
                for k in range(2):
                    row = scr_mask[0][bass.ds(2 * g - 2 + k, 1), :].rearrange("a t -> (a t)")
                    sp.dma_start(mask[I0 * k:I0 * (k + 1), j, :], row.partition_broadcast(I0)).then_inc(FF_MASK[0][j], 16)

            def raw1(g, j):
                sp.dma_start(w_raw[:, j, :], scr_w1[g]).then_inc(FF_RAW[1][j], 16)

            def mask1(g, j):
                parts = pieces(P * g, min(P * (g + 1), I1 * (E1 + 1)))
                if len(parts) == 1:
                    e, i, n = parts[0]
                    parts = [(e, i, I0), (e, i, P - I0)]
                at_row = 0
                for e, i, n in parts:
                    row = scr_one if e < 0 else scr_mask[1][e]
                    sp.dma_start(mask[at_row:at_row + n, j, :], row.partition_broadcast(n)).then_inc(FF_MASK[1][j], 16)
                    at_row += n

            def stored_masks(f, b0, b1):
                E = EXPERTS[f]
                for q in range(P // 32):
                    n, tiles = min(E, 32), slice(TPB * b0, TPB * b1)
                    for blk in range(-(-E // 32)):
                        src = wT[f][32 * q:32 * q + n, tiles, 32 * blk:32 * (blk + 1)]
                        dst = at(scr_mask[f], 32 * blk * TOK + P * TPB * b0 + 32 * q, [[TOK, n], [P, TPB * (b1 - b0)], [1, 32]])
                        sp.dma_start(dst, src).then_inc(s_mst, 16)

            sp.wait_ge(s_one, 16)
            raw0(1, 1)
            sp.wait_ge(s_upd, B)
            for k in range(2):
                sp.dma_start(mask[I0 * k:I0 * (k + 1), 0, :], scr_one.partition_broadcast(I0)).then_inc(FF_MASK[0][0], 16)
            for b in range(B):
                sp.wait_ge(s_wt, b + 1)
                stored_masks(0, b, b + 1)
            sp.wait_ge(s_mst, 16 * 8 * B)
            mask0(1, 1)
            with sp.Fori(0, GROUPS[0] // 2 - 1) as t:
                for j in range(2):
                    g = 2 * t + 2 + j
                    sp.wait_ge(FF[0]["wlo"], g - 1)
                    raw0(g, j)
                    sp.wait_ge(FF[0]["act"], CHUNKS * (g - 1))
                    mask0(g, j)
            g = GROUPS[0] - 1
            sp.wait_ge(FF[0]["wlo"], g - 1)
            raw0(g, 0)
            sp.wait_ge(FF[0]["act"], CHUNKS * (g - 1))
            mask0(g, 0)
            for j in range(2):
                sp.wait_ge(s_pst[j], 16 * ((GROUPS[1] + 1 - j) // 2))
            sp.wait_ge(FF[0]["wlo"], GROUPS[0])
            raw1(0, 0)
            raw1(1, 1)
            sp.wait_ge(s_au, TILES)
            mask1(0, 0)
            mask1(1, 1)
            sp.wait_ge(s_wt, B + 1)
            stored_masks(1, 0, B)
            sp.wait_ge(s_mst, 16 * (8 * B + 4))
            for g in range(2, GROUPS[1]):
                j = g % 2
                sp.wait_ge(FF[1]["wlo"], g - 1)
                raw1(g, j)
                sp.wait_ge(FF[1]["act"], CHUNKS * (g - 1))
                mask1(g, j)
            sp.wait_ge(s_upd, 3 * B)
            sp.wait_ge(s_au, TILES)
            for b in range(B):
                sp.dma_start(out_t[b], x_res[:, TPB * b:TPB * (b + 1), :]).then_inc(s_out, 16)
            sp.wait_ge(s_out, 16 * B)

        @block.gpsimd
        def _(pool):
            nc.gpsimd.memset(w_raw[:, 0, :], 0.0).then_inc(s_pool, 1)
            nc.gpsimd.memset(ones[:], 1.0).then_inc(s_pool, 1)
            pool.wait_ge(s_pool, 2)
            nc.gpsimd.affine_select(out=ident[:], in_=ones[:], compare_op=ALU.is_equal, fill=0.0, base=0,
                                    pattern=[[-1, P]], channel_multiplier=1).then_inc(s_pool, 1)
            nc.gpsimd.iota(iota_e[:], pattern=[[1, E1]], base=0, channel_multiplier=0,
                           allow_small_or_imprecise_dtypes=True).then_inc(s_pool, 1)
            nc.gpsimd.memset(v_ext[:], 1.0).then_inc(s_pool, 1)
            nc.gpsimd.memset(v_flat[:], 0.0).then_inc(s_pool, 1)
            nc.gpsimd.affine_select(out=headmask[:], in_=ones[:, 0:HEADS], compare_op=ALU.is_ge, fill=0.0, base=0,
                                    pattern=[[-HD, HEADS]], channel_multiplier=1).then_inc(s_pool, 1)
            pool.wait_ge(s_pool, 7)
            nc.gpsimd.affine_select(out=headmask[:], in_=headmask[:], compare_op=ALU.is_ge, fill=0.0, base=HD - 1,
                                    pattern=[[HD, HEADS]], channel_multiplier=-1).then_inc(s_pool, 1)
            nc.gpsimd.memset(dl, 0.0).then_inc(s_pool, 1)
            nc.gpsimd.iota(jrow[:], pattern=[[1, S]], base=0, channel_multiplier=0,
                           allow_small_or_imprecise_dtypes=True).then_inc(s_pool, 1)
            nc.gpsimd.memset(rst[:, 0, :], BIG).then_inc(s_pool, 1)
            nc.gpsimd.memset(ecol[:], S - 1.0).then_inc(s_pool, 1)
            pool.wait_ge(s_pool, 12)
            for b in range(B):
                nc.gpsimd.memset(rst[LANES[b]:LANES[b] + 1, 0, 0:1], 0.0).then_inc(s_pool, 1)

            pool.wait_ge(s_pool, POOL_CONST)
            def attention_prep():
                pool.wait_ge(s_khi, 1)
                nc.gpsimd.tensor_tensor(wq_lo[:], w4[:, 0, :], wq_hi[:].bitcast(F32), ALU.subtract).then_inc(s_wql, 1)
                nc.gpsimd.tensor_tensor(kT_lo[:], kT[:], kT_hi[:].bitcast(F32), ALU.subtract).then_inc(s_klo, 1)

            def normalise(k):
                for b in range(B):
                    pool.wait_ge(s_rstd, B * k + (b if k < 3 else 0) + 1)
                    for t in range(TPB * b + ND, TPB * (b + 1)):
                        nc.gpsimd.tensor_scalar(xn[:, t, :], x_res[:, t, :], mv[:, t, 0:1], rstd[:, 3, t:t + 1],
                                                ALU.subtract, ALU.mult).then_inc(s_xnp, 1)

            normalise(0)
            loads = [0, 0]

            def prep_store(g):
                pool.wait_ge(s_pout, g + 1)
                pool.dma_start(scr_w1[g], prep_out[:, g % 2, :]).then_inc(s_pst[g % 2], 16)

            for g in range(GROUPS[1]):
                j = g % 2
                if g >= 2:
                    pool.wait_ge(s_pt, g - 1)
                if P * (g + 1) > I1 * (E1 + 1):
                    nc.gpsimd.memset(prep_in[:, j, :], 0.0).then_inc(s_pzero, 1)
                    pool.wait_ge(s_pzero, 1)
                at_row = 0
                for e, i, n in pieces(P * g, min(P * (g + 1), I1 * (E1 + 1))):
                    wg, wu, wd = (swg1, swu1, swd1) if e < 0 else (wg1[e], wu1[e], wd1[e])
                    rows = slice(at_row, at_row + n)
                    pool.dma_start(prep_in[rows, j, 0:P], wg[i:i + n, :]).then_inc(s_pin[j], 16)
                    pool.dma_start(prep_in[rows, j, UP:UP + P], wu[i:i + n, :]).then_inc(s_pin[j], 16)
                    pool.dma_start(prep_in[:, j, DOWN + at_row:DOWN + at_row + n], wd[:, i:i + n]).then_inc(s_pin[j], 16)
                    at_row += n
                if g == 1:
                    attention_prep()
                if g >= 1:
                    prep_store(g - 1)
            prep_store(GROUPS[1] - 1)

            def attention():
                pool.wait_ge(s_xlo, 2 * B + 1)
                nc.gpsimd.memset(expw[:, :, FLAT:], 0.0).then_inc(s_epad, 1)

                def tile(i, j):
                    if isinstance(i, int):
                        tok = slice(P * i, P * (i + 1))
                        pool.wait_ge(s_qlo, min(i // TPB + 1, CHUNKS))
                        if i >= 2:
                            pool.wait_ge(s_sc, 3 * (i - 1))
                    else:
                        tok = bass.ds(P * i, P)
                        pool.wait_ge(s_sc, 3 * i - 3)
                    nc.gpsimd.tensor_copy(qs_hi[:, j, :], qT_hi[:, tok].bitcast(F32))
                    nc.gpsimd.tensor_copy(qs_lo[:, j, :], qT_lo[:, tok].bitcast(F32)).then_inc(s_qs, 1)

                for i in range(TPB):
                    tile(i, i % 2)
                pool.wait_ge(s_qlo, CHUNKS)
                with pool.Fori(1, B) as t:
                    for q in range(TPB):
                        tile(TPB * t + q, q % 2)

            def feed_forward(f):
                T = GROUPS[f] // 2
                def unit(g, k):
                    u = CHUNKS * g + k
                    pool.wait_ge(FF[f]["ahi"], u + 1)
                    if not (isinstance(g, int) and u < 2):
                        pool.wait_ge(FF[f]["down"], u - 1)
                    nc.gpsimd.tensor_tensor(act_lo[:, k % 2, :], act_a[:, k % 2, :], act_hi[:, k % 2, :].bitcast(F32),
                                            ALU.subtract).then_inc(FF[f]["alo"], 1)

                for k in range(CHUNKS):
                    unit(0, k)
                with pool.Fori(0, T) as t:
                    for jj in range(2):
                        for k in range(CHUNKS):
                            unit(2 * t + 1 + jj, k)

            normalise(1)
            feed_forward(0)
            normalise(2)
            attention()
            normalise(3)
            feed_forward(1)

        @block.scalar
        def _(act):
            act.wait_ge(s_gate, 32)
            nc.scalar.activation(tgate[:], gates[:], ACT.Tanh)
            act.wait_ge(s_ct, 1)
            nc.scalar.activation(ctxT[:], ps[6][:, 0:B * KEYS].rearrange("p (b k) -> p b k", b=B), ACT.Copy)
            nc.scalar.activation(ctxT_hi[:], ps[6][:, 0:B * KEYS].rearrange("p (b k) -> p b k", b=B),
                                 ACT.Copy).then_inc(s_cthi, 1)

            def root(k, b):
                act.wait_ge(s_bn, B * k + b + 1)
                tiles = slice(TPB * b, TPB * (b + 1)) if k < 3 else slice(0, TILES)
                nc.scalar.activation(std[:, tiles], veps[:, tiles], ACT.Sqrt).then_inc(s_std, 1)

            def high(k, b):
                act.wait_ge(s_xt, B * k + b + 1)
                bank = ps[b % 2]
                if k == 0:
                    nc.scalar.activation(xn_hi[:, sl(b)], bank[:], ACT.Copy)
                    if b >= 2:
                        act.wait_ge(s_ab, 2 * b - 2)
                    nc.scalar.activation(sq[:, b % 2, :], bank[:], ACT.Square).then_inc(s_xhi, 1)
                else:
                    nc.scalar.activation(xn_hi[:, sl(b)], bank[:], ACT.Copy).then_inc(s_xhi, 1)

            def query(n):
                act.wait_ge(s_qp, n + 1)
                nc.scalar.activation(qT_hi[:, 512 * n:512 * (n + 1)], ps[2 + n % 2][:], ACT.Identity,
                                     bias=bias2[:, 0:1]).then_inc(s_qhi, 1)

            def norm(k):
                for b in range(B):
                    if k < 3 or b == 0:
                        root(k, b)
                    if b >= 1:
                        high(k, b - 1)
                    if k == 2 and b >= 2:
                        query(b - 2)
                if k in (0, 2):
                    high(k, B - 1)
                if k == 2:
                    query(B - 2)
                    query(B - 1)

            norm(0)
            for b in range(B):
                act.wait_ge(s_d2, b + 1)
                nc.scalar.activation(droot[0:KEYS, b, :], d2[0:KEYS, b, :], ACT.Sqrt).then_inc(s_act, 1)
                act.wait_ge(s_act, b + 1)
                nc.scalar.activation(droot2[0:KEYS, b, :], droot[0:KEYS, b, :], ACT.Square).then_inc(s_root, 1)
            act.wait_ge(s_aw, 16 * 8)
            nc.scalar.activation(wq_hi[:], w4[:, 0, :], ACT.Copy)
            act.wait_ge(s_kp, 1)
            nc.scalar.activation(kT[:], ps[4][:, 0:B * KEYS], ACT.Identity, bias=bias2[:, 1:2])
            nc.scalar.activation(kT_hi[:], ps[4][:, 0:B * KEYS], ACT.Identity, bias=bias2[:, 1:2]).then_inc(s_khi, 1)
            act.wait_ge(s_vp, 1)
            act.wait_ge(s_pool, POOL_CONST)
            nc.scalar.activation(v_ext[:, :, :, 0:HD], ps[5][0:KEYS, :].rearrange("p (b h d) -> p b h d", b=B, d=HD),
                                 ACT.Copy).then_inc(s_vx, 1)
            act.wait_ge(s_khi, 1)
            for g in range(GROUPS[1]):
                act.wait_ge(s_pt, g + 1)
                if g >= 2:
                    act.wait_ge(s_pst[g % 2], 16 * (g // 2))
                nc.scalar.activation(prep_out[:, g % 2, :], ps[7][:, 0:WIDE], ACT.Copy).then_inc(s_pout, 1)
                if 2 <= g < 2 + HEADS:
                    h = g - 2
                    if h == 0:
                        act.wait_ge(s_klo, 1)
                    for k_all, k_head in ((kT_hi, kbd_hi), (kT_lo, kbd_lo)):
                        ins = nc.scalar.activation(k_head[:, :, h, :], k_all[:].bitcast(F32).rearrange("p (b k) -> p b k", b=B),
                                                   ACT.Copy, scale=headmask[:, h:h + 1])
                    ins.then_inc(s_kbd, 1)
            act.wait_ge(s_rw[0], 16)
            nc.scalar.activation(router_hi[0][:], router[0][:], ACT.Copy).then_inc(s_rhi, 1)
            act.wait_ge(s_rt, 1)
            nc.scalar.activation(router[1][:], ps[6][:, 0:E1], ACT.Copy)
            nc.scalar.activation(router_hi[1][:], ps[6][:, 0:E1], ACT.Copy).then_inc(s_rhi, 1)
            act.wait_ge(s_et, 1)
            nc.scalar.activation(erow[:], ps[6][0:KEYS, CHASE], ACT.Copy).then_inc(s_er, 1)

            def route(f):
                def scores(b):
                    act.wait_ge(s_logit, B * f + b + 1)
                    nc.scalar.activation(affT[0:EXPERTS[f], sl(b)], ps[2 + b % 2][0:EXPERTS[f], :],
                                         ACT.Sigmoid if f == 0 else ACT.Copy).then_inc(s_aff, 1)

                def by_token(b):
                    act.wait_ge(s_affT, B * f + b + 1)
                    tiles = slice(TPB * b, TPB * (b + 1))
                    nc.scalar.activation(aff[f][:, tiles, :], ps[7][:, 0:TPB * EXPERTS[f]].rearrange("p (t e) -> p t e", t=TPB),
                                         ACT.Copy).then_inc(s_score, 1)

                scores(0)
                high(2 * f + 1, B - 1)
                for b in range(1, B):
                    scores(b)
                    by_token(b - 1)
                by_token(B - 1)
                if f == 1:
                    act.wait_ge(s_rsub, 1)
                    nc.scalar.activation(rest[1], rest[1], ACT.Exp).then_inc(s_rexp, 1)

            def feed_forward(f):
                T, units = GROUPS[f] // 2, CHUNKS * GROUPS[f]

                def hi(u, j):
                    act.wait_ge(FF[f]["act"], u + 1)
                    if not (isinstance(u, int) and u < 2):
                        act.wait_ge(FF[f]["alo"], u - 1)
                        act.wait_ge(FF[f]["down"], u - 1)
                    nc.scalar.activation(act_hi[:, j, :], act_a[:, j, :], ACT.Copy).then_inc(FF[f]["ahi"], 1)

                def unit(g, k, j, load=None):
                    u = CHUNKS * g + k
                    if k == SPLIT_AT and load is not None:
                        act.wait_ge(FF[f]["down"], CHUNKS * g)
                        act.wait_ge(FF_RAW[f][1 - j], 16 * RAW_DMAS[f] * load)
                        nc.scalar.activation(w_hi[:, 1 - j, :], w_raw[:, 1 - j, :], ACT.Copy).then_inc(FF[f]["whi"], 1)
                    act.wait_ge(FF[f]["gate"], u + 1)
                    if not (isinstance(g, int) and u < 2):
                        act.wait_ge(FF[f]["t"], u - 1)
                    nc.scalar.activation(act_s[:, k % 2, :], ps[4 + k % 2][:], ACT.Silu).then_inc(FF[f]["silu"], 1)
                    if not (isinstance(g, int) and u < 1):
                        hi(u - 1, (k + 1) % 2)

                for k in range(CHUNKS):
                    unit(0, k, 0)
                with act.Fori(0, T - 1) as t:
                    for jj in range(2):
                        for k in range(CHUNKS):
                            unit(2 * t + 1 + jj, k, 1 - jj, t + 2)
                for jj in range(2):
                    for k in range(CHUNKS):
                        unit(2 * T - 1 + jj, k, 1 - jj, T + 1 if jj == 0 else None)
                hi(units - 1, 1)
                for n in range(CHUNKS):
                    act.wait_ge(FF[f]["sum"], n + 1)
                    nc.scalar.activation(yT[:, n, :], ps[n][:], ACT.Copy).then_inc(FF[f]["yT"], 1)

            def split_first(f):
                for g in range(2):
                    act.wait_ge(FF_RAW[f][g], 16 * RAW_DMAS[f])
                    nc.scalar.activation(w_hi[:, g, :], w_raw[:, g, :], ACT.Copy).then_inc(FF[f]["whi"], 1)

            def attention():
                def copy_av(i):
                    act.wait_ge(s_avt, i + 1)
                    nc.scalar.activation(avT, ps[6][:, 0:P], ACT.Copy).then_inc(s_avc, 1)

                def copy_exp(i):
                    if not (isinstance(i, int) and i == 0):
                        act.wait_ge(s_av, i)
                    for r in range(RT):
                        act.wait_ge(s_tr, RT * i + r + 1)
                        n = min(HT, FT - HT * r)
                        nc.scalar.activation(expT[:, HT * r:HT * r + n, :].rearrange("p c t -> p (c t)"),
                                             ps[EXP_BANKS[r]][:, 0:P * n], ACT.Copy).then_inc(s_ev, 1)

                def exp(i, j):
                    act.wait_ge(s_sub, 3 * i + 3)
                    nc.scalar.activation(expw[:, j, 0:FLAT], expw[:, j, 0:FLAT], ACT.Exp, scale=float(HD) ** -0.5).then_inc(s_exp, 1)

                def step(i, j):
                    first = isinstance(i, int)
                    if not (first and i < 2):
                        copy_av(i - 2)
                    if not (first and i < 1):
                        copy_exp(i - 1)
                    exp(i, j)

                for i in range(TPB):
                    step(i, i % 2)
                with act.Fori(1, B) as t:
                    for q in range(TPB):
                        step(TPB * t + q, q % 2)
                copy_av(TILES - 2)
                copy_exp(TILES - 1)
                copy_av(TILES - 1)

            split_first(0)
            norm(1)
            route(0)
            feed_forward(0)
            norm(2)
            split_first(1)
            attention()
            norm(3)
            route(1)
            feed_forward(1)

        @block.tensor
        def _(pe):
            pe.wait_ge(s_ctx, 16)
            pe.wait_ge(s_pool, 3)
            for b in range(B):
                mm = nc.tensor.transpose(ps[6][:, KEYS * b:KEYS * (b + 1)], ctx_sb[:, b, :], ident[0:KEYS, 0:KEYS])
            mm.then_inc(s_ct, 1)

            def turn(k, b):
                if b >= 2:
                    pe.wait_ge(s_xlo, B * k + b - 1)
                for q in range(TPB):
                    t = TPB * b + q
                    if q < ND:
                        pe.wait_ge(s_xn, (B * k + b) * ND + q + 1)
                    else:
                        pe.wait_ge(s_xnp, (B * k + b) * (TPB - ND) + q - ND + 1)
                    mm = nc.tensor.transpose(ps[b % 2][:, P * q:P * (q + 1)], xn[:, t, :], ident[:])
                mm.then_inc(s_xt, 1)

            def norm(k, after=None):
                for b in range(B):
                    turn(k, b)
                    if after is not None and b >= 1:
                        after(b - 1)
                if after is not None:
                    after(B - 1)

            def distances(b):
                pe.wait_ge(s_xhi, b + 1)
                if b >= 2:
                    pe.wait_ge(s_d2, b - 1)
                nc.tensor.matmul(ps[4 + b % 2][0:KEYS, :], ones[:, 0:KEYS], sq[:, b % 2, :],
                                 start=True, stop=True).then_inc(s_ab, 1)
                pe.wait_ge(s_ctlo, 1)
                pe.wait_ge(s_xlo, b + 1)
                prod = ps[2 + b % 2][0:KEYS, :]
                nc.tensor.matmul(prod, ctxT_hi[:, b, :], xn_hi[:, sl(b)], start=True, stop=False)
                nc.tensor.matmul(prod, ctxT_lo[:, b, :], xn_hi[:, sl(b)], start=False, stop=False)
                nc.tensor.matmul(prod, ctxT_hi[:, b, :], xn_lo[:, sl(b)], start=False, stop=True).then_inc(s_ab, 1)

            norm(0, distances)
            pe.wait_ge(s_aw, 16 * 8)
            pe.wait_ge(s_d2, B)
            nc.tensor.matmul(ps[4][:, 0:B * KEYS], w4[:, 1, :], ctxT[:].rearrange("p b k -> p (b k)"),
                             start=True, stop=True).then_inc(s_kp, 1)
            for b in range(B):
                out_b = ps[5][0:KEYS, P * b:P * (b + 1)]
                nc.tensor.matmul(out_b, ctxT[:, b, :], w4[:, 2, :], start=True, stop=False)
                mm = nc.tensor.matmul(out_b, ones[0:1, 0:KEYS], brow2[:, 0, :], start=False, stop=True)
            mm.then_inc(s_vp, 1)
            loads = [0, 0]
            for g in range(GROUPS[1]):
                j = g % 2
                loads[j] += 3 * 16 * len(pieces(P * g, min(P * (g + 1), I1 * (E1 + 1))))
                pe.wait_ge(s_pin[j], loads[j])
                if g >= 1:
                    pe.wait_ge(s_pout, g)
                for m in range(3):
                    mm = nc.tensor.transpose(ps[7][:, P * m:P * (m + 1)], prep_in[:, j, P * m:P * (m + 1)], ident[:])
                mm.then_inc(s_pt, 1)
            pe.wait_ge(s_rw[1], 16)
            pe.wait_ge(s_ctlo, 1)
            nc.tensor.transpose(ps[6][:, 0:E1], router1_rows[:], ident[0:E1, 0:E1]).then_inc(s_rt, 1)
            pe.wait_ge(s_chase, KEYS - 1)
            pe.wait_ge(s_rhi, 2)
            nc.tensor.transpose(ps[6][0:KEYS, 0:P], ecol[:], ident[:]).then_inc(s_et, 1)
            pe.wait_ge(s_vx, 1)
            pe.wait_ge(s_er, 1)
            for b in range(B):
                pe.wait_ge(s_path, b + 1)
                for q in range(TPB):
                    mm = nc.tensor.matmul(ps[4 + b][:, P * q:P * (q + 1)], pmask[0:KEYS, b, P * q:P * (q + 1)],
                                          ctx_sb[:, b, :], start=True, stop=True)
                mm.then_inc(s_xa, 1)

            def three_pass(out, w_h, w_l, x_h, x_l, start=True, stop=True):
                nc.tensor.matmul(out, w_h, x_h, start=start, stop=False)
                nc.tensor.matmul(out, w_l, x_h, start=False, stop=False)
                return nc.tensor.matmul(out, w_h, x_l, start=False, stop=stop)

            def query(n):
                pe.wait_ge(s_wql, 1)
                pe.wait_ge(s_xlo, 2 * B + n + 1)
                if n >= 2:
                    pe.wait_ge(s_qlo, n - 1)
                tok = slice(512 * n, 512 * (n + 1))
                three_pass(ps[2 + n % 2][:], wq_hi[:], wq_lo[:], xn_hi[:, tok], xn_lo[:, tok]).then_inc(s_qp, 1)

            def attention():
                pe.wait_ge(s_kbd, HEADS)
                pe.wait_ge(s_vf, 16 * sum(LAST_HEAD[c] + 1 - FIRST_HEAD[c] for c in range(FT)))
                pe.wait_ge(s_epad, 1)
                pe.wait_ge(s_qlo, CHUNKS)

                def scores(i, b, j):
                    pe.wait_ge(s_qs, i + 1)
                    for r, (h0, h1) in enumerate(HSPLIT):
                        if not (isinstance(i, int) and i == 0):
                            pe.wait_ge(s_sub, 3 * i - 2 + r)
                        if isinstance(b, int):
                            k_hi, k_lo = kbd_hi[:, b, h0:h1, :], kbd_lo[:, b, h0:h1, :]
                        else:
                            k_hi, k_lo = [k[:].rearrange("p b h k -> p (b h k)")[:, bass.ds(b * (HEADS * KEYS) + h0 * KEYS, (h1 - h0) * KEYS)]
                                          for k in (kbd_hi, kbd_lo)]
                        three_pass(ps[r][:, 0:(h1 - h0) * KEYS], qs_hi[:, j, :], qs_lo[:, j, :], k_hi, k_lo).then_inc(s_sc, 1)

                def exp_back(i, j):
                    pe.wait_ge(s_exp, i + 1)
                    for r in range(RT):
                        if not (isinstance(i, int) and i == 0):
                            pe.wait_ge(s_ev, RT * i + r - RT + 1)
                        for c in range(HT * r, min(HT * (r + 1), FT)):
                            mm = nc.tensor.transpose(ps[EXP_BANKS[r]][:, P * (c % HT):P * (c % HT + 1)],
                                                     expw[:, j, P * c:P * (c + 1)], ident[:])
                        mm.then_inc(s_tr, 1)

                def values(i, b):
                    if not (isinstance(i, int) and i == 0):
                        pe.wait_ge(s_nrm, i)
                    total = ps[5][:, 0:HEADS * (HD + 1)]
                    nc.tensor.matmul(total, zeros[0:1, 0:P], zeros[0:1, 0:HEADS * (HD + 1)], start=True, stop=False)
                    for c in range(FT):
                        if c % HT == 0:
                            pe.wait_ge(s_ev, RT * i + c // HT + 1)
                        h0, cols = FIRST_HEAD[c], (HD + 1) * (LAST_HEAD[c] + 1 - FIRST_HEAD[c])
                        if isinstance(b, int):
                            v = v_flat[:, b, c, 0:cols]
                        else:
                            v = v_flat[:].rearrange("p b c d -> p (b c d)")[:, bass.ds(b * (FT * FH * (HD + 1)) + c * (FH * (HD + 1)), cols)]
                        nc.tensor.matmul(ps[5][:, (HD + 1) * h0:(HD + 1) * h0 + cols], expT[:, c, :], v, start=False, stop=False)
                    nc.tensor.matmul(total, zeros[0:1, 0:P], zeros[0:1, 0:HEADS * (HD + 1)], start=False, stop=True).then_inc(s_av, 1)

                def av_back(i, j):
                    pe.wait_ge(s_nrm, i + 1)
                    if not (isinstance(i, int) and i == 0):
                        pe.wait_ge(s_au, i)
                    nc.tensor.transpose(ps[6][:, 0:P], av[:, j, :], ident[:]).then_inc(s_avt, 1)

                def project(i):
                    pe.wait_ge(s_avc, i + 1)
                    nc.tensor.matmul(ps[6][:, P:2 * P], avT, w4[:, 3, :], start=True, stop=False)
                    nc.tensor.matmul(ps[6][:, P:2 * P], ones[0:1, :], brow2[:, 1, :], start=False, stop=True).then_inc(s_wo, 1)

                def step(i, b, b_before, j):
                    first = isinstance(i, int)
                    scores(i, b, j)
                    if not (first and i < 2):
                        av_back(i - 2, j)
                    if not (first and i < 1):
                        exp_back(i - 1, 1 - j)
                    if not (first and i < 2):
                        project(i - 2)
                    if not (first and i < 1):
                        values(i - 1, b_before)

                for i in range(TPB):
                    step(i, 0, 0, i % 2)
                with pe.Fori(1, B) as t:
                    for q in range(TPB):
                        step(TPB * t + q, t, t - 1 if q == 0 else t, q % 2)
                av_back(TILES - 2, 0)
                exp_back(TILES - 1, 1)
                project(TILES - 2)
                values(TILES - 1, B - 1)
                av_back(TILES - 1, 1)
                project(TILES - 1)

            def route(f, between):
                E, k = EXPERTS[f], 2 * f + 1

                def logits(b):
                    pe.wait_ge(s_xlo, B * k + b + 1)
                    if b >= 2:
                        pe.wait_ge(s_aff, B * f + b - 1)
                    three_pass(ps[2 + b % 2][0:E, :], router_hi[f][:], router_lo[f][:],
                               xn_hi[:, sl(b)], xn_lo[:, sl(b)]).then_inc(s_logit, 1)

                def by_token(b):
                    pe.wait_ge(s_aff, B * f + b + 1)
                    if b >= 1:
                        pe.wait_ge(s_score, B * f + b)
                    for q in range(TPB):
                        t = TPB * b + q
                        mm = nc.tensor.transpose(ps[7][:, E * q:E * (q + 1)], affT[0:E, P * t:P * (t + 1)], ident[0:E, 0:E])
                    mm.then_inc(s_affT, 1)

                pe.wait_ge(s_rlo, f + 1)
                turn(k, 0)
                turn(k, 1)
                logits(0)
                turn(k, 2)
                logits(1)
                turn(k, 3)
                by_token(0)
                logits(2)
                by_token(1)
                logits(3)
                between()
                by_token(2)
                by_token(3)

            def feed_forward(f):
                T, units = GROUPS[f] // 2, CHUNKS * GROUPS[f]

                def gate_up(g, k, j):
                    u = CHUNKS * g + k
                    if k == 0:
                        pe.wait_ge(FF[f]["wlo"], g + 1)
                    if not (isinstance(g, int) and u < 2):
                        pe.wait_ge(FF[f]["silu"], u - 1)
                        pe.wait_ge(FF[f]["t"], u - 1)
                    tok = slice(512 * k, 512 * (k + 1))
                    three_pass(ps[4 + k % 2][:], w_hi[:, j, 0:P], w_lo[:, j, 0:P],
                               xn_hi[:, tok], xn_lo[:, tok]).then_inc(FF[f]["gate"], 1)
                    three_pass(ps[6 + k % 2][:], w_hi[:, j, UP:UP + P], w_lo[:, j, UP:UP + P],
                               xn_hi[:, tok], xn_lo[:, tok]).then_inc(FF[f]["up"], 1)

                def down(u, n, j):
                    i = n % 2
                    pe.wait_ge(FF[f]["ahi"], u + 1)
                    nc.tensor.matmul(ps[n][:], w_hi[:, j, DOWN:DOWN + P], act_hi[:, i, :], start=False, stop=False)
                    nc.tensor.matmul(ps[n][:], w_lo[:, j, DOWN:DOWN + P], act_hi[:, i, :], start=False, stop=False)
                    pe.wait_ge(FF[f]["alo"], u + 1)
                    nc.tensor.matmul(ps[n][:], w_hi[:, j, DOWN:DOWN + P], act_lo[:, i, :],
                                     start=False, stop=False).then_inc(FF[f]["down"], 1)

                route(f, lambda: gate_up(0, 0, 0))
                pe.wait_ge(s_score, B * (f + 1))
                gate_up(0, 1, 0)
                pe.wait_ge(s_xlo, B * (2 * f + 2))
                pe.wait_ge(s_aff, B * (f + 1))
                for n in range(CHUNKS):
                    nc.tensor.matmul(ps[n][:], zeros[0:1, 0:P], zeros[0:1, :], start=True, stop=False)
                for k in range(2, CHUNKS):
                    gate_up(0, k, 0)
                    down(k - 2, k - 2, 0)
                with pe.Fori(0, T) as t:
                    for jj in range(2):
                        g, j = 2 * t + 1 + jj, 1 - jj
                        for k in range(CHUNKS):
                            gate_up(g, k, j)
                            down(CHUNKS * g + k - 2, (k + 2) % CHUNKS, j if k >= 2 else 1 - j)
                for n in range(CHUNKS - 2, CHUNKS):
                    down(units - CHUNKS + n, n, 0)
                for n in range(CHUNKS):
                    nc.tensor.matmul(ps[n][:], zeros[0:1, 0:P], zeros[0:1, :], start=False, stop=True).then_inc(FF[f]["sum"], 1)
                pe.wait_ge(FF[f]["t"], units)
                for n in range(CHUNKS):
                    pe.wait_ge(FF[f]["yT"], n + 1)
                    for q in range(4):
                        mm = nc.tensor.transpose(ps[4 + n][:, P * q:P * (q + 1)], yT[:, n, P * q:P * (q + 1)], ident[:])
                    mm.then_inc(FF[f]["back"], 1)

            feed_forward(0)
            norm(2, query)
            attention()
            feed_forward(1)

        @block.vector
        def _(dve):
            steps = [0]

            def done(ins):
                steps[0] += 1
                ins.then_inc(s_dve, 1)

            def settle(but=0):
                dve.wait_ge(s_dve, steps[0] - but)

            def stats(k, b):
                tiles = slice(TPB * b, TPB * (b + 1))
                for t in range(TILES)[tiles]:
                    done(nc.vector.bn_stats(stat[:, t, :], x_res[:, t, :]))
                settle()
                for t in range(TILES)[tiles]:
                    done(nc.vector.bn_aggr(mv[:, t, :], stat[:, t, :]))
                settle()
                nc.vector.tensor_scalar(veps[:, tiles], mv[:, tiles, 1], LN_EPS, None, ALU.add).then_inc(s_bn, 1)

            def rsqrt(k, b, tiles):
                dve.wait_ge(s_std, B * k + b + 1)
                done(nc.vector.reciprocal(rstd[:, 0, tiles], std[:, tiles]))
                settle()
                done(nc.vector.tensor_tensor(rstd[:, 1, tiles], rstd[:, 0, tiles], rstd[:, 0, tiles], ALU.mult))
                settle()
                done(nc.vector.scalar_tensor_tensor(rstd[:, 2, tiles], rstd[:, 1, tiles], -0.5, veps[:, tiles],
                                                    ALU.mult, ALU.mult))
                settle()
                nc.vector.scalar_tensor_tensor(rstd[:, 3, tiles], rstd[:, 2, tiles], 1.5, rstd[:, 0, tiles],
                                               ALU.add, ALU.mult).then_inc(s_rstd, 1)

            def normalise(k, b):
                dve.wait_ge(s_rstd, B * k + (b if k < 3 else 0) + 1)
                for t in range(TPB * b, TPB * b + ND):
                    nc.vector.tensor_scalar(xn[:, t, :], x_res[:, t, :], mv[:, t, 0:1], rstd[:, 3, t:t + 1],
                                            ALU.subtract, ALU.mult).then_inc(s_xn, 1)

            def low(k, b):
                dve.wait_ge(s_xhi, B * k + b + 1)
                nc.vector.tensor_tensor(xn_lo[:, sl(b)], ps[b % 2][:], xn_hi[:, sl(b)].bitcast(F32),
                                        ALU.subtract).then_inc(s_xlo, 1)

            def update(n, col):
                xb = x_res[:, TPB * n:TPB * (n + 1), :].rearrange("p q h -> p (q h)")
                nc.vector.scalar_tensor_tensor(xb, ps[4 + n][:], tgate[:, col:col + 1], xb, ALU.mult, ALU.add).then_inc(s_upd, 1)

            def query(n):
                dve.wait_ge(s_qhi, n + 1)
                tok = slice(512 * n, 512 * (n + 1))
                nc.vector.scalar_tensor_tensor(qT_lo[:, tok], ps[2 + n % 2][:], bias2[:, 0:1], qT_hi[:, tok].bitcast(F32),
                                               ALU.add, ALU.subtract).then_inc(s_qlo, 1)

            def norm(k, ready):
                for b in range(B):
                    ready(b)
                    stats(k, b)
                    if b >= 1:
                        rsqrt(k, b - 1, slice(TPB * (b - 1), TPB * b))
                        normalise(k, b - 1)
                    if b >= 2:
                        low(k, b - 2)
                    if b >= 3 and k == 2:
                        query(b - 3)
                rsqrt(k, B - 1, slice(TPB * (B - 1), TILES))
                normalise(k, B - 1)
                for b in range(B - 2, B):
                    low(k, b)
                    if k == 2:
                        query(b - 1)
                if k == 2:
                    query(B - 1)

            dve.wait_ge(s_ctx, 16)
            done(nc.vector.tensor_tensor(aasq[:], ctx_sb[:], ctx_sb[:], ALU.mult))
            settle()
            done(nc.vector.tensor_reduce(aa[:], aasq[:], AX_X, ALU.add))
            dve.wait_ge(s_cthi, 1)
            nc.vector.tensor_tensor(ctxT_lo[:], ps[6][:, 0:B * KEYS].rearrange("p (b k) -> p b k", b=B),
                                    ctxT_hi[:].bitcast(F32), ALU.subtract).then_inc(s_ctlo, 1)
            norm(0, lambda b: dve.wait_ge(s_x[b], 16))
            settle()
            for b in range(B):
                j = b % 2
                dve.wait_ge(s_ab, 2 * b + 2)
                done(nc.vector.tensor_scalar(dsum[0:KEYS, b, :], ps[4 + j][0:KEYS, :], aa[:, b:b + 1], None, ALU.add))
                settle()
                done(nc.vector.scalar_tensor_tensor(dsum[0:KEYS, b, :], ps[2 + j][0:KEYS, :], -2.0, dsum[0:KEYS, b, :],
                                                    ALU.mult, ALU.add))
                settle()
                nc.vector.tensor_scalar(d2[0:KEYS, b, :], dsum[0:KEYS, b, :], TINY, None, ALU.max).then_inc(s_d2, 1)
            for b in range(B):
                dve.wait_ge(s_root, b + 1)
                done(nc.vector.reciprocal(dsum[0:KEYS, b, :], droot[0:KEYS, b, :]))
                done(nc.vector.tensor_tensor(d2[0:KEYS, b, :], d2[0:KEYS, b, :], droot2[0:KEYS, b, :], ALU.subtract))
                settle()
                done(nc.vector.tensor_tensor(d2[0:KEYS, b, :], d2[0:KEYS, b, :], dsum[0:KEYS, b, :], ALU.mult))
                settle()
                nc.vector.scalar_tensor_tensor(drows[0:KEYS, b, :], d2[0:KEYS, b, :], 0.5, droot[0:KEYS, b, :],
                                               ALU.mult, ALU.add).then_inc(s_dist, 1)

            for b in range(B):
                dve.wait_ge(s_dld[b], 16)
            dve.wait_ge(s_pool, POOL_CONST)
            shift = [31] + list(range(CH - 1)) + [31] * (32 - CH)

            def left_steps(s):
                nc.vector.tensor_tensor(lg[:, s, 0, :], rst[:, s + 1, 0:CW], mst[:, s % MST, :], ALU.is_lt).then_inc(s_steps, 1)

            for s in range(SLOTS):
                if s >= 1:
                    dve.wait_ge(s_scan, s)
                prev, cur = rst[:, s, :], rst[:, s + 1, :]
                if s >= MST:
                    dve.wait_ge(s_steps, s - MST + 1)
                nc.vector.tensor_tensor(mst[:, s % MST, :], prev[:, 1:CW + 1], prev[:, 0:CW], ALU.min)
                nc.vector.stream_shuffle(cur[:, 0:1], prev[:, CW:CW + 1], shift).then_inc(s_halo, 1)
                nc.vector.tensor_tensor(lg[:, s, 1, :], prev[:, 0:CW], prev[:, 1:CW + 1], ALU.is_le)
                dve.wait_ge(s_halo, s + 1)
                nc.vector.tensor_tensor_scan(cur[:, 1:CW + 1], mst[:, s % MST, :], dl[:, s, :], cur[:, 0:1],
                                             ALU.min, ALU.add).then_inc(s_scan, 1)
                if s >= 1:
                    left_steps(s - 1)
            dve.wait_ge(s_scan, SLOTS)
            left_steps(SLOTS - 1)

            done(nc.vector.memset(srow[0:KEYS, :, S:S + 1], 2.0 * S))
            for b in range(B):
                dve.wait_ge(s_lgld[b], 32)
                jr = jrow[0:KEYS, :]
                left, diag = lgr[0:KEYS, 0, b, :], lgr[0:KEYS, 1, b, :]
                done(nc.vector.scalar_tensor_tensor(nlj[0:KEYS, b, :], left, 1.0, jr, ALU.is_lt, ALU.mult))
                done(nc.vector.tensor_tensor(nup[0:KEYS, b, :], left, diag, ALU.max))
                settle()
                done(nc.vector.tensor_tensor_scan(srow[0:KEYS, b, 0:S][:, ::-1],
                                                  left[:, ::-1], nlj[0:KEYS, b, :][:, ::-1], 2.0 * S, ALU.mult, ALU.add))
                done(nc.vector.scalar_tensor_tensor(ubig[0:KEYS, b, :], nup[0:KEYS, b, :], 2.0 * S, jr, ALU.mult, ALU.add))
                settle()
                nc.vector.tensor_tensor(trow[0:KEYS, b, :], ubig[0:KEYS, b, :], srow[0:KEYS, b, 1:S + 1],
                                        ALU.min).then_inc(s_trow, 1)

            for b in range(B):
                dve.wait_ge(s_tch[b], 16)
            for i in range(KEYS - 1, 0, -1):
                if i < KEYS - 1:
                    dve.wait_ge(s_chase, KEYS - 1 - i)
                nc.vector.tensor_scalar(junk[CHASE, 1:S], chase[:, i, 1:S], ecol[CHASE, i:i + 1], 0.0, ALU.is_le, ALU.add,
                                        accum_out=ecol[CHASE, i - 1:i]).then_inc(s_chase, 1)

            dve.wait_ge(s_pool, POOL_CONST)
            nc.vector.tensor_scalar(zeros[:], jrow[0:1, :], 0.0, None, ALU.mult)
            for f in range(2):
                dve.wait_ge(s_rhi, f + 1)
                nc.vector.tensor_tensor(router_lo[f][:], router[f][:], router_hi[f][:].bitcast(F32),
                                        ALU.subtract).then_inc(s_rlo, 1)

            dve.wait_ge(s_er, 1)
            for b in range(B):
                done(nc.vector.tensor_scalar(pcond[0:KEYS, b, :], srow[0:KEYS, b, 1:S + 1], erow[:, b:b + 1], None, ALU.is_gt))
                settle()
                nc.vector.scalar_tensor_tensor(pmask[0:KEYS, b, :], jrow[0:KEYS, :], erow[:, b:b + 1], pcond[0:KEYS, b, :],
                                               ALU.is_le, ALU.mult).then_inc(s_path, 1)

            def add_aligned(b):
                dve.wait_ge(s_xa, b + 1)
                update(b, 0)
                dve.wait_ge(s_upd, b + 1)

            def add_ffn(f):
                def add(n):
                    dve.wait_ge(FF[f]["back"], n + 1)
                    update(n, 2 + f)
                    dve.wait_ge(s_upd, B * (f + 1) + n + 1)
                return add

            def first_lo(f):
                for g in range(2):
                    dve.wait_ge(FF[f]["whi"], g + 1)
                    nc.vector.tensor_tensor(w_lo[:, g, :], w_raw[:, g, :], w_hi[:, g, :].bitcast(F32),
                                            ALU.subtract).then_inc(FF[f]["wlo"], 1)

            def route0(b):
                tiles = slice(TPB * b, TPB * (b + 1))
                dve.wait_ge(s_score, b + 1)
                for t in range(TILES)[tiles]:
                    done(nc.vector.max(top8[:, t, :], aff[0][:, t, :]))
                settle()
                done(nc.vector.tensor_reduce(rsum[:, 0, tiles], top8[:, tiles, :], AX_X, ALU.add))
                for t in range(TILES)[tiles]:
                    done(nc.vector.match_replace(rest[0][:, t, :], top8[:, t, :], aff[0][:, t, :], 0.0))
                settle(but=TPB)
                done(nc.vector.tensor_scalar(rsum[:, 1, tiles], rsum[:, 0, tiles], 1e-9, None, ALU.add))
                settle()
                done(nc.vector.reciprocal(rsum[:, 2, tiles], rsum[:, 1, tiles]))
                done(nc.vector.tensor_tensor(rest[0][:, tiles, :], aff[0][:, tiles, :], rest[0][:, tiles, :], ALU.subtract))
                settle()
                done(nc.vector.tensor_tensor(wsel[0][:, tiles, :], rest[0][:, tiles, :],
                                             rsum[:, 2, tiles].unsqueeze(2).broadcast_to([P, TPB, E0]), ALU.mult))
                settle()
                nc.vector.transpose(wT[0][:, tiles, :].rearrange("p t e -> p (t e)"),
                                    wsel[0][:, tiles, :].rearrange("p t e -> p (t e)")).then_inc(s_wt, 1)

            def route1(part):
                E = E1
                sc, ex = aff[1], rest[1]

                def by_tile(col):
                    return rsum[:, col, :].unsqueeze(2).broadcast_to([P, TILES, E])

                if part == 0:
                    dve.wait_ge(s_score, 2 * B)
                    done(nc.vector.tensor_reduce(rsum[:, 0, :], sc, AX_X, ALU.max))
                    settle()
                    nc.vector.tensor_tensor(ex, sc, by_tile(0), ALU.subtract).then_inc(s_rsub, 1)
                    done(nc.vector.memset(wsel[1], 0.0))
                if part == 1:
                    dve.wait_ge(s_rexp, 1)
                    done(nc.vector.tensor_reduce(rsum[:, 1, :], ex, AX_X, ALU.add))
                    settle()
                    done(nc.vector.reciprocal(rsum[:, 2, :], rsum[:, 1, :]))
                    settle()
                    done(nc.vector.tensor_tensor(sc, ex, by_tile(2), ALU.mult))
                    settle()
                    for t in range(TILES):
                        done(nc.vector.max(top8[:, t, :], sc[:, t, :]))
                if part == 2:
                    settle()
                    for t in range(TILES):
                        done(nc.vector.max_index(topi[:, t, :], top8[:, t, :], sc[:, t, :]))
                    done(nc.vector.tensor_tensor(rsum[:, 0, :], top8[:, :, 0], top8[:, :, 1], ALU.add))
                    settle()
                    done(nc.vector.tensor_scalar(rsum[:, 1, :], rsum[:, 0, :], 1e-20, None, ALU.add))
                    done(nc.vector.tensor_copy(topf, topi))
                    settle()
                    done(nc.vector.reciprocal(rsum[:, 2, :], rsum[:, 1, :]))
                if part == 3:
                    settle()
                    for c in range(2):
                        done(nc.vector.tensor_tensor(hit[c], iota_e[:].unsqueeze(1).broadcast_to([P, TILES, E]),
                                                     topf[:, :, c:c + 1].broadcast_to([P, TILES, E]), ALU.is_equal))
                    done(nc.vector.tensor_tensor(ex, sc, by_tile(2), ALU.mult))
                    settle()
                    done(nc.vector.tensor_tensor(hit[0], hit[0], hit[1], ALU.add))
                    settle()
                    done(nc.vector.tensor_tensor(wsel[1][:, :, 0:E], ex, hit[0], ALU.mult))
                    settle()
                    nc.vector.transpose(wT[1].rearrange("p t e -> p (t e)"),
                                        wsel[1].rearrange("p t e -> p (t e)")).then_inc(s_wt, 1)

            def attention():
                first_lo(1)

                def shift_scores(i, j):
                    for r, (h0, h1) in enumerate(HSPLIT):
                        dve.wait_ge(s_sc, 3 * i + r + 1)
                        sc = ps[r][:, 0:(h1 - h0) * KEYS].rearrange("p (h k) -> p h k", k=KEYS)
                        nc.vector.tensor_reduce(smax[:, j, h0:h1], sc, AX_X, ALU.max).then_inc(s_mx, 1)
                    if not (isinstance(i, int) and i < 2):
                        dve.wait_ge(s_tr, RT * (i - 1))
                    for r, (h0, h1) in enumerate(HSPLIT):
                        dve.wait_ge(s_mx, 3 * i + r + 1)
                        sc = ps[r][:, 0:(h1 - h0) * KEYS].rearrange("p (h k) -> p h k", k=KEYS)
                        to = expw[:, j, h0 * KEYS:h1 * KEYS].rearrange("p (h k) -> p h k", k=KEYS)
                        nc.vector.tensor_tensor(to, sc, smax[:, j, h0:h1].unsqueeze(2).broadcast_to([P, h1 - h0, KEYS]),
                                                ALU.subtract).then_inc(s_sub, 1)

                def normalise_heads(i, j):
                    dve.wait_ge(s_av, i + 1)
                    o = ps[5][:, 0:HEADS * (HD + 1)].rearrange("p (h d) -> p h d", d=HD + 1)
                    nc.vector.reciprocal(rden[:, j, :], o[:, :, HD]).then_inc(s_rd, 1)
                    dve.wait_ge(s_rd, i + 1)
                    if not (isinstance(i, int) and i < 2):
                        dve.wait_ge(s_avt, i - 1)
                    nc.vector.tensor_tensor(av[:, j, :].rearrange("p (h d) -> p h d", d=HD), o[:, :, 0:HD],
                                            rden[:, j, :].unsqueeze(2).broadcast_to([P, HEADS, HD]), ALU.mult).then_inc(s_nrm, 1)

                def add_tile(i):
                    dve.wait_ge(s_wo, i + 1)
                    xi = x_res[:, i, :] if isinstance(i, int) else x_res[:].rearrange("p t h -> p (t h)")[:, bass.ds(P * i, P)]
                    nc.vector.scalar_tensor_tensor(xi, ps[6][:, P:2 * P], tgate[:, 1:2], xi,
                                                   ALU.mult, ALU.add).then_inc(s_au, 1)

                def tile_stats(i):
                    dve.wait_ge(s_au, i + 1)
                    if isinstance(i, int):
                        xi, st = x_res[:, i, :], stat[:, i, :]
                    else:
                        xi = x_res[:].rearrange("p t h -> p (t h)")[:, bass.ds(P * i, P)]
                        st = stat[:].rearrange("p t s -> p (t s)")[:, bass.ds(6 * i, 6)]
                    nc.vector.bn_stats(st, xi).then_inc(s_st, 1)

                def step(i, j):
                    first = isinstance(i, int)
                    shift_scores(i, j)
                    if not (first and i < 2):
                        add_tile(i - 2)
                    if not (first and i < 1):
                        normalise_heads(i - 1, 1 - j)
                    if not (first and i < 2):
                        tile_stats(i - 2)

                for i in range(TPB):
                    step(i, i % 2)
                with dve.Fori(1, B) as t:
                    for q in range(TPB):
                        step(TPB * t + q, q % 2)
                add_tile(TILES - 2)
                normalise_heads(TILES - 1, 1)
                tile_stats(TILES - 2)
                add_tile(TILES - 1)
                tile_stats(TILES - 1)

            def feed_forward(f):
                T, units = GROUPS[f] // 2, CHUNKS * GROUPS[f]

                def split_lo(g, j):
                    dve.wait_ge(FF[f]["whi"], g + 1)
                    nc.vector.tensor_tensor(w_lo[:, j, :], w_raw[:, j, :], w_hi[:, j, :].bitcast(F32),
                                            ALU.subtract).then_inc(FF[f]["wlo"], 1)

                def unit(g, k, j, load, last=False):
                    u = CHUNKS * g + k
                    i = k % 2
                    early = isinstance(g, int) and u < 2
                    if k == SPLIT_AT and not last and not (isinstance(g, int) and g == 0):
                        split_lo(g + 1, 1 - j)
                    dve.wait_ge(FF[f]["silu"], u + 1)
                    dve.wait_ge(FF[f]["up"], u + 1)
                    if not early:
                        dve.wait_ge(FF[f]["act"], u - 1)
                    nc.vector.tensor_tensor(act_t[:, i, :], act_s[:, i, :], ps[6 + i][:], ALU.mult).then_inc(FF[f]["t"], 1)
                    if k == 0:
                        dve.wait_ge(FF_MASK[f][j], 16 * MASK_DMAS * load)
                    dve.wait_ge(FF[f]["t"], u + 1)
                    if not early:
                        dve.wait_ge(FF[f]["alo"], u - 1)
                    nc.vector.tensor_tensor(act_a[:, i, :], act_t[:, i, :], mask[:, j, 512 * k:512 * (k + 1)],
                                            ALU.mult).then_inc(FF[f]["act"], 1)

                if f == 0:
                    for b in range(B):
                        route0(b)
                for k in range(CHUNKS):
                    if f == 1:
                        route1(k)
                    unit(0, k, 0, 1)
                with dve.Fori(0, T - 1) as t:
                    for jj in range(2):
                        for k in range(CHUNKS):
                            unit(2 * t + 1 + jj, k, 1 - jj, t + 1 + jj)
                for jj in range(2):
                    for k in range(CHUNKS):
                        unit(2 * T - 1 + jj, k, 1 - jj, T + jj, last=jj == 1)

            first_lo(0)
            norm(1, add_aligned)
            feed_forward(0)
            norm(2, add_ffn(0))
            attention()
            dve.wait_ge(s_st, TILES)
            for t in range(TILES):
                done(nc.vector.bn_aggr(mv[:, t, :], stat[:, t, :]))
            settle()
            nc.vector.tensor_scalar(veps[:], mv[:, :, 1], LN_EPS, None, ALU.add).then_inc(s_bn, 1)
            rsqrt(3, 0, slice(0, TILES))
            for b in range(B):
                normalise(3, b)
            for b in range(B):
                low(3, b)
            feed_forward(1)
            for n in range(CHUNKS):
                add_ffn(1)(n)


INPUTS = ["x", "ctx_1024", "g_xattn", "g_ffn", "L0_ffn_router_w", "L0_ffn_shared_gate_w", "L0_ffn_shared_up_w",
          "L0_ffn_shared_down_w", "L0_ffn_expert_gate_k", "L0_ffn_expert_up_k", "L0_ffn_expert_down_k",
          "L1_xattn_Wq", "L1_xattn_bq", "L1_xattn_Wk", "L1_xattn_bk", "L1_xattn_Wv", "L1_xattn_bv",
          "L1_xattn_Wo", "L1_xattn_bo", "L1_ffn_gate_w", "L1_ffn_wg", "L1_ffn_wu", "L1_ffn_wd",
          "L1_ffn_swg", "L1_ffn_swu", "L1_ffn_swd"]


def kernel(**inputs):
    import numpy as _np
    import concourse.bacc as _bacc
    from concourse import mybir as _mybir
    from concourse.bass_utils import run_bass_kernel_spmd as _run

    nc = _bacc.Bacc("TRN2", target_bir_lowering=False, num_devices=1)
    arrays, args = {}, []
    for name in INPUTS:
        a = _np.ascontiguousarray(inputs[name])
        arrays[f"in_{name}"] = a
        args.append(nc.dram_tensor(f"in_{name}", a.shape, _mybir.dt.from_np(a.dtype), kind="ExternalInput").ap())
    shape = tuple(inputs["x"].shape)
    args.append(nc.dram_tensor("out", shape, _mybir.dt.float32, kind="ExternalOutput").ap())
    program(nc, *args)
    r = _run(nc, [arrays], core_ids=[0])
    return r.results[0]["out"]
```

```python
from contextlib import ExitStack

import concourse.bass as bass
import concourse.mybir as mybir
from concourse.alu_op_type import AluOpType as ALU

F32 = mybir.dt.float32
F32R = mybir.dt.float32r
F16 = mybir.dt.float16
U32 = mybir.dt.uint32
I32 = mybir.dt.int32
ACT = mybir.ActivationFunctionType
AX_X = mybir.AxisListType.X

P = 128
BIG = 1e30
TINY = 1e-30
HALF_OVER = 0x7E7311C3
LN_EPS = 1e-5


def program(nc, x, ctx_1024, g_xattn, g_ffn, r0_w, sg0, su0, sd0, eg0, eu0, ed0,
            Wq, bq, Wk, bk, Wv, bv, Wo, bo, r1_w, wg1, wu1, wd1, swg1, swu1, swd1, out):
    B, S, H = x.shape
    KEYS = ctx_1024.shape[1]
    TOK = B * S
    TILES = TOK // P
    TPB = S // P
    assert H == P and S == 512 and B == 4

    CH = 16
    CW = S // CH
    SLOTS = KEYS + CH - 1
    LANE = SLOTS * CW
    LANES = [32 * b for b in range(B)]

    E0, I0 = eg0.shape[0], eg0.shape[2]
    E1, I1 = wg1.shape[0], wg1.shape[1]
    K0 = 8
    assert P == 2 * I0 and E0 == 64 and E1 <= 32
    EXPERTS = [E0, E1]
    CHUNKS = TOK // 512
    GROUPS = [1 + E0 // 2, -(-I1 * (E1 + 1) // P)]
    PEEL, BODY, REST = 3, 4, 2
    LOOPS = [(n - PEEL - REST) // BODY for n in GROUPS]
    assert all(PEEL + BODY * t + REST == n for n, t in zip(GROUPS, LOOPS)) and PEEL % 2 == 1
    ROUTE1_TILES = [slice(0, TILES - TPB), slice(TILES - TPB, TILES)]
    ROUTE1_BEFORE = {0: [(0, 1), (1, 0), (0, 2)], 1: [(0, 3)], 2: [(0, 4), (1, 1)], 3: [(1, 2), (1, 3)], 4: [(1, 4), (1, 5)]}
    SPLIT_AT = 2
    UP, DOWN, WIDE = P, 2 * P, 3 * P

    HEADS, HD = 16, H // 16
    HPB = 6
    HSPLIT = [(0, HPB), (HPB, 2 * HPB), (2 * HPB, HEADS)]
    FLAT = HEADS * KEYS
    FT = -(-FLAT // P)
    HT = 4
    FIRST_HEAD = [P * c // KEYS for c in range(FT)]
    LAST_HEAD = [(min(P * (c + 1), FLAT) - 1) // KEYS for c in range(FT)]
    FH = max(b - a for a, b in zip(FIRST_HEAD, LAST_HEAD)) + 1
    RT = -(-FT // HT)
    EXP_BANKS = [3, 4, 7]
    assert RT == len(EXP_BANKS)

    def pieces(first, last):
        found = []
        while first < last:
            n = min(last, (first // I1 + 1) * I1) - first
            found.append((first // I1 - 1, first % I1, n))
            first += n
        return found

    ctx = ExitStack()
    with ctx:
        def sb(name, shape, dt=F32):
            return ctx.enter_context(nc.sbuf_tensor(name, shape, dt))

        def sem(name):
            return ctx.enter_context(nc.semaphore(name))

        ps = [ctx.enter_context(nc.psum_tensor(f"bank{i}", [P, 512], F32)) for i in range(8)]

        scr_d = nc.dram_tensor("scr_d", (B, CH, SLOTS, CW), F32).ap()
        scr_one = nc.dram_tensor("scr_one", (TOK,), F32).ap()
        scr_w1 = nc.dram_tensor("scr_w1", (GROUPS[1], P, WIDE), F32).ap()
        scr_mask = [nc.dram_tensor("scr_mask0", (E0 // 2, B, 2, S), F32).ap(),
                    nc.dram_tensor("scr_mask1", (E1, TOK), F32).ap()]
        scr_lg = nc.dram_tensor("scr_lg", (B, CH, SLOTS, 2, CW), F16).ap()

        ND = TPB - 1

        x_res = sb("x_res", [P, TILES, H])
        xn = sb("xn", [P, TILES, H])
        xn_hi = sb("xn_hi", [P, TOK], F32R)
        xn_lo = sb("xn_lo", [P, TOK], F32R)
        stat = sb("stat", [P, TILES, 6])
        mv = sb("mv", [P, TILES, 2])
        veps = sb("veps", [P, TILES])
        std = sb("std", [P, TILES])
        rstd = sb("rstd", [P, 4, TILES])
        ident = sb("ident", [P, P])
        ones = sb("ones", [P, P])
        gates = sb("gates", [P, 4])
        tgate = sb("tgate", [P, 4])
        ctx_sb = sb("ctx_sb", [KEYS, B, H])
        ctxT = sb("ctxT", [P, B, KEYS])
        ctxT_hi = sb("ctxT_hi", [P, B, KEYS], F32R)
        ctxT_lo = sb("ctxT_lo", [P, B, KEYS], F32R)
        zeros = sb("zeros", [1, 512], F32R)
        iota_e = sb("iota_e", [P, E1])
        jrow = sb("jrow", [P, S], F16)
        ecol = sb("ecol", [P, KEYS])
        erow = sb("erow", [KEYS, B])
        erow_half = sb("erow_half", [KEYS, B])
        junk = sb("junk", [P, S], F16)
        aa = sb("aa", [KEYS, B])
        aasq = sb("aasq", [KEYS, B, H])

        w_raw = sb("w_raw", [P, 2, WIDE])
        w_hi = sb("w_hi", [P, 2, WIDE], F32R)
        w_lo = sb("w_lo", [P, 2, WIDE], F32R)
        prep_in = sb("prep_in", [P, 2, WIDE])
        prep_out = sb("prep_out", [P, 2, WIDE])
        router = [sb("router0", [P, E0]), sb("router1", [P, E1])]
        act_hi = sb("act_hi", [P, 2, 512], F32R)
        act_lo = sb("act_lo", [P, 2, 512], F32R)
        kT = sb("kT", [P, B * KEYS])
        kT_hi = sb("kT_hi", [P, B * KEYS], F32R)
        kT_lo = sb("kT_lo", [P, B * KEYS], F32R)
        v_ext = sb("v_ext", [KEYS, B, HEADS, HD + 1])
        v_flat = sb("v_flat", [P, B, FT, FH * (HD + 1)])
        kbd_hi = sb("kbd_hi", [P, B, HEADS, KEYS], F32R)
        kbd_lo = sb("kbd_lo", [P, B, HEADS, KEYS], F32R)
        qs_hi = sb("qs_hi", [P, 2, P], F32R)
        qs_lo = sb("qs_lo", [P, 2, P], F32R)
        router1_rows = sb("router1_rows", [E1, P])
        w4 = sb("w4", [P, 4, P])
        wq_hi = sb("wq_hi", [P, P], F32R)
        wq_lo = sb("wq_lo", [P, P], F32R)
        bias2 = sb("bias2", [P, 2])
        brow2 = sb("brow2", [1, 2, P])
        headmask = sb("headmask", [P, HEADS])

        ARENA = 20600
        arena = sb("arena", [P, ARENA])
        mark = [0]

        def view(shape, dt=F32):
            n = 1
            for k in shape:
                n *= k
            cols = n // 2 if dt == F16 else n
            v = arena[:, mark[0]:mark[0] + cols]
            mark[0] += cols
            assert mark[0] <= ARENA
            if dt != F32:
                v = v.bitcast(dt)
            if len(shape) == 2:
                v = v.rearrange("p (a b) -> p a b", a=shape[0])
            if len(shape) == 3:
                v = v.rearrange("p (a b c) -> p a b c", a=shape[0], b=shape[1])
            return v

        sq = view([2, S])
        dinv = view([B, S])
        d2 = view([B, S])
        droot = view([B, S])
        droot2 = view([B, S])
        drows = view([B, S])
        dl = view([SLOTS, CW])
        rst = view([SLOTS + 1, CW + 1])
        MST = 8
        mst = view([MST, CW])
        lg = view([SLOTS, 2, CW], F16)
        mark[0] = 0
        lgr = view([2, B, S], F16)
        nlj = view([B, S], F16)
        nup = view([B, S], F16)
        ubig = view([B, S], F16)
        srow = view([B, S + 8], F16)
        trow = view([B, S], F16)
        before = view([B, S], F16)
        mark[0] = 0
        pmask = view([B, S])
        CHASE = slice(96, 96 + B)
        mark[0] = 0
        chase = view([KEYS, S], F16)[CHASE]
        mark[0] = 0
        mask = view([2, TOK])
        act_s = view([2, 512])
        act_t = view([2, 512])
        act_a = view([2, 512])
        yT = view([CHUNKS, 512])
        mark[0] += FT * P
        XT_FROM = mark[0]
        xT = view([TOK])
        aff = [view([TILES, E]) for E in EXPERTS]
        rest = [view([TILES, E]) for E in EXPERTS]
        wsel = [view([B, 2 * TPB, 32]), view([TILES, 32])]
        wT = [view([B, 2 * TPB, 32]), view([TILES, 32])]
        top8 = view([TILES, 8])
        topi = view([TILES, 8], U32)
        topf = view([TILES, 8])
        hit = [view([TILES, E1]) for c in range(2)]
        rsum = view([4, TILES])

        mark[0] = 0
        qT_hi = view([TOK], F32R)
        qT_lo = view([TOK], F32R)
        expw = view([2, FT * P])
        smax = view([2, HEADS])
        expT = view([2, FT * P])
        rden = view([2, HEADS])
        av = view([2, H])
        avT = view([P])
        assert mark[0] <= XT_FROM

        s_aw = sem("attn_weights_loaded")
        s_kp = sem("k_projected")
        s_vp = sem("v_projected")
        s_khi = sem("kT_hi_ready")
        s_klo = sem("kT_lo_ready")
        s_vx = sem("v_ready")
        s_vf = sem("v_flat_loaded")
        s_epad = sem("exp_padded")
        s_kbd = sem("kbd_ready")
        s_wql = sem("wq_lo_ready")
        s_wqh = sem("wq_hi_ready")
        s_qp = sem("q_projected")
        s_qhi = sem("qT_hi_ready")
        s_qlo = sem("qT_lo_ready")
        s_qs = sem("q_tile_ready")
        s_sc = sem("scores")
        s_mx = sem("scores_max")
        s_sub = sem("scores_shifted")
        s_exp = sem("exp_ready")
        s_tr = sem("exp_transposed")
        s_ev = sem("exp_copied")
        s_av = sem("av_products")
        s_rd = sem("av_reciprocal")
        s_nrm = sem("av_normalised")
        s_avt = sem("av_transposed")
        s_avc = sem("av_copied")
        s_wo = sem("out_projected")
        s_st = sem("tile_stats")
        s_au = sem("x_updated_attn")
        s_one = sem("ones_stored")
        s_rw = [sem("router0_loaded"), sem("router1_loaded")]
        s_rt = sem("router1_transposed")
        s_r1 = sem("router1_ready")
        s_xT = sem("xT_ready")
        s_logit = sem("router_logits")
        s_score = sem("router_scores")
        s_rsub = sem("router_shifted")
        s_rexp = sem("router_exp")
        s_pad = sem("router_padded")
        s_rcp = sem("router_sums_inverted")
        s_dif = sem("router_chosen_scores")
        s_sel = sem("router_chosen_weights")
        s_wt = sem("router_weights_ready")
        s_mst = [sem(f"mask0_stored{b}") for b in range(B)] + [sem("mask1_stored")]
        s_pin = [sem(f"prep_loaded{j}") for j in range(2)]
        s_pzero = sem("prep_zeroed")
        s_pt = sem("prep_transposed")
        s_pout = sem("prep_copied")
        s_pst = [sem(f"prep_stored{j}") for j in range(2)]
        FF = [dict((n, sem(f"ff{f}_{n}")) for n in (
            "whi", "wlo", "gate", "up", "silu", "t", "act", "ahi", "alo", "down", "sum", "yT", "back")) for f in range(2)]
        FF_RAW = [[sem(f"ff{f}_raw_loaded{j}") for j in range(2)] for f in range(2)]
        FF_MASK = [[sem(f"ff{f}_mask_loaded{j}") for j in range(2)] for f in range(2)]
        s_mask1 = [sem(f"ff0_group1_mask_loaded{b}") for b in range(B)]
        RAW_DMAS, MASK_DMAS = [4, 1], 2

        def raw_loaded(f, g):
            return 16 * RAW_DMAS[f] * (g // 2 + 1)

        def mask_loaded(f, half, odd):
            first = 1 if f == 0 and odd else 0
            return 16 * MASK_DMAS * (half + 1 - first)
        s_x = [sem(f"x_loaded{b}") for b in range(B)]
        s_ctx = sem("ctx_loaded")
        s_gate = sem("gates_loaded")
        s_zero = sem("scratch_zeroed")
        s_pool = sem("pool_step")
        s_dve = sem("dve_step")
        s_act = sem("act_step")
        s_bn = sem("ln_var_ready")
        s_std = sem("ln_std_ready")
        s_rstd = sem("ln_rstd_ready")
        s_xn = sem("xn_ready_dve")
        s_xnp = sem("xn_ready_pool")
        s_xt = sem("xn_transposed")
        s_xhi = sem("xn_hi_ready")
        s_xlo = sem("xn_lo_ready")
        s_ct = sem("ctx_transposed")
        s_cthi = sem("ctxT_hi_ready")
        s_ctlo = sem("ctxT_lo_ready")
        s_ab = sem("dist_products")
        s_dsum = sem("dist_sum")
        s_d2 = sem("dist_squared")
        s_root = sem("dist_root")
        s_err = sem("dist_root_error")
        s_dist = sem("dist_ready")
        s_dst = [sem(f"dist_stored{b}") for b in range(B)]
        s_dld = [sem(f"dist_lanes{b}") for b in range(B)]
        s_halo = sem("wave_halo")
        s_scan = sem("wave_row")
        s_steps = sem("wave_steps")
        s_lgst = [sem(f"steps_stored{b}") for b in range(B)]
        s_lgld = [sem(f"steps_rows{b}") for b in range(B)]
        s_trow = sem("t_rows_ready")
        s_tch = [sem(f"chase_rows{b}") for b in range(B)]
        s_chase = sem("chase_step")
        s_et = sem("entries_transposed")
        s_er = sem("entries_by_row")
        s_erh = sem("entries_and_half")
        s_before = sem("path_before_entry")
        s_path = sem("path_ready")
        s_xa = sem("aligned_sum")
        s_upd = sem("x_updated")
        s_out = sem("out_stored")

        x_t = x.rearrange("b (q p) h -> b p q h", p=P)
        out_t = out.rearrange("b (q p) h -> b p q h", p=P)

        def at(t, offset, ap):
            return bass.AP(tensor=t.tensor, offset=t.offset + offset, ap=ap)

        def sl(b):
            return slice(S * b, S * (b + 1))

        def turn_bank(k, b):
            return ps[b if k == 3 else b % 2]

        def logit_bank(f, b):
            E = EXPERTS[f]
            bank, col = (2 + b % 2, 0) if f == 0 else (0, b * TPB * E) if b < B - 1 else (1, 0)
            return ps[bank][:, col:col + TPB * E].rearrange("p (t e) -> p t e", e=E)

        def prep_rows(first, last):
            found = []
            for m, (shared, experts) in enumerate(((swg1, wg1), (swu1, wu1))):
                if first < I1:
                    n = min(last, I1) - first
                    found.append((slice(0, n), m, shared[first:first + n, :]))
                if last > I1:
                    n = max(first, I1)
                    found.append((slice(n - first, last - first), m, experts.rearrange("e i h -> (e i) h")[n - I1:last - I1, :]))
            return found

        block = ctx.enter_context(nc.Block())
        POOL_CONST = 12 + B

        @block.sync
        def _(sp):
            for b in range(B):
                sp.dma_start(x_res[:, TPB * b:TPB * (b + 1), :], x_t[b]).then_inc(s_x[b], 16)
                if b == 0:
                    sp.dma_start(ctx_sb[:], ctx_1024.rearrange("b k d -> k b d")).then_inc(s_ctx, 16)
            sp.dma_start(gates[:, 0:2], g_xattn.partition_broadcast(P)).then_inc(s_gate, 16)
            sp.dma_start(gates[:, 2:4], g_ffn.partition_broadcast(P)).then_inc(s_gate, 16)
            sp.dma_start(router[0][:], r0_w).then_inc(s_rw[0], 16)
            for m, w in enumerate((Wq, Wk, Wv, Wo)):
                sp.dma_start(w4[:, m, :], w).then_inc(s_aw, 16)
            for m, v in enumerate((bq, bk)):
                sp.dma_start(bias2[:, m:m + 1], v.rearrange("(p o) -> p o", o=1)).then_inc(s_aw, 16)
            for m, v in enumerate((bv, bo)):
                sp.dma_start(brow2[:, m, :], v.rearrange("(o p) -> o p", o=1)).then_inc(s_aw, 16)
            sp.dma_start(router1_rows[:], r1_w).then_inc(s_rw[1], 16)
            sp.wait_ge(s_pool, 2)
            sp.dma_start(scr_one.rearrange("(p c) -> p c", c=P), ones[0:TOK // P, :]).then_inc(s_one, 16)
            sp.dma_start(w_raw[:, 0, 0:I0], sg0).then_inc(FF_RAW[0][0], 16)
            sp.dma_start(w_raw[:, 0, UP:UP + I0], su0).then_inc(FF_RAW[0][0], 16)
            for k in range(2):
                sp.dma_start(w_raw[k * I0 // 2:(k + 1) * I0 // 2, 0, DOWN:DOWN + P],
                             sd0[k * I0 // 2:(k + 1) * I0 // 2]).then_inc(FF_RAW[0][0], 16)
            sp.wait_ge(s_pool, POOL_CONST)
            sp.dma_start(scr_d.rearrange("b c s w -> (b c) (s w)"),
                         dl[0:B * CH].rearrange("p s w -> p (s w)")).then_inc(s_zero, 16)
            sp.wait_ge(s_zero, 16)
            for b in range(B):
                sp.wait_ge(s_dist, b + 1)
                sp.dma_start(at(scr_d[b], 0, [[CW, KEYS], [LANE + CW, CH], [1, CW]]),
                             drows[0:KEYS, b, :].rearrange("i (c w) -> i c w", w=CW)).then_inc(s_dst[b], 16)
            for b in range(B):
                sp.wait_ge(s_dst[b], 16)
                sp.dma_start(dl[LANES[b]:LANES[b] + CH].rearrange("c s w -> c (s w)"),
                             scr_d[b].rearrange("c s w -> c (s w)")).then_inc(s_dld[b], 16)
            sp.wait_ge(s_vx, 1)
            for h in range(HEADS):
                for c in range(FT):
                    r0, r1 = max(KEYS * h, P * c), min(KEYS * (h + 1), P * (c + 1))
                    if r0 < r1:
                        col = (HD + 1) * (h - FIRST_HEAD[c])
                        sp.dma_start(v_flat[r0 - P * c:r1 - P * c, :, c, col:col + HD + 1],
                                     v_ext[r0 - KEYS * h:r1 - KEYS * h, :, h, :]).then_inc(s_vf, 16)
            sp.wait_ge(s_steps, SLOTS)
            for b in range(B):
                sp.dma_start(scr_lg[b].rearrange("c s a w -> c (s a w)"),
                             lg[LANES[b]:LANES[b] + CH].rearrange("c s a w -> c (s a w)")).then_inc(s_lgst[b], 16)
            for b in range(B):
                sp.wait_ge(s_lgst[b], 16)
                for a in range(2):
                    sp.dma_start(lgr[0:KEYS, a, b, :].rearrange("i (c w) -> i c w", w=CW),
                                 at(scr_lg[b], a * CW, [[2 * CW, KEYS], [2 * (LANE + CW), CH], [1, CW]])
                                 ).then_inc(s_lgld[b], 16)
            for b in range(B):
                sp.wait_ge(s_trow, b + 1)
                sp.dma_start(chase[b:b + 1], trow[0:KEYS, b, :]).then_inc(s_tch[b], 16)

            def raw0(g, j):
                r = bass.ds(g - 1, 1)
                dst = w_raw[:, j, 0:DOWN].rearrange("p (m k i) -> p m k i", m=2, k=2)
                for m, w in enumerate((eg0, eu0)):
                    src = w.rearrange("(k r) h i -> r h k i", k=2)[r].rearrange("a h k i -> (a h) k i")
                    sp.dma_start(dst[:, m], src).then_inc(FF_RAW[0][j], 16)
                for k in range(2):
                    src = ed0[32 * k:32 * (k + 1)][r].rearrange("a i h -> (a i) h")
                    sp.dma_start(w_raw[I0 * k:I0 * (k + 1), j, DOWN:DOWN + P], src).then_inc(FF_RAW[0][j], 16)

            def mask0(g, j, chunks, loaded):
                for k in range(2):
                    row = scr_mask[0][bass.ds(g - 1, 1), chunks, k, :].rearrange("a b s -> (a b) s")
                    dst = mask[I0 * k:I0 * (k + 1), j, S * chunks.start:S * chunks.stop].rearrange("p (b s) -> p b s", s=S)
                    sp.dma_start(dst, row.partition_broadcast(I0)).then_inc(loaded, 16)

            def raw1(g, j):
                sp.dma_start(w_raw[:, j, :], scr_w1[g]).then_inc(FF_RAW[1][j], 16)

            def mask1(g, j):
                parts = pieces(P * g, min(P * (g + 1), I1 * (E1 + 1)))
                if len(parts) == 1:
                    e, i, n = parts[0]
                    parts = [(e, i, I0), (e, i, P - I0)]
                at_row = 0
                for e, i, n in parts:
                    row = scr_one if e < 0 else scr_mask[1][e]
                    sp.dma_start(mask[at_row:at_row + n, j, :], row.partition_broadcast(n)).then_inc(FF_MASK[1][j], 16)
                    at_row += n

            def store_masks0(b):
                sp.wait_ge(s_wt, b + 1)
                for q in range(P // 32):
                    dst = at(scr_mask[0], 2 * S * b + 32 * q, [[2 * TOK, 32], [P, 2 * TPB], [1, 32]])
                    sp.dma_start(dst, wT[0][32 * q:32 * (q + 1), b]).then_inc(s_mst[b], 16)

            def store_masks1():
                sp.wait_ge(s_wt, B + 1)
                for q in range(P // 32):
                    dst = at(scr_mask[1], 32 * q, [[TOK, E1], [P, TILES], [1, 32]])
                    sp.dma_start(dst, wT[1][32 * q:32 * q + E1]).then_inc(s_mst[B], 16)

            sp.wait_ge(s_one, 16)
            raw0(1, 1)
            sp.wait_ge(FF[0]["wlo"], 1)
            raw0(2, 0)
            sp.wait_ge(s_upd, B)
            for k in range(2):
                sp.dma_start(mask[I0 * k:I0 * (k + 1), 0, :], scr_one.partition_broadcast(I0)).then_inc(FF_MASK[0][0], 16)
            store_masks0(0)
            for b in range(B):
                if b + 1 < B:
                    store_masks0(b + 1)
                sp.wait_ge(s_mst[b], 16 * 4)
                mask0(1, 1, slice(b, b + 1), s_mask1[b])
            sp.wait_ge(FF[0]["act"], CHUNKS)
            mask0(2, 0, slice(0, B), FF_MASK[0][0])
            with sp.Fori(0, (GROUPS[0] - PEEL) // 2) as t:
                for jj in range(2):
                    g, j = 2 * t + PEEL + jj, 1 - jj
                    sp.wait_ge(FF[0]["wlo"], g - 1)
                    raw0(g, j)
                    sp.wait_ge(FF[0]["act"], CHUNKS * (g - 1))
                    mask0(g, j, slice(0, B), FF_MASK[0][j])
            for j in range(2):
                sp.wait_ge(s_pst[j], 16 * ((GROUPS[1] + 1 - j) // 2))
            sp.wait_ge(FF[0]["wlo"], GROUPS[0])
            raw1(0, 0)
            raw1(1, 1)
            sp.wait_ge(FF[1]["wlo"], 1)
            raw1(2, 0)
            sp.wait_ge(s_au, TILES)
            mask1(0, 0)
            mask1(1, 1)
            store_masks1()
            sp.wait_ge(s_mst[B], 16 * 4)
            for g in range(2, GROUPS[1]):
                j = g % 2
                if g >= 3:
                    sp.wait_ge(FF[1]["wlo"], g - 1)
                    raw1(g, j)
                sp.wait_ge(FF[1]["act"], CHUNKS * (g - 1))
                mask1(g, j)
            for b in range(B):
                sp.wait_ge(s_upd, 2 * B + b + 1)
                sp.dma_start(out_t[b], x_res[:, TPB * b:TPB * (b + 1), :]).then_inc(s_out, 16)
            sp.wait_ge(s_out, 16 * B)

        @block.gpsimd
        def _(pool):
            nc.gpsimd.memset(w_raw[:, 0, :], 0.0).then_inc(s_pool, 1)
            nc.gpsimd.memset(ones[:], 1.0).then_inc(s_pool, 1)
            pool.wait_ge(s_pool, 2)
            nc.gpsimd.affine_select(out=ident[:], in_=ones[:], compare_op=ALU.is_equal, fill=0.0, base=0,
                                    pattern=[[-1, P]], channel_multiplier=1).then_inc(s_pool, 1)
            nc.gpsimd.iota(iota_e[:], pattern=[[1, E1]], base=0, channel_multiplier=0,
                           allow_small_or_imprecise_dtypes=True).then_inc(s_pool, 1)
            nc.gpsimd.memset(v_ext[:], 1.0).then_inc(s_pool, 1)
            nc.gpsimd.memset(v_flat[:], 0.0).then_inc(s_pool, 1)
            nc.gpsimd.affine_select(out=headmask[:], in_=ones[:, 0:HEADS], compare_op=ALU.is_ge, fill=0.0, base=0,
                                    pattern=[[-HD, HEADS]], channel_multiplier=1).then_inc(s_pool, 1)
            pool.wait_ge(s_pool, 7)
            nc.gpsimd.affine_select(out=headmask[:], in_=headmask[:], compare_op=ALU.is_ge, fill=0.0, base=HD - 1,
                                    pattern=[[HD, HEADS]], channel_multiplier=-1).then_inc(s_pool, 1)
            nc.gpsimd.memset(dl, 0.0).then_inc(s_pool, 1)
            nc.gpsimd.iota(jrow[:], pattern=[[1, S]], base=0, channel_multiplier=0,
                           allow_small_or_imprecise_dtypes=True).then_inc(s_pool, 1)
            nc.gpsimd.memset(rst[:, 0, :], BIG).then_inc(s_pool, 1)
            nc.gpsimd.memset(ecol[:], S - 1.0).then_inc(s_pool, 1)
            pool.wait_ge(s_pool, 12)
            for b in range(B):
                nc.gpsimd.memset(rst[LANES[b]:LANES[b] + 1, 0, 0:1], 0.0).then_inc(s_pool, 1)

            pool.wait_ge(s_pool, POOL_CONST)
            def attention_prep():
                pool.wait_ge(s_khi, 1)
                nc.gpsimd.tensor_tensor(wq_lo[:], w4[:, 0, :], wq_hi[:].bitcast(F32), ALU.subtract).then_inc(s_wql, 1)
                nc.gpsimd.tensor_tensor(kT_lo[:], kT[:], kT_hi[:].bitcast(F32), ALU.subtract).then_inc(s_klo, 1)

            def normalise(k):
                for b in range(B):
                    pool.wait_ge(s_rstd, B * k + b + 1)
                    for t in range(TPB * b + ND, TPB * (b + 1)):
                        nc.gpsimd.tensor_scalar(xn[:, t, :], x_res[:, t, :], mv[:, t, 0:1], rstd[:, 3, t:t + 1],
                                                ALU.subtract, ALU.mult).then_inc(s_xnp, 1)

            normalise(0)
            def prep_store(g):
                pool.wait_ge(s_pout, g + 1)
                pool.dma_start(scr_w1[g], prep_out[:, g % 2, :]).then_inc(s_pst[g % 2], 16)

            for g in range(GROUPS[1]):
                j = g % 2
                if g >= 2:
                    pool.wait_ge(s_pt, g - 1)
                if P * (g + 1) > I1 * (E1 + 1):
                    nc.gpsimd.memset(prep_in[:, j, :], 0.0).then_inc(s_pzero, 1)
                    pool.wait_ge(s_pzero, 1)
                r0, r1 = P * g, min(P * (g + 1), I1 * (E1 + 1))
                for rows, m, src in prep_rows(r0, r1):
                    pool.dma_start(prep_in[rows, j, P * m:P * (m + 1)], src).then_inc(s_pin[j], 16)
                at_row = 0
                for e, i, n in pieces(r0, r1):
                    wd = swd1 if e < 0 else wd1[e]
                    pool.dma_start(prep_in[:, j, DOWN + at_row:DOWN + at_row + n], wd[:, i:i + n]).then_inc(s_pin[j], 16)
                    at_row += n
                if g == 1:
                    for b in range(B):
                        pool.wait_ge(s_root, b + 1)
                        nc.gpsimd.tensor_tensor(d2[0:KEYS, b, :], d2[0:KEYS, b, :], droot2[0:KEYS, b, :],
                                                ALU.subtract).then_inc(s_err, 1)
                    attention_prep()
                if g >= 1:
                    prep_store(g - 1)
            prep_store(GROUPS[1] - 1)

            def attention():
                pool.wait_ge(s_xlo, 2 * B + 1)
                nc.gpsimd.memset(expw[:, :, FLAT:], 0.0).then_inc(s_epad, 1)

                def tile(i, j):
                    if isinstance(i, int):
                        tok = slice(P * i, P * (i + 1))
                        pool.wait_ge(s_qlo, min(i // TPB + 1, CHUNKS))
                        if i >= 2:
                            pool.wait_ge(s_sc, 3 * (i - 1))
                    else:
                        tok = bass.ds(P * i, P)
                        pool.wait_ge(s_sc, 3 * i - 3)
                    nc.gpsimd.tensor_copy(qs_hi[:, j, :], qT_hi[:, tok].bitcast(F32))
                    nc.gpsimd.tensor_copy(qs_lo[:, j, :], qT_lo[:, tok].bitcast(F32)).then_inc(s_qs, 1)

                for i in range(TPB):
                    tile(i, i % 2)
                pool.wait_ge(s_qlo, CHUNKS)
                with pool.Fori(1, B) as t:
                    for q in range(TPB):
                        tile(TPB * t + q, q % 2)

            def route0(b):
                tiles = slice(TPB * b, TPB * (b + 1))
                pool.wait_ge(s_rcp, b + 1)
                nc.gpsimd.tensor_tensor(rest[0][:, tiles, :], aff[0][:, tiles, :], rest[0][:, tiles, :],
                                        ALU.subtract).then_inc(s_dif, 1)
                pool.wait_ge(s_dif, b + 1)
                for k in range(2):
                    ins = nc.gpsimd.tensor_tensor(wsel[0][:, b, TPB * k:TPB * (k + 1), :], rest[0][:, tiles, 32 * k:32 * (k + 1)],
                                                  rsum[:, 2, tiles].unsqueeze(2).broadcast_to([P, TPB, 32]), ALU.mult)
                ins.then_inc(s_sel, 1)

            def feed_forward(f):
                def unit(g, k):
                    u = CHUNKS * g + k
                    pool.wait_ge(FF[f]["ahi"], u + 1)
                    if not (isinstance(g, int) and u < 2):
                        pool.wait_ge(FF[f]["down"], u - 1)
                    nc.gpsimd.tensor_tensor(act_lo[:, k % 2, :], act_a[:, k % 2, :], act_hi[:, k % 2, :].bitcast(F32),
                                            ALU.subtract).then_inc(FF[f]["alo"], 1)

                for u in range(CHUNKS * PEEL):
                    if f == 0 and u == 0:
                        for b in range(B):
                            route0(b)
                    unit(u // CHUNKS, u % CHUNKS)
                with pool.Fori(0, LOOPS[f]) as t:
                    for u in range(BODY * CHUNKS):
                        unit(BODY * t + PEEL + u // CHUNKS, u % CHUNKS)
                for u in range(CHUNKS * (GROUPS[f] - REST), CHUNKS * GROUPS[f]):
                    unit(u // CHUNKS, u % CHUNKS)

            normalise(1)
            feed_forward(0)
            normalise(2)
            attention()
            normalise(3)
            feed_forward(1)

        @block.scalar
        def _(act):
            def context():
                act.wait_ge(s_ct, 1)
                nc.scalar.activation(ctxT[:], ps[6][:, 0:B * KEYS].rearrange("p (b k) -> p b k", b=B), ACT.Copy)
                nc.scalar.activation(ctxT_hi[:], ps[6][:, 0:B * KEYS].rearrange("p (b k) -> p b k", b=B),
                                     ACT.Copy, scale=-2.0).then_inc(s_cthi, 1)

            def root(k, b):
                act.wait_ge(s_bn, B * k + b + 1)
                tiles = slice(TPB * b, TPB * (b + 1))
                nc.scalar.activation(std[:, tiles], veps[:, tiles], ACT.Sqrt).then_inc(s_std, 1)

            def high(k, b):
                act.wait_ge(s_xt, B * k + b + 1)
                bank = turn_bank(k, b)
                if k == 0:
                    nc.scalar.activation(xn_hi[:, sl(b)], bank[:], ACT.Copy)
                    if b >= 2:
                        act.wait_ge(s_ab, b - 1)
                    nc.scalar.activation(sq[:, b % 2, :], bank[:], ACT.Square).then_inc(s_xhi, 1)
                else:
                    if k in (1, 3):
                        nc.scalar.activation(xT[:, sl(b)], bank[:], ACT.Copy).then_inc(s_xT, 1)
                    nc.scalar.activation(xn_hi[:, sl(b)], bank[:], ACT.Copy).then_inc(s_xhi, 1)

            def query(n):
                act.wait_ge(s_qp, n + 1)
                nc.scalar.activation(qT_hi[:, 512 * n:512 * (n + 1)], ps[2 + n % 2][:], ACT.Identity,
                                     bias=bias2[:, 0:1]).then_inc(s_qhi, 1)

            def norm(k):
                for b in range(B):
                    root(k, b)
                    if k == 0 and b == 0:
                        context()
                    if b >= 1:
                        high(k, b - 1)
                    if k == 2 and b >= 2:
                        query(b - 2)
                if k in (0, 2):
                    high(k, B - 1)
                if k == 2:
                    query(B - 2)
                    query(B - 1)

            norm(0)
            for b in range(B):
                act.wait_ge(s_d2, b + 1)
                nc.scalar.activation(droot[0:KEYS, b, :], d2[0:KEYS, b, :], ACT.Sqrt).then_inc(s_act, 1)
                act.wait_ge(s_act, b + 1)
                nc.scalar.activation(droot2[0:KEYS, b, :], droot[0:KEYS, b, :], ACT.Square).then_inc(s_root, 1)
            act.wait_ge(s_gate, 32)
            nc.scalar.activation(tgate[:], gates[:], ACT.Tanh)
            act.wait_ge(s_aw, 16 * 8)
            nc.scalar.activation(wq_hi[:], w4[:, 0, :], ACT.Copy)
            act.wait_ge(s_kp, 1)
            nc.scalar.activation(kT[:], ps[4][:, 0:B * KEYS], ACT.Identity, bias=bias2[:, 1:2])
            nc.scalar.activation(kT_hi[:], ps[4][:, 0:B * KEYS], ACT.Identity, bias=bias2[:, 1:2]).then_inc(s_khi, 1)
            act.wait_ge(s_vp, 1)
            act.wait_ge(s_pool, POOL_CONST)
            nc.scalar.activation(v_ext[:, :, :, 0:HD], ps[5][0:KEYS, :].rearrange("p (b h d) -> p b h d", b=B, d=HD),
                                 ACT.Copy).then_inc(s_vx, 1)
            act.wait_ge(s_khi, 1)
            for g in range(GROUPS[1]):
                act.wait_ge(s_pt, g + 1)
                if g >= 2:
                    act.wait_ge(s_pst[g % 2], 16 * (g // 2))
                nc.scalar.activation(prep_out[:, g % 2, :], ps[7][:, 0:WIDE], ACT.Copy).then_inc(s_pout, 1)
                if 2 <= g < 2 + HEADS:
                    h = g - 2
                    if h == 0:
                        act.wait_ge(s_klo, 1)
                    for k_all, k_head in ((kT_hi, kbd_hi), (kT_lo, kbd_lo)):
                        ins = nc.scalar.activation(k_head[:, :, h, :], k_all[:].bitcast(F32).rearrange("p (b k) -> p b k", b=B),
                                                   ACT.Copy, scale=headmask[:, h:h + 1])
                    ins.then_inc(s_kbd, 1)
            act.wait_ge(s_rt, 1)
            nc.scalar.activation(router[1][:], ps[6][:, 0:E1], ACT.Copy).then_inc(s_r1, 1)
            act.wait_ge(s_et, 1)
            nc.scalar.activation(erow[:], ps[6][0:KEYS, CHASE], ACT.Copy).then_inc(s_er, 1)
            nc.scalar.activation(erow_half[:], ps[6][0:KEYS, CHASE], ACT.Copy, bias=0.5).then_inc(s_erh, 1)
            act.wait_ge(s_erh, 1)
            for b in range(B):
                nc.scalar.activation(before[0:KEYS, b, :], jrow[0:KEYS, :], ACT.Sign, scale=-1.0,
                                     bias=erow_half[:, b:b + 1]).then_inc(s_before, 1)

            def scores0(b):
                act.wait_ge(s_logit, b + 1)
                nc.scalar.activation(aff[0][:, TPB * b:TPB * (b + 1), :], logit_bank(0, b), ACT.Sigmoid).then_inc(s_score, 1)

            def exp1(part):
                act.wait_ge(s_rsub, part + 1)
                nc.scalar.activation(rest[1][:, ROUTE1_TILES[part], :], rest[1][:, ROUTE1_TILES[part], :], ACT.Exp).then_inc(s_rexp, 1)

            def feed_forward(f):
                units = CHUNKS * GROUPS[f]

                def hi(u, j):
                    act.wait_ge(FF[f]["act"], u + 1)
                    if not (isinstance(u, int) and u < 2):
                        act.wait_ge(FF[f]["alo"], u - 1)
                        act.wait_ge(FF[f]["down"], u - 1)
                    nc.scalar.activation(act_hi[:, j, :], act_a[:, j, :], ACT.Copy).then_inc(FF[f]["ahi"], 1)

                def unit(g, k, j, load=None):
                    u = CHUNKS * g + k
                    if k == SPLIT_AT and load is not None:
                        act.wait_ge(FF[f]["down"], CHUNKS * g)
                        act.wait_ge(FF_RAW[f][1 - j], load)
                        nc.scalar.activation(w_hi[:, 1 - j, :], w_raw[:, 1 - j, :], ACT.Copy).then_inc(FF[f]["whi"], 1)
                    act.wait_ge(FF[f]["gate"], u + 1)
                    if not (isinstance(g, int) and u < 2):
                        act.wait_ge(FF[f]["t"], u - 1)
                    nc.scalar.activation(act_s[:, k % 2, :], ps[4 + k % 2][:], ACT.Silu).then_inc(FF[f]["silu"], 1)
                    if not (isinstance(g, int) and u < 1):
                        hi(u - 1, (k + 1) % 2)

                for g in range(PEEL):
                    for k in range(CHUNKS):
                        unit(g, k, g % 2, raw_loaded(f, g + 1) if g >= 1 else None)
                with act.Fori(0, LOOPS[f]) as t:
                    for i in range(BODY):
                        for k in range(CHUNKS):
                            unit(BODY * t + PEEL + i, k, (PEEL + i) % 2, raw_loaded(f, PEEL + i + 1) + raw_loaded(f, 0) * (BODY // 2) * t)
                for g in range(GROUPS[f] - REST, GROUPS[f]):
                    for k in range(CHUNKS):
                        unit(g, k, g % 2, raw_loaded(f, g + 1) if g + 1 < GROUPS[f] else None)
                hi(units - 1, 1)
                for n in range(CHUNKS):
                    act.wait_ge(FF[f]["sum"], n + 1)
                    nc.scalar.activation(yT[:, n, :], ps[n][:], ACT.Copy).then_inc(FF[f]["yT"], 1)

            def split_first(f):
                for g in range(2):
                    act.wait_ge(FF_RAW[f][g], 16 * RAW_DMAS[f])
                    nc.scalar.activation(w_hi[:, g, :], w_raw[:, g, :], ACT.Copy).then_inc(FF[f]["whi"], 1)

            def attention():
                def copy_av(i):
                    act.wait_ge(s_avt, i + 1)
                    nc.scalar.activation(avT, ps[6][:, 0:P], ACT.Copy).then_inc(s_avc, 1)

                def copy_exp(i, j):
                    if not (isinstance(i, int) and i < 2):
                        act.wait_ge(s_av, i - 1)
                    for r in range(RT):
                        act.wait_ge(s_tr, RT * i + r + 1)
                        n = min(HT, FT - HT * r)
                        nc.scalar.activation(expT[:, j, P * HT * r:P * (HT * r + n)],
                                             ps[EXP_BANKS[r]][:, 0:P * n], ACT.Copy).then_inc(s_ev, 1)

                def exp(i, j):
                    act.wait_ge(s_sub, 3 * i + 3)
                    nc.scalar.activation(expw[:, j, 0:FLAT], expw[:, j, 0:FLAT], ACT.Exp, scale=float(HD) ** -0.5).then_inc(s_exp, 1)

                def step(i, j):
                    first = isinstance(i, int)
                    if not (first and i < 3):
                        copy_av(i - 3)
                    if not (first and i < 1):
                        copy_exp(i - 1, 1 - j)
                    exp(i, j)

                for i in range(TPB):
                    step(i, i % 2)
                with act.Fori(1, B) as t:
                    for q in range(TPB):
                        step(TPB * t + q, q % 2)
                copy_av(TILES - 3)
                copy_exp(TILES - 1, 1)
                for b in range(B - 1):
                    root(3, b)
                copy_av(TILES - 2)
                high(3, 0)
                copy_av(TILES - 1)
                high(3, 1)
                root(3, B - 1)
                high(3, 2)

            split_first(0)
            norm(1)
            scores0(0)
            scores0(1)
            high(1, B - 1)
            scores0(2)
            scores0(3)
            feed_forward(0)
            norm(2)
            split_first(1)
            attention()
            exp1(0)
            high(3, B - 1)
            exp1(1)
            feed_forward(1)

        @block.tensor
        def _(pe):
            pe.wait_ge(s_ctx, 16)
            pe.wait_ge(s_pool, 3)
            for b in range(B):
                mm = nc.tensor.transpose(ps[6][:, KEYS * b:KEYS * (b + 1)], ctx_sb[:, b, :], ident[0:KEYS, 0:KEYS])
            mm.then_inc(s_ct, 1)

            def turn(k, b):
                if b >= 2 and k < 3:
                    pe.wait_ge(s_xhi if k == 1 else s_xlo, B * k + b - 1)
                for q in range(TPB):
                    t = TPB * b + q
                    if q < ND:
                        pe.wait_ge(s_xn, (B * k + b) * ND + q + 1)
                    else:
                        pe.wait_ge(s_xnp, (B * k + b) * (TPB - ND) + q - ND + 1)
                    mm = nc.tensor.transpose(turn_bank(k, b)[:, P * q:P * (q + 1)], xn[:, t, :], ident[:])
                mm.then_inc(s_xt, 1)

            def norm(k, after=None):
                for b in range(B):
                    turn(k, b)
                    if after is not None and b >= 1:
                        after(b - 1)
                if after is not None:
                    after(B - 1)

            def distances(b):
                pe.wait_ge(s_xhi, b + 1)
                if b >= 2:
                    pe.wait_ge(s_d2, b - 1)
                d = ps[2 + b % 2][0:KEYS, :]
                nc.tensor.matmul(d, ones[:, 0:KEYS], sq[:, b % 2, :], start=True, stop=False)
                pe.wait_ge(s_ctlo, 1)
                pe.wait_ge(s_xlo, b + 1)
                nc.tensor.matmul(d, ctxT_hi[:, b, :], xn_hi[:, sl(b)], start=False, stop=False)
                nc.tensor.matmul(d, ctxT_lo[:, b, :], xn_hi[:, sl(b)], start=False, stop=False)
                nc.tensor.matmul(d, ctxT_hi[:, b, :], xn_lo[:, sl(b)], start=False, stop=True).then_inc(s_ab, 1)

            norm(0, distances)
            pe.wait_ge(s_aw, 16 * 8)
            nc.tensor.matmul(ps[4][:, 0:B * KEYS], w4[:, 1, :], ctxT[:].rearrange("p b k -> p (b k)"),
                             start=True, stop=True).then_inc(s_kp, 1)
            for b in range(B):
                out_b = ps[5][0:KEYS, P * b:P * (b + 1)]
                nc.tensor.matmul(out_b, ctxT[:, b, :], w4[:, 2, :], start=True, stop=False)
                mm = nc.tensor.matmul(out_b, ones[0:1, 0:KEYS], brow2[:, 0, :], start=False, stop=True)
            mm.then_inc(s_vp, 1)
            loads = [0, 0]
            for g in range(GROUPS[1]):
                j = g % 2
                r0, r1 = P * g, min(P * (g + 1), I1 * (E1 + 1))
                loads[j] += 16 * (len(prep_rows(r0, r1)) + len(pieces(r0, r1)))
                pe.wait_ge(s_pin[j], loads[j])
                if g >= 1:
                    pe.wait_ge(s_pout, g)
                for m in range(3):
                    mm = nc.tensor.transpose(ps[7][:, P * m:P * (m + 1)], prep_in[:, j, P * m:P * (m + 1)], ident[:])
                mm.then_inc(s_pt, 1)
            pe.wait_ge(s_rw[1], 16)
            pe.wait_ge(s_ctlo, 1)
            nc.tensor.transpose(ps[6][:, 0:E1], router1_rows[:], ident[0:E1, 0:E1]).then_inc(s_rt, 1)
            pe.wait_ge(s_chase, KEYS - 1)
            pe.wait_ge(s_r1, 1)
            nc.tensor.transpose(ps[6][0:KEYS, 0:P], ecol[:], ident[:]).then_inc(s_et, 1)
            pe.wait_ge(s_vx, 1)
            pe.wait_ge(s_er, 1)
            for b in range(B):
                pe.wait_ge(s_path, b + 1)
                for q in range(TPB):
                    mm = nc.tensor.matmul(ps[4 + b][:, P * q:P * (q + 1)], pmask[0:KEYS, b, P * q:P * (q + 1)],
                                          ctx_sb[:, b, :], start=True, stop=True)
                mm.then_inc(s_xa, 1)

            def three_pass(out, w_h, w_l, x_h, x_l, start=True, stop=True):
                nc.tensor.matmul(out, w_h, x_h, start=start, stop=False)
                nc.tensor.matmul(out, w_l, x_h, start=False, stop=False)
                return nc.tensor.matmul(out, w_h, x_l, start=False, stop=stop)

            def query(n):
                pe.wait_ge(s_wql, 1)
                pe.wait_ge(s_xlo, 2 * B + n + 1)
                if n >= 2:
                    pe.wait_ge(s_qlo, n - 1)
                tok = slice(512 * n, 512 * (n + 1))
                three_pass(ps[2 + n % 2][:], wq_hi[:], wq_lo[:], xn_hi[:, tok], xn_lo[:, tok]).then_inc(s_qp, 1)

            def attention():
                pe.wait_ge(s_kbd, HEADS)
                pe.wait_ge(s_vf, 16 * sum(LAST_HEAD[c] + 1 - FIRST_HEAD[c] for c in range(FT)))
                pe.wait_ge(s_epad, 1)
                pe.wait_ge(s_qlo, CHUNKS)

                def scores(i, b, j, r):
                    h0, h1 = HSPLIT[r]
                    if r == 0:
                        pe.wait_ge(s_qs, i + 1)
                    if not (isinstance(i, int) and i == 0):
                        pe.wait_ge(s_sub, 3 * i - 2 + r)
                    if isinstance(b, int):
                        k_hi, k_lo = kbd_hi[:, b, h0:h1, :], kbd_lo[:, b, h0:h1, :]
                    else:
                        k_hi, k_lo = [k[:].rearrange("p b h k -> p (b h k)")[:, bass.ds(b * (HEADS * KEYS) + h0 * KEYS, (h1 - h0) * KEYS)]
                                      for k in (kbd_hi, kbd_lo)]
                    three_pass(ps[r][:, 0:(h1 - h0) * KEYS], qs_hi[:, j, :], qs_lo[:, j, :], k_hi, k_lo).then_inc(s_sc, 1)

                def exp_back(i, j):
                    pe.wait_ge(s_exp, i + 1)
                    for r in range(RT):
                        if not (isinstance(i, int) and i == 0):
                            pe.wait_ge(s_ev, RT * i + r - RT + 1)
                        for c in range(HT * r, min(HT * (r + 1), FT)):
                            mm = nc.tensor.transpose(ps[EXP_BANKS[r]][:, P * (c % HT):P * (c % HT + 1)],
                                                     expw[:, j, P * c:P * (c + 1)], ident[:])
                        mm.then_inc(s_tr, 1)

                def values(i, b, j, r):
                    total = ps[5][:, 0:HEADS * (HD + 1)]
                    if r == 0:
                        if not (isinstance(i, int) and i == 0):
                            pe.wait_ge(s_nrm, i)
                        nc.tensor.matmul(total, zeros[0:1, 0:P], zeros[0:1, 0:HEADS * (HD + 1)], start=True, stop=False)
                    pe.wait_ge(s_ev, RT * i + r + 1)
                    for c in range(HT * r, min(HT * (r + 1), FT)):
                        h0, cols = FIRST_HEAD[c], (HD + 1) * (LAST_HEAD[c] + 1 - FIRST_HEAD[c])
                        if isinstance(b, int):
                            v = v_flat[:, b, c, 0:cols]
                        else:
                            v = v_flat[:].rearrange("p b c d -> p (b c d)")[:, bass.ds(b * (FT * FH * (HD + 1)) + c * (FH * (HD + 1)), cols)]
                        nc.tensor.matmul(ps[5][:, (HD + 1) * h0:(HD + 1) * h0 + cols], expT[:, j, P * c:P * (c + 1)], v,
                                         start=False, stop=False)
                    if r == RT - 1:
                        nc.tensor.matmul(total, zeros[0:1, 0:P], zeros[0:1, 0:HEADS * (HD + 1)], start=False, stop=True).then_inc(s_av, 1)

                def av_back(i, j):
                    pe.wait_ge(s_nrm, i + 1)
                    if not (isinstance(i, int) and i == 0):
                        pe.wait_ge(s_au, i)
                    nc.tensor.transpose(ps[6][:, 0:P], av[:, j, :], ident[:]).then_inc(s_avt, 1)

                def project(i):
                    pe.wait_ge(s_avc, i + 1)
                    nc.tensor.matmul(ps[6][:, P:2 * P], avT, w4[:, 3, :], start=True, stop=False)
                    nc.tensor.matmul(ps[6][:, P:2 * P], ones[0:1, :], brow2[:, 1, :], start=False, stop=True).then_inc(s_wo, 1)

                def step(i, b, b_values, j):
                    first = isinstance(i, int)
                    for r in range(RT):
                        if not (first and i >= TILES):
                            scores(i, b, j, r)
                        if r == 0 and not (first and i < 3):
                            av_back(i - 3, 1 - j)
                        if not (first and i < 2):
                            values(i - 2, b_values, j, r)
                        if r == 1 and not (first and i < 3):
                            project(i - 3)
                    if not (first and (i < 1 or i > TILES)):
                        exp_back(i - 1, 1 - j)

                for i in range(TPB):
                    step(i, 0, 0, i % 2)
                with pe.Fori(1, B) as t:
                    for q in range(TPB):
                        step(TPB * t + q, t, t - 1 if q < 2 else t, q % 2)
                step(TILES, None, B - 1, 0)
                step(TILES + 1, None, B - 1, 1)
                turn(3, 0)
                av_back(TILES - 1, 1)
                project(TILES - 1)
                turn(3, 1)
                turn(3, 2)

            def logits(f, b):
                pe.wait_ge(s_xT, B * f + b + 1)
                if f == 0 and b >= 2:
                    pe.wait_ge(s_score, b - 1)
                for q in range(TPB):
                    tok = slice(S * b + P * q, S * b + P * (q + 1))
                    mm = nc.tensor.matmul(logit_bank(f, b)[:, q, :], xT[:, tok], router[f][:], start=True, stop=True)
                mm.then_inc(s_logit, 1)

            def feed_forward(f):
                units = CHUNKS * GROUPS[f]

                def gate_up(g, k, j):
                    u = CHUNKS * g + k
                    if k == 0:
                        pe.wait_ge(FF[f]["wlo"], g + 1)
                    if not (isinstance(g, int) and u < 2):
                        pe.wait_ge(FF[f]["silu"], u - 1)
                        pe.wait_ge(FF[f]["t"], u - 1)
                    tok = slice(512 * k, 512 * (k + 1))
                    three_pass(ps[4 + k % 2][:], w_hi[:, j, 0:P], w_lo[:, j, 0:P],
                               xn_hi[:, tok], xn_lo[:, tok]).then_inc(FF[f]["gate"], 1)
                    three_pass(ps[6 + k % 2][:], w_hi[:, j, UP:UP + P], w_lo[:, j, UP:UP + P],
                               xn_hi[:, tok], xn_lo[:, tok]).then_inc(FF[f]["up"], 1)

                def down(u, n, j):
                    i = n % 2
                    pe.wait_ge(FF[f]["ahi"], u + 1)
                    nc.tensor.matmul(ps[n][:], w_hi[:, j, DOWN:DOWN + P], act_hi[:, i, :], start=False, stop=False)
                    nc.tensor.matmul(ps[n][:], w_lo[:, j, DOWN:DOWN + P], act_hi[:, i, :], start=False, stop=False)
                    pe.wait_ge(FF[f]["alo"], u + 1)
                    nc.tensor.matmul(ps[n][:], w_hi[:, j, DOWN:DOWN + P], act_lo[:, i, :],
                                     start=False, stop=False).then_inc(FF[f]["down"], 1)

                if f == 0:
                    pe.wait_ge(s_rw[0], 16)
                    turn(1, 0)
                    turn(1, 1)
                    logits(0, 0)
                    turn(1, 2)
                    logits(0, 1)
                    turn(1, 3)
                    logits(0, 2)
                else:
                    pe.wait_ge(s_r1, 1)
                    for b in range(B - 1):
                        logits(1, b)
                    turn(3, B - 1)
                logits(f, B - 1)
                for k in range(2):
                    pe.wait_ge(s_xlo, B * (2 * f + 1) + k + 1)
                    gate_up(0, k, 0)
                pe.wait_ge(s_xhi, B * (2 * f + 2))
                if f == 0:
                    pe.wait_ge(s_score, B)
                else:
                    pe.wait_ge(s_rsub, 2)
                for n in range(CHUNKS):
                    nc.tensor.matmul(ps[n][:], zeros[0:1, 0:P], zeros[0:1, :], start=True, stop=False)
                for u in range(2, CHUNKS * PEEL):
                    gate_up(u // CHUNKS, u % CHUNKS, u // CHUNKS % 2)
                    down(u - 2, (u - 2) % CHUNKS, (u - 2) // CHUNKS % 2)
                with pe.Fori(0, LOOPS[f]) as t:
                    for i in range(BODY):
                        g, j = BODY * t + PEEL + i, (PEEL + i) % 2
                        for k in range(CHUNKS):
                            gate_up(g, k, j)
                            down(CHUNKS * g + k - 2, (k + 2) % CHUNKS, j if k >= 2 else 1 - j)
                for u in range(CHUNKS * (GROUPS[f] - REST), units):
                    gate_up(u // CHUNKS, u % CHUNKS, u // CHUNKS % 2)
                    down(u - 2, (u - 2) % CHUNKS, (u - 2) // CHUNKS % 2)

                def close(n):
                    nc.tensor.matmul(ps[n][:], zeros[0:1, 0:P], zeros[0:1, :], start=False, stop=True).then_inc(FF[f]["sum"], 1)

                def back(n):
                    if n == 0:
                        pe.wait_ge(FF[f]["silu"], units)
                    if n == 2:
                        pe.wait_ge(FF[f]["t"], units)
                    pe.wait_ge(FF[f]["yT"], n + 1)
                    for q in range(4):
                        mm = nc.tensor.transpose(ps[4 + n][:, P * q:P * (q + 1)], yT[:, n, P * q:P * (q + 1)], ident[:])
                    mm.then_inc(FF[f]["back"], 1)

                close(0)
                close(1)
                down(units - 2, 2, 0)
                close(2)
                back(0)
                down(units - 1, 3, 0)
                close(3)
                for n in range(1, CHUNKS):
                    back(n)

            feed_forward(0)
            norm(2, query)
            attention()
            feed_forward(1)

        @block.vector
        def _(dve):
            steps = [0]

            def done(ins):
                steps[0] += 1
                ins.then_inc(s_dve, 1)
                return steps[0]

            def after(step):
                dve.wait_ge(s_dve, step)

            def settle(but=0):
                dve.wait_ge(s_dve, steps[0] - but)

            def rsqrt(k, b, tiles):
                dve.wait_ge(s_std, B * k + b + 1)
                done(nc.vector.reciprocal(rstd[:, 0, tiles], std[:, tiles]))
                settle()
                done(nc.vector.tensor_tensor(rstd[:, 1, tiles], rstd[:, 0, tiles], rstd[:, 0, tiles], ALU.mult))
                settle()
                done(nc.vector.scalar_tensor_tensor(rstd[:, 2, tiles], rstd[:, 1, tiles], -0.5, veps[:, tiles],
                                                    ALU.mult, ALU.mult))
                settle()
                nc.vector.scalar_tensor_tensor(rstd[:, 3, tiles], rstd[:, 2, tiles], 1.5, rstd[:, 0, tiles],
                                               ALU.add, ALU.mult).then_inc(s_rstd, 1)

            def normalise(k, b):
                dve.wait_ge(s_rstd, B * k + b + 1)
                for t in range(TPB * b, TPB * b + ND):
                    nc.vector.tensor_scalar(xn[:, t, :], x_res[:, t, :], mv[:, t, 0:1], rstd[:, 3, t:t + 1],
                                            ALU.subtract, ALU.mult).then_inc(s_xn, 1)

            def low(k, b):
                dve.wait_ge(s_xhi, B * k + b + 1)
                x_all = xT[:, sl(b)] if k in (1, 3) else turn_bank(k, b)[:]
                nc.vector.tensor_tensor(xn_lo[:, sl(b)], x_all, xn_hi[:, sl(b)].bitcast(F32),
                                        ALU.subtract).then_inc(s_xlo, 1)

            def update(n, col):
                xb = x_res[:, TPB * n:TPB * (n + 1), :].rearrange("p q h -> p (q h)")
                nc.vector.scalar_tensor_tensor(xb, ps[4 + n][:], tgate[:, col:col + 1], xb, ALU.mult, ALU.add).then_inc(s_upd, 1)

            def query(n):
                dve.wait_ge(s_qhi, n + 1)
                tok = slice(512 * n, 512 * (n + 1))
                nc.vector.scalar_tensor_tensor(qT_lo[:, tok], ps[2 + n % 2][:], bias2[:, 0:1], qT_hi[:, tok].bitcast(F32),
                                               ALU.add, ALU.subtract).then_inc(s_qlo, 1)

            def norm(k, ready):
                for b in range(B + 1):
                    p = b - 1
                    new, old = slice(TPB * b, TPB * (b + 1)), slice(TPB * p, TPB * (p + 1))
                    if b < B:
                        ready(b)
                    if p >= 0:
                        dve.wait_ge(s_std, B * k + p + 1)
                        r0 = done(nc.vector.reciprocal(rstd[:, 0, old], std[:, old]))
                    if b < B:
                        if k in (1, 2):
                            dve.wait_ge(s_upd, B * (k - 1) + b + 1)
                        for t in range(TPB * b, TPB * b + 2):
                            st = done(nc.vector.bn_stats(stat[:, t, :], x_res[:, t, :]))
                    if p >= 0:
                        after(r0)
                        r1 = done(nc.vector.tensor_tensor(rstd[:, 1, old], rstd[:, 0, old], rstd[:, 0, old], ALU.mult))
                    if b < B:
                        for t in range(TPB * b + 2, TPB * (b + 1)):
                            st = done(nc.vector.bn_stats(stat[:, t, :], x_res[:, t, :]))
                    if p >= 0:
                        after(r1)
                        r2 = done(nc.vector.scalar_tensor_tensor(rstd[:, 2, old], rstd[:, 1, old], -0.5, veps[:, old],
                                                                 ALU.mult, ALU.mult))
                    if b < B:
                        after(st)
                        for t in range(TILES)[new]:
                            ag = done(nc.vector.bn_aggr(mv[:, t, :], stat[:, t, :]))
                    if p >= 0:
                        after(r2)
                        nc.vector.scalar_tensor_tensor(rstd[:, 3, old], rstd[:, 2, old], 1.5, rstd[:, 0, old],
                                                       ALU.add, ALU.mult).then_inc(s_rstd, 1)
                    if b < B:
                        after(ag)
                        nc.vector.tensor_scalar(veps[:, new], mv[:, new, 1], LN_EPS, None, ALU.add).then_inc(s_bn, 1)
                    if p >= 1:
                        low(k, p - 1)
                    if p >= 0:
                        normalise(k, p)
                    if k == 2 and p >= 2:
                        query(p - 2)
                low(k, B - 1)
                if k == 2:
                    query(B - 2)
                    query(B - 1)

            def context():
                dve.wait_ge(s_ctx, 16)
                sq_step = done(nc.vector.tensor_tensor(aasq[:], ctx_sb[:], ctx_sb[:], ALU.mult))
                dve.wait_ge(s_cthi, 1)
                nc.vector.scalar_tensor_tensor(ctxT_lo[:], ps[6][:, 0:B * KEYS].rearrange("p (b k) -> p b k", b=B), -2.0,
                                               ctxT_hi[:].bitcast(F32), ALU.mult, ALU.subtract).then_inc(s_ctlo, 1)
                after(sq_step)
                done(nc.vector.tensor_reduce(aa[:], aasq[:], AX_X, ALU.add))

            def loaded(b):
                if b == 1:
                    context()
                dve.wait_ge(s_x[b], 16)

            norm(0, loaded)
            settle()

            def squared(b):
                dve.wait_ge(s_ab, b + 1)
                nc.vector.tensor_scalar(d2[0:KEYS, b, :], ps[2 + b % 2][0:KEYS, :], aa[:, b:b + 1], TINY,
                                        ALU.add, ALU.max).then_inc(s_d2, 1)

            def corrected(b):
                dve.wait_ge(s_root, b + 1)
                done(nc.vector.tensor_scalar(dinv[0:KEYS, b, :].bitcast(I32), droot[0:KEYS, b, :].bitcast(I32), -1, HALF_OVER,
                                             ALU.mult, ALU.add))
                settle()
                dve.wait_ge(s_err, b + 1)
                done(nc.vector.tensor_tensor(d2[0:KEYS, b, :], d2[0:KEYS, b, :], dinv[0:KEYS, b, :], ALU.mult))
                settle()
                nc.vector.tensor_tensor(drows[0:KEYS, b, :], d2[0:KEYS, b, :], droot[0:KEYS, b, :], ALU.add).then_inc(s_dist, 1)

            squared(0)
            for b in range(1, B):
                squared(b)
                corrected(b - 1)
            corrected(B - 1)

            for b in range(B):
                dve.wait_ge(s_dld[b], 16)
            dve.wait_ge(s_pool, POOL_CONST)
            shift = [31] + list(range(CH - 1)) + [31] * (32 - CH)

            def left_steps(s):
                nc.vector.tensor_tensor(lg[:, s, 0, :], rst[:, s + 1, 0:CW], mst[:, s % MST, :], ALU.is_lt).then_inc(s_steps, 1)

            for s in range(SLOTS):
                if s >= 1:
                    dve.wait_ge(s_scan, s)
                prev, cur = rst[:, s, :], rst[:, s + 1, :]
                if s >= MST:
                    dve.wait_ge(s_steps, s - MST + 1)
                nc.vector.tensor_tensor(mst[:, s % MST, :], prev[:, 1:CW + 1], prev[:, 0:CW], ALU.min)
                nc.vector.stream_shuffle(cur[:, 0:1], prev[:, CW:CW + 1], shift).then_inc(s_halo, 1)
                nc.vector.tensor_tensor(lg[:, s, 1, :], prev[:, 0:CW], prev[:, 1:CW + 1], ALU.is_le)
                dve.wait_ge(s_halo, s + 1)
                nc.vector.tensor_tensor_scan(cur[:, 1:CW + 1], mst[:, s % MST, :], dl[:, s, :], cur[:, 0:1],
                                             ALU.min, ALU.add).then_inc(s_scan, 1)
                if s >= 1:
                    left_steps(s - 1)
            dve.wait_ge(s_scan, SLOTS)
            left_steps(SLOTS - 1)

            done(nc.vector.memset(srow[0:KEYS, :, S:S + 1], 2.0 * S))
            for b in range(B):
                dve.wait_ge(s_lgld[b], 32)
                jr = jrow[0:KEYS, :]
                left, diag = lgr[0:KEYS, 0, b, :], lgr[0:KEYS, 1, b, :]
                done(nc.vector.scalar_tensor_tensor(nlj[0:KEYS, b, :], left, 1.0, jr, ALU.is_lt, ALU.mult))
                done(nc.vector.tensor_tensor(nup[0:KEYS, b, :], left, diag, ALU.max))
                settle()
                done(nc.vector.tensor_tensor_scan(srow[0:KEYS, b, 0:S][:, ::-1],
                                                  left[:, ::-1], nlj[0:KEYS, b, :][:, ::-1], 2.0 * S, ALU.mult, ALU.add))
                done(nc.vector.scalar_tensor_tensor(ubig[0:KEYS, b, :], nup[0:KEYS, b, :], 2.0 * S, jr, ALU.mult, ALU.add))
                settle()
                nc.vector.tensor_tensor(trow[0:KEYS, b, :], ubig[0:KEYS, b, :], srow[0:KEYS, b, 1:S + 1],
                                        ALU.min).then_inc(s_trow, 1)

            for b in range(B):
                dve.wait_ge(s_tch[b], 16)
            for i in range(KEYS - 1, 0, -1):
                if i < KEYS - 1:
                    dve.wait_ge(s_chase, KEYS - 1 - i)
                nc.vector.tensor_scalar(junk[CHASE, 1:S], chase[:, i, 1:S], ecol[CHASE, i:i + 1], 0.0, ALU.is_le, ALU.add,
                                        accum_out=ecol[CHASE, i - 1:i]).then_inc(s_chase, 1)

            dve.wait_ge(s_pool, POOL_CONST)
            nc.vector.tensor_scalar(zeros[:], jrow[0:1, :], 0.0, None, ALU.mult)

            dve.wait_ge(s_er, 1)
            for b in range(B):
                dve.wait_ge(s_before, b + 1)
                nc.vector.scalar_tensor_tensor(pmask[0:KEYS, b, :], srow[0:KEYS, b, 1:S + 1], erow[:, b:b + 1],
                                               before[0:KEYS, b, :], ALU.is_gt, ALU.is_equal).then_inc(s_path, 1)

            def add_aligned(b):
                dve.wait_ge(s_xa, b + 1)
                update(b, 0)

            def add_ffn(f):
                def add(n):
                    dve.wait_ge(FF[f]["back"], n + 1)
                    update(n, 2 + f)
                return add

            def first_lo(f):
                for g in range(2):
                    dve.wait_ge(FF[f]["whi"], g + 1)
                    nc.vector.tensor_tensor(w_lo[:, g, :], w_raw[:, g, :], w_hi[:, g, :].bitcast(F32),
                                            ALU.subtract).then_inc(FF[f]["wlo"], 1)

            def route0(b):
                tiles = slice(TPB * b, TPB * (b + 1))
                dve.wait_ge(s_score, b + 1)
                for t in range(TILES)[tiles]:
                    best = done(nc.vector.max(top8[:, t, :], aff[0][:, t, :]))
                after(best)
                total = done(nc.vector.tensor_reduce(rsum[:, 0, tiles], top8[:, tiles, :], AX_X, ALU.add))
                for t in range(TILES)[tiles]:
                    done(nc.vector.match_replace(rest[0][:, t, :], top8[:, t, :], aff[0][:, t, :], 0.0))
                after(total)
                total = done(nc.vector.tensor_scalar(rsum[:, 1, tiles], rsum[:, 0, tiles], 1e-9, None, ALU.add))
                after(total)
                nc.vector.reciprocal(rsum[:, 2, tiles], rsum[:, 1, tiles]).then_inc(s_rcp, 1)

            def turn0(b):
                dve.wait_ge(s_sel, b + 1)
                nc.vector.transpose(wT[0][:, b].rearrange("p t c -> p (t c)"),
                                    wsel[0][:, b].rearrange("p t c -> p (t c)")).then_inc(s_wt, 1)

            def route1(part, step):
                E = E1
                tiles = ROUTE1_TILES[part]
                n = tiles.stop - tiles.start
                sc, ex = aff[1][:, tiles, :], rest[1][:, tiles, :]
                hits = [h[:, tiles, :] for h in hit]

                def by_tile(col):
                    return rsum[:, col, tiles].unsqueeze(2).broadcast_to([P, n, E])

                if step == 0:
                    dve.wait_ge(s_logit, B + -(-tiles.stop // TPB))
                    lo = ps[part][:, 0:E * n].rearrange("p (t e) -> p t e", e=E)
                    most = done(nc.vector.tensor_reduce(rsum[:, 0, tiles], lo, AX_X, ALU.max))
                    after(most)
                    nc.vector.tensor_tensor(ex, lo, by_tile(0), ALU.subtract).then_inc(s_rsub, 1)
                if step == 1:
                    dve.wait_ge(s_rexp, part + 1)
                    done(nc.vector.tensor_reduce(rsum[:, 1, tiles], ex, AX_X, ALU.add))
                    settle()
                    done(nc.vector.reciprocal(rsum[:, 2, tiles], rsum[:, 1, tiles]))
                    settle()
                    done(nc.vector.tensor_tensor(sc, ex, by_tile(2), ALU.mult))
                if step == 2:
                    settle()
                    for t in range(TILES)[tiles]:
                        done(nc.vector.max(top8[:, t, :], aff[1][:, t, :]))
                if step == 3:
                    settle()
                    for t in range(TILES)[tiles]:
                        done(nc.vector.max_index(topi[:, t, :], top8[:, t, :], aff[1][:, t, :]))
                    done(nc.vector.tensor_tensor(rsum[:, 0, tiles], top8[:, tiles, 0], top8[:, tiles, 1], ALU.add))
                    settle()
                    done(nc.vector.tensor_scalar(rsum[:, 1, tiles], rsum[:, 0, tiles], 1e-20, None, ALU.add))
                    done(nc.vector.tensor_copy(topf[:, tiles, :], topi[:, tiles, :]))
                    settle()
                    done(nc.vector.reciprocal(rsum[:, 2, tiles], rsum[:, 1, tiles]))
                if step == 4:
                    settle()
                    for c in range(2):
                        done(nc.vector.tensor_tensor(hits[c], iota_e[:].unsqueeze(1).broadcast_to([P, n, E]),
                                                     topf[:, tiles, c:c + 1].broadcast_to([P, n, E]), ALU.is_equal))
                    done(nc.vector.tensor_tensor(ex, sc, by_tile(2), ALU.mult))
                    settle()
                    done(nc.vector.tensor_tensor(hits[0], hits[0], hits[1], ALU.add))
                    settle()
                    done(nc.vector.tensor_tensor(wsel[1][:, tiles, 0:E], ex, hits[0], ALU.mult))
                if step == 5:
                    settle()
                    nc.vector.transpose(wT[1].rearrange("p t e -> p (t e)"),
                                        wsel[1].rearrange("p t e -> p (t e)")).then_inc(s_wt, 1)

            def attention():
                first_lo(1)

                def shift_scores(i, j, between):
                    for r, (h0, h1) in enumerate(HSPLIT):
                        dve.wait_ge(s_sc, 3 * i + r + 1)
                        sc = ps[r][:, 0:(h1 - h0) * KEYS].rearrange("p (h k) -> p h k", k=KEYS)
                        nc.vector.tensor_reduce(smax[:, j, h0:h1], sc, AX_X, ALU.max).then_inc(s_mx, 1)
                    if not (isinstance(i, int) and i < 2):
                        dve.wait_ge(s_tr, RT * (i - 1))
                    for r, (h0, h1) in enumerate(HSPLIT):
                        dve.wait_ge(s_mx, 3 * i + r + 1)
                        sc = ps[r][:, 0:(h1 - h0) * KEYS].rearrange("p (h k) -> p h k", k=KEYS)
                        to = expw[:, j, h0 * KEYS:h1 * KEYS].rearrange("p (h k) -> p h k", k=KEYS)
                        nc.vector.tensor_tensor(to, sc, smax[:, j, h0:h1].unsqueeze(2).broadcast_to([P, h1 - h0, KEYS]),
                                                ALU.subtract).then_inc(s_sub, 1)
                        if r == 0:
                            between()

                def normalise_heads(i, j):
                    dve.wait_ge(s_av, i + 1)
                    o = ps[5][:, 0:HEADS * (HD + 1)].rearrange("p (h d) -> p h d", d=HD + 1)
                    nc.vector.reciprocal(rden[:, j, :], o[:, :, HD]).then_inc(s_rd, 1)
                    dve.wait_ge(s_rd, i + 1)
                    if not (isinstance(i, int) and i < 2):
                        dve.wait_ge(s_avt, i - 1)
                    nc.vector.tensor_tensor(av[:, j, :].rearrange("p (h d) -> p h d", d=HD), o[:, :, 0:HD],
                                            rden[:, j, :].unsqueeze(2).broadcast_to([P, HEADS, HD]), ALU.mult).then_inc(s_nrm, 1)

                def add_tile(i):
                    dve.wait_ge(s_wo, i + 1)
                    xi = x_res[:, i, :] if isinstance(i, int) else x_res[:].rearrange("p t h -> p (t h)")[:, bass.ds(P * i, P)]
                    nc.vector.scalar_tensor_tensor(xi, ps[6][:, P:2 * P], tgate[:, 1:2], xi,
                                                   ALU.mult, ALU.add).then_inc(s_au, 1)

                def tile_stats(i):
                    dve.wait_ge(s_au, i + 1)
                    if isinstance(i, int):
                        xi, st = x_res[:, i, :], stat[:, i, :]
                    else:
                        xi = x_res[:].rearrange("p t h -> p (t h)")[:, bass.ds(P * i, P)]
                        st = stat[:].rearrange("p t s -> p (t s)")[:, bass.ds(6 * i, 6)]
                    nc.vector.bn_stats(st, xi).then_inc(s_st, 1)

                def step(i, j):
                    first = isinstance(i, int)

                    def earlier():
                        if not (first and i < 3):
                            add_tile(i - 3)
                        if not (first and i < 2):
                            normalise_heads(i - 2, j)

                    shift_scores(i, j, earlier)
                    if not (first and i < 3):
                        tile_stats(i - 3)

                for i in range(TPB):
                    step(i, i % 2)
                with dve.Fori(1, B) as t:
                    for q in range(TPB):
                        step(TPB * t + q, q % 2)
                def mean_var(b):
                    dve.wait_ge(s_st, TPB * (b + 1))
                    tiles = slice(TPB * b, TPB * (b + 1))
                    for t in range(TILES)[tiles]:
                        done(nc.vector.bn_aggr(mv[:, t, :], stat[:, t, :]))
                    settle()
                    nc.vector.tensor_scalar(veps[:, tiles], mv[:, tiles, 1], LN_EPS, None, ALU.add).then_inc(s_bn, 1)

                def last_norm(b):
                    rsqrt(3, b, slice(TPB * b, TPB * (b + 1)))
                    normalise(3, b)

                for b in range(B - 1):
                    mean_var(b)
                add_tile(TILES - 3)
                normalise_heads(TILES - 2, 0)
                tile_stats(TILES - 3)
                last_norm(0)
                add_tile(TILES - 2)
                normalise_heads(TILES - 1, 1)
                tile_stats(TILES - 2)
                last_norm(1)
                add_tile(TILES - 1)
                tile_stats(TILES - 1)
                mean_var(B - 1)
                low(3, 0)
                last_norm(2)
                done(nc.vector.memset(wsel[1], 0.0))
                low(3, 1)
                last_norm(B - 1)
                low(3, 2)
                route1(0, 0)

            def feed_forward(f):
                def split_lo(g, j):
                    dve.wait_ge(FF[f]["whi"], g + 1)
                    nc.vector.tensor_tensor(w_lo[:, j, :], w_raw[:, j, :], w_hi[:, j, :].bitcast(F32),
                                            ALU.subtract).then_inc(FF[f]["wlo"], 1)

                def unit(g, k, j, half, last=False):
                    u = CHUNKS * g + k
                    i = k % 2
                    early = isinstance(g, int) and u < 2
                    if k == SPLIT_AT and not last and not (isinstance(g, int) and g == 0):
                        split_lo(g + 1, 1 - j)
                    dve.wait_ge(FF[f]["silu"], u + 1)
                    dve.wait_ge(FF[f]["up"], u + 1)
                    if not early:
                        dve.wait_ge(FF[f]["act"], u - 1)
                    nc.vector.tensor_tensor(act_t[:, i, :], act_s[:, i, :], ps[6 + i][:], ALU.mult).then_inc(FF[f]["t"], 1)
                    if f == 0 and isinstance(g, int) and g == 1:
                        dve.wait_ge(s_mask1[k], 16 * MASK_DMAS)
                    elif k == 0:
                        dve.wait_ge(FF_MASK[f][j], mask_loaded(f, half, j))
                    dve.wait_ge(FF[f]["t"], u + 1)
                    if not early:
                        dve.wait_ge(FF[f]["alo"], u - 1)
                    nc.vector.tensor_tensor(act_a[:, i, :], act_t[:, i, :], mask[:, j, 512 * k:512 * (k + 1)],
                                            ALU.mult).then_inc(FF[f]["act"], 1)

                for g in range(PEEL):
                    for k in range(CHUNKS):
                        u = CHUNKS * g + k
                        if f == 0 and u == 0:
                            route0(0)
                            for b in range(1, B):
                                route0(b)
                                turn0(b - 1)
                        if f == 0 and u == 1:
                            turn0(B - 1)
                        if f == 1 and u in ROUTE1_BEFORE:
                            for part, step in ROUTE1_BEFORE[u]:
                                route1(part, step)
                        unit(g, k, g % 2, g // 2)
                with dve.Fori(0, LOOPS[f]) as t:
                    for i in range(BODY):
                        for k in range(CHUNKS):
                            unit(BODY * t + PEEL + i, k, (PEEL + i) % 2, BODY // 2 * t + (PEEL + i) // 2)
                for g in range(GROUPS[f] - REST, GROUPS[f]):
                    for k in range(CHUNKS):
                        unit(g, k, g % 2, g // 2, last=g == GROUPS[f] - 1)

            first_lo(0)
            norm(1, add_aligned)
            feed_forward(0)
            norm(2, add_ffn(0))
            attention()
            low(3, B - 1)
            feed_forward(1)
            for n in range(CHUNKS):
                add_ffn(1)(n)


INPUTS = ["x", "ctx_1024", "g_xattn", "g_ffn", "L0_ffn_router_w", "L0_ffn_shared_gate_w", "L0_ffn_shared_up_w",
          "L0_ffn_shared_down_w", "L0_ffn_expert_gate_k", "L0_ffn_expert_up_k", "L0_ffn_expert_down_k",
          "L1_xattn_Wq", "L1_xattn_bq", "L1_xattn_Wk", "L1_xattn_bk", "L1_xattn_Wv", "L1_xattn_bv",
          "L1_xattn_Wo", "L1_xattn_bo", "L1_ffn_gate_w", "L1_ffn_wg", "L1_ffn_wu", "L1_ffn_wd",
          "L1_ffn_swg", "L1_ffn_swu", "L1_ffn_swd"]


def kernel(**inputs):
    import numpy as _np
    import concourse.bacc as _bacc
    from concourse import mybir as _mybir
    from concourse.bass_utils import run_bass_kernel_spmd as _run

    nc = _bacc.Bacc("TRN2", target_bir_lowering=False, num_devices=1)
    arrays, args = {}, []
    for name in INPUTS:
        a = _np.ascontiguousarray(inputs[name])
        arrays[f"in_{name}"] = a
        args.append(nc.dram_tensor(f"in_{name}", a.shape, _mybir.dt.from_np(a.dtype), kind="ExternalInput").ap())
    shape = tuple(inputs["x"].shape)
    args.append(nc.dram_tensor("out", shape, _mybir.dt.float32, kind="ExternalOutput").ap())
    program(nc, *args)
    r = _run(nc, [arrays], core_ids=[0])
    return r.results[0]["out"]
```
